# Optimizing a Trainium2 kernel written in Bass

```python
import numpy as np
import jax
import jax.numpy as jnp

def _softmax(x, axis=-1):
    return jax.nn.softmax(x, axis=axis)

def _gelu(x):
    return jax.nn.gelu(x, approximate=True)

def _silu(x):
    return jax.nn.silu(x)

def _sigmoid(x):
    return jax.nn.sigmoid(x)

def _layernorm(x, axis=-1, eps=1e-05):
    m = jnp.mean(x, axis=axis, keepdims=True)
    v = jnp.var(x, axis=axis, keepdims=True)
    return (x - m) / jnp.sqrt(v + eps)

def _scatter_add(tgt, idx, src, axis=0):
    return tgt.at[idx].add(src)

def _segment_sum(src, seg, n):
    return jax.ops.segment_sum(src, seg, n)
kernel_name = 'mk_perceiver_d1_seqx_r4_0feb3e'

def setup_inputs(seed: int=0):
    np.random.seed(seed)
    _w = jnp.asarray

    def _rec_inputs():
        import jax
        import jax.numpy as jnp
        _rk = jax.random.key(seed)
        x = -1.394e-06 + 0.9999 * jax.random.normal(jax.random.fold_in(_rk, 1), (16, 64, 256), jnp.float32)
        _lenS = 64 - jax.random.randint(jax.random.fold_in(_rk, 7), (16,), 0, max(1, 64 // 4) + 1, jnp.int32)
        _lenS2 = 1601 - jax.random.randint(jax.random.fold_in(_rk, 8), (16,), 0, max(1, 1601 // 4) + 1, jnp.int32)
        _ctx_1024P = jax.random.normal(jax.random.fold_in(_rk, 11), (16, 16, 256), jnp.float32)
        _ctx_1024c = jax.random.dirichlet(jax.random.fold_in(_rk, 511), 0.3 * jnp.ones((16,), jnp.float32), (16, 1601))
        _ctx_1024t = jnp.einsum('bsk,bkd->bsd', _ctx_1024c, _ctx_1024P)
        _ctx_1024t = _ctx_1024t * jax.lax.rsqrt(jnp.mean(jnp.square(_ctx_1024t)) + 1e-12) * 0.953939
        ctx_1024 = 7.22013e-05 + 1.00017 * (_ctx_1024t + 0.3 * jax.random.normal(jax.random.fold_in(_rk, 611), (16, 1601, 256), jnp.float32))
        _validS = jnp.arange(64)[None, :] < _lenS[:, None]
        _validS2 = jnp.arange(1601)[None, :] < _lenS2[:, None]
        _causal = jnp.tril(jnp.ones((64, 64), dtype=bool))
        mask_Bx1x1xS2_bk0 = jnp.logical_not(jnp.broadcast_to(_validS2[:, None, None, :], (16, 1, 1, 1601)))
        return (x, ctx_1024, mask_Bx1x1xS2_bk0)
    x, ctx_1024, mask_Bx1x1xS2_bk0 = _rec_inputs()

    def _L0_xattn_setup():
        import math
        import jax, jax.numpy as jnp
        import numpy as np
        NUM_BUCKETS = 32
        MAX_DISTANCE = 128
        H = 16
        D_MODEL = 256
        D_K = D_MODEL // H

        def _relative_position_bucket(relative_position):
            nb = NUM_BUCKETS // 2
            buckets = (relative_position > 0).astype(jnp.int32) * nb
            rp = jnp.abs(relative_position)
            max_exact = nb // 2
            is_small = rp < max_exact
            rp_large = max_exact + (jnp.log(jnp.maximum(rp, 1).astype(jnp.float32) / max_exact) / math.log(MAX_DISTANCE / max_exact) * (nb - max_exact)).astype(jnp.int32)
            rp_large = jnp.minimum(rp_large, nb - 1)
            return buckets + jnp.where(is_small, rp, rp_large)
        key = jax.random.key(seed)
        ks = jax.random.split(key, 8)
        B, T_k, T_q = (4, 512, 256)
        std = D_MODEL ** (-0.5)
        inp = {'src': jax.random.normal(ks[0], (B, T_k, D_MODEL), dtype=jnp.float32), 'dst': jax.random.normal(ks[1], (B, T_q, D_MODEL), dtype=jnp.float32), 'mask': jax.random.randint(ks[2], (B, 1, 1, T_k), 0, 2).astype(bool), 'Wq': jax.random.normal(ks[3], (D_MODEL, D_MODEL), dtype=jnp.float32) * std, 'Wk': jax.random.normal(ks[4], (D_MODEL, D_MODEL), dtype=jnp.float32) * std, 'Wv': jax.random.normal(ks[5], (D_MODEL, D_MODEL), dtype=jnp.float32) * std, 'Wo': jax.random.normal(ks[6], (D_MODEL, D_MODEL), dtype=jnp.float32) * std, 'rel_bias': jax.random.normal(ks[7], (H, NUM_BUCKETS), dtype=jnp.float32) * NUM_BUCKETS ** (-0.5)}
        return inp
    _L0_xattn_all = _L0_xattn_setup()
    _L0_xattn_in = {k: v for k, v in _L0_xattn_all.items() if k in ('Wq', 'Wk', 'Wv', 'Wo', 'rel_bias')}
    del _L0_xattn_all

    def _L0_attn_setup():
        import math
        import jax, jax.numpy as jnp
        import numpy as np
        B, T, C = (2, 512, 256)
        H = 16
        D = C // H

        def alibi_slopes(n_heads):

            def pow2_slopes(n):
                start = 2.0 ** (-2.0 ** (-(math.log2(n) - 3)))
                return [start * start ** i for i in range(n)]
            if n_heads & n_heads - 1 == 0:
                s = pow2_slopes(n_heads)
            else:
                cp2 = 2 ** math.floor(math.log2(n_heads))
                s = pow2_slopes(cp2)
                extra_base = 2.0 ** (-2.0 ** (-(math.log2(2 * cp2) - 3)))
                s.extend([extra_base * extra_base ** i for i in range(n_heads - cp2)])
                s = s[:n_heads]
            return jnp.asarray(s, dtype=jnp.float32)
        key = jax.random.key(seed)
        k1, k2, k3 = jax.random.split(key, 3)
        x = jax.random.normal(k1, (B, T, C), dtype=jnp.float32)
        W_attn = jax.random.normal(k2, (3 * C, C), dtype=jnp.float32) * 0.02
        W_proj = jax.random.normal(k3, (C, C), dtype=jnp.float32) * 0.02
        return {'x': x, 'W_attn': W_attn, 'W_proj': W_proj}
    _L0_attn_all = _L0_attn_setup()
    _L0_attn_in = {k: v for k, v in _L0_attn_all.items() if k in ('W_attn', 'W_proj')}
    del _L0_attn_all

    def _L0_ffn_setup():
        import jax, jax.numpy as jnp
        import numpy as np
        B, S, D = (2, 512, 256)
        H, E, P, K = (8, 8, 128, 2)
        SCALE = 1.0 / np.sqrt(P)

        def _get_sel_gate(x, w, route_scale):
            logits = jnp.einsum('bsd,ed->bse', x, w).astype(jnp.float32)
            raw = logits.reshape(x.shape[0], x.shape[1], H, E)
            probs = jax.nn.sigmoid(raw)
            vals, idx = jax.lax.top_k(probs, K)
            vals = vals / jnp.clip(vals.sum(-1, keepdims=True), 1e-09)
            vals = vals * route_scale
            gate = (jax.nn.one_hot(idx, E, dtype=vals.dtype) * vals[..., None]).sum(-2)
            return gate
        key = jax.random.key(seed)
        ks = jax.random.split(key, 8)
        std = 1.0 / np.sqrt(D)
        return {'x': jax.random.normal(ks[0], (B, S, D), jnp.float32), 'q_w': jax.random.normal(ks[1], (H * P, D), jnp.float32) * std, 'k_w': jax.random.normal(ks[2], (H * P, D), jnp.float32) * std, 'v_w': jax.random.normal(ks[3], (H * E, D, P), jnp.float32) * std, 'o_w': jax.random.normal(ks[4], (H * E, P, D), jnp.float32) * (1.0 / np.sqrt(H * P)), 'sel_v_w': jax.random.normal(ks[5], (H * E, D), jnp.float32) * std, 'sel_o_w': jax.random.normal(ks[6], (H * E, D), jnp.float32) * std, 'route_scale': jnp.ones((1,), jnp.float32)}
    _L0_ffn_all = _L0_ffn_setup()
    _L0_ffn_in = {k: v for k, v in _L0_ffn_all.items() if k in ('q_w', 'k_w', 'v_w', 'o_w', 'sel_v_w', 'sel_o_w', 'route_scale')}
    del _L0_ffn_all
    return {'x': x, 'ctx_1024': ctx_1024, 'mask_Bx1x1xS2_bk0': mask_Bx1x1xS2_bk0, 'L0_xattn_Wq': _L0_xattn_in['Wq'], 'L0_xattn_Wk': _L0_xattn_in['Wk'], 'L0_xattn_Wv': _L0_xattn_in['Wv'], 'L0_xattn_Wo': _L0_xattn_in['Wo'], 'L0_xattn_rel_bias': _L0_xattn_in['rel_bias'], 'L0_attn_W_attn': _L0_attn_in['W_attn'], 'L0_attn_W_proj': _L0_attn_in['W_proj'], 'L0_ffn_q_w': _L0_ffn_in['q_w'], 'L0_ffn_k_w': _L0_ffn_in['k_w'], 'L0_ffn_v_w': _L0_ffn_in['v_w'], 'L0_ffn_o_w': _L0_ffn_in['o_w'], 'L0_ffn_sel_v_w': _L0_ffn_in['sel_v_w'], 'L0_ffn_sel_o_w': _L0_ffn_in['sel_o_w'], 'L0_ffn_route_scale': _L0_ffn_in['route_scale']}

def reference(x, ctx_1024, mask_Bx1x1xS2_bk0, L0_xattn_Wq, L0_xattn_Wk, L0_xattn_Wv, L0_xattn_Wo, L0_xattn_rel_bias, L0_attn_W_attn, L0_attn_W_proj, L0_ffn_q_w, L0_ffn_k_w, L0_ffn_v_w, L0_ffn_o_w, L0_ffn_sel_v_w, L0_ffn_sel_o_w, L0_ffn_route_scale):
    import jax
    import jax.numpy as jnp

    def _L0_xattn_ref(src, dst, mask, Wq, Wk, Wv, Wo, rel_bias):
        import math
        import jax, jax.numpy as jnp
        import numpy as np
        NUM_BUCKETS = 32
        MAX_DISTANCE = 128
        H = 16
        D_MODEL = 256
        D_K = D_MODEL // H

        def _relative_position_bucket(relative_position):
            nb = NUM_BUCKETS // 2
            buckets = (relative_position > 0).astype(jnp.int32) * nb
            rp = jnp.abs(relative_position)
            max_exact = nb // 2
            is_small = rp < max_exact
            rp_large = max_exact + (jnp.log(jnp.maximum(rp, 1).astype(jnp.float32) / max_exact) / math.log(MAX_DISTANCE / max_exact) * (nb - max_exact)).astype(jnp.int32)
            rp_large = jnp.minimum(rp_large, nb - 1)
            return buckets + jnp.where(is_small, rp, rp_large)
        B, T_k, _ = src.shape
        T_q = dst.shape[1]
        q = (dst @ Wq.T).reshape(B, T_q, H, D_K)
        k = (src @ Wk.T).reshape(B, T_k, H, D_K)
        v = (src @ Wv.T).reshape(B, T_k, H, D_K)
        scores = jnp.einsum('bqhd,bkhd->bhqk', q, k)
        rel_pos = jnp.arange(T_k)[None, :] - jnp.arange(T_q)[:, None]
        rp_bucket = _relative_position_bucket(rel_pos)
        bias = rel_bias[:, rp_bucket]
        scores = scores + bias[None]
        scores = jnp.where(mask, scores, -1000000000.0)
        attn = jax.nn.softmax(scores, axis=-1)
        out = jnp.einsum('bhqk,bkhd->bqhd', attn, v).reshape(B, T_q, H * D_K)
        return out @ Wo.T

    def _L0_attn_ref(x, W_attn, W_proj):
        import math
        import jax, jax.numpy as jnp
        import numpy as np
        B, T, C = (2, 512, 256)
        H = 16
        D = C // H

        def alibi_slopes(n_heads):

            def pow2_slopes(n):
                start = 2.0 ** (-2.0 ** (-(math.log2(n) - 3)))
                return [start * start ** i for i in range(n)]
            if n_heads & n_heads - 1 == 0:
                s = pow2_slopes(n_heads)
            else:
                cp2 = 2 ** math.floor(math.log2(n_heads))
                s = pow2_slopes(cp2)
                extra_base = 2.0 ** (-2.0 ** (-(math.log2(2 * cp2) - 3)))
                s.extend([extra_base * extra_base ** i for i in range(n_heads - cp2)])
                s = s[:n_heads]
            return jnp.asarray(s, dtype=jnp.float32)
        b, t, c = x.shape
        slopes = alibi_slopes(H)
        qkv = jnp.einsum('btc,fc->btf', x, W_attn)
        q, k, v = jnp.split(qkv, 3, axis=-1)
        q = q.reshape(b, t, H, D).transpose(0, 2, 1, 3)
        k = k.reshape(b, t, H, D).transpose(0, 2, 1, 3)
        v = v.reshape(b, t, H, D).transpose(0, 2, 1, 3)
        scale = 1.0 / math.sqrt(D)
        scores = jnp.einsum('bhqd,bhkd->bhqk', q, k) * scale
        pos = jnp.arange(t, dtype=jnp.float32)
        rel = pos[None, :] - pos[:, None]
        causal = pos[None, :] <= pos[:, None]
        bias = slopes[:, None, None] * rel[None, :, :]
        bias = jnp.where(causal[None, :, :], bias, -jnp.inf)
        scores = scores + bias[None]
        att = jax.nn.softmax(scores, axis=-1)
        y = jnp.einsum('bhqk,bhkd->bhqd', att, v)
        y = y.transpose(0, 2, 1, 3).reshape(b, t, c)
        y = jnp.einsum('btc,oc->bto', y, W_proj)
        return y

    def _L0_ffn_ref(x, q_w, k_w, v_w, o_w, sel_v_w, sel_o_w, route_scale):
        import jax, jax.numpy as jnp
        import numpy as np
        B, S, D = (2, 512, 256)
        H, E, P, K = (8, 8, 128, 2)
        SCALE = 1.0 / np.sqrt(P)

        def _get_sel_gate(x, w, route_scale):
            logits = jnp.einsum('bsd,ed->bse', x, w).astype(jnp.float32)
            raw = logits.reshape(x.shape[0], x.shape[1], H, E)
            probs = jax.nn.sigmoid(raw)
            vals, idx = jax.lax.top_k(probs, K)
            vals = vals / jnp.clip(vals.sum(-1, keepdims=True), 1e-09)
            vals = vals * route_scale
            gate = (jax.nn.one_hot(idx, E, dtype=vals.dtype) * vals[..., None]).sum(-2)
            return gate
        rs = route_scale[0]
        gate_v = _get_sel_gate(x, sel_v_w, rs)
        gate_o = _get_sel_gate(x, sel_o_w, rs)
        q = jnp.einsum('bsd,hpd->bhsp', x, q_w.reshape(H, P, D))
        k = jnp.einsum('bsd,hpd->bhsp', x, k_w.reshape(H, P, D))
        xv = jnp.einsum('bsd,hedp->bshep', x, v_w.reshape(H, E, D, P))
        v = jnp.einsum('bshep,bshe->bhsp', xv, gate_v)
        att = jax.nn.softmax(jnp.einsum('bhqp,bhkp->bhqk', q, k) * SCALE, axis=-1)
        ctx = jnp.einsum('bhqk,bhkp->bqhp', att, v)
        weighted = ctx[:, :, :, None, :] * gate_o[..., None]
        out = jnp.einsum('bshep,hepd->bsd', weighted, o_w.reshape(H, E, P, D))
        return out
    x = x + _L0_xattn_ref(ctx_1024, _layernorm(x, axis=-1), mask_Bx1x1xS2_bk0, L0_xattn_Wq, L0_xattn_Wk, L0_xattn_Wv, L0_xattn_Wo, L0_xattn_rel_bias)
    x = x + _L0_attn_ref(_layernorm(x, axis=-1), L0_attn_W_attn, L0_attn_W_proj)
    x = x + _L0_ffn_ref(_layernorm(x, axis=-1), L0_ffn_q_w, L0_ffn_k_w, L0_ffn_v_w, L0_ffn_o_w, L0_ffn_sel_v_w, L0_ffn_sel_o_w, L0_ffn_route_scale)
    return x

_drawn_inputs = setup_inputs


def setup_inputs(seed=0):
    import zlib

    import numpy as np

    out = dict(_drawn_inputs(seed))
    spreads = {}
    factors = {}
    for name, (base, spread) in spreads.items():
        noise = np.random.default_rng([zlib.crc32(name.encode()), seed]).standard_normal(out[name].shape)
        drawn = base * np.exp(spread * noise) if base else spread * noise
        out[name] = jnp.asarray(drawn.astype(out[name].dtype))
    for name, factor in factors.items():
        out[name] = (out[name] * factor).astype(out[name].dtype)
    return out
```

```python
import math
from contextlib import ExitStack

import numpy as np

import concourse.bass as bass
from concourse import mybir

F32 = mybir.dt.float32
F32R = mybir.dt.float32r
BF16 = mybir.dt.bfloat16
U8 = mybir.dt.uint8
ALU = mybir.AluOpType
ACT = mybir.ActivationFunctionType
AX = mybir.AxisListType

P = 128
B, TQ, DM = 16, 64, 256
TOK = B * TQ
NT = TOK // P
KT = DM // P
H, DK = 16, 16
HT = P // DK
TK = 1601
KTILES = [(t * P, min(P, TK - t * P)) for t in range((TK + P - 1) // P)]
NKT = len(KTILES)
CHUNKS = [(0, 1, 2, 3), (4, 5, 6), (7, 8, 9), (10, 11, 12)]
NC = len(CHUNKS)
CSPAN = [(KTILES[c[0]][0], sum(KTILES[t][1] for t in c)) for c in CHUNKS]
NEAR = 256
NEG = 1.0e9
EPS = 1e-5
FH, FE, FP = 8, 8, 128
BUCKETS, MAXDIST = 32, 128


def relative_buckets(rel):
    nb = BUCKETS // 2
    rp = np.abs(rel)
    exact = nb // 2
    large = exact + (np.log(np.maximum(rp, 1).astype(np.float32) / np.float32(exact))
                     / np.float32(math.log(MAXDIST / exact)) * np.float32(nb - exact)).astype(np.int32)
    large = np.minimum(large, nb - 1)
    return (rel > 0).astype(np.int32) * nb + np.where(rp < exact, rp, large)


def constants():
    rel = np.arange(NEAR + TQ - 1) - (TQ - 1)
    onehot = (np.arange(BUCKETS)[:, None] == relative_buckets(rel)[None, :]).astype(np.float32)
    assert relative_buckets(np.arange(NEAR - TQ + 1, TK)).min() == BUCKETS - 1
    part = np.arange(P)
    head_rows = (part[:, None] // DK == np.arange(HT)[None, :]).astype(np.float32)
    den_rows = (part[:, None] == 32 * (part[None, :] // 32) + DK).astype(np.float32)
    start = 2.0 ** (-2.0 ** (-(math.log2(H) - 3)))
    slopes = np.array([start * start ** i for i in range(H)], np.float32)
    pos = np.arange(TQ, dtype=np.float32)
    dist = pos[None, :] - pos[:, None]
    alibi = slopes[None, :, None] * dist[:, None, :]
    alibi = np.where((dist <= 0)[:, None, :], alibi, np.float32(-1e30)).reshape(TQ, H * TQ)
    return {
        "c_onehot": onehot,
        "c_head_rows": head_rows,
        "c_head_rows4": (part[:, None] % 64 // DK == np.arange(4)[None, :]).astype(np.float32),
        "c_den_rows": den_rows,
        "c_rank": (FE - np.arange(FE, dtype=np.float32)).reshape(1, FE),
        "c_ident": np.eye(P, dtype=np.float32),
        "c_alibi": np.concatenate([alibi, alibi]).astype(np.float32),
    }


def tok_rows(par):
    return slice(TQ * par, TQ * par + TQ)


def layer_norm_steps(v, x, stats, mv, rstd, xn, step, nc_scalar=None):
    for n in range(NT):
        v.bn_stats(stats[:, n, :], x[:, n, :]).then_inc(step, 1)
    v.wait_ge(step, NT)
    for n in range(NT):
        v.bn_aggr(mv[:, n, :], stats[:, n, :]).then_inc(step, 1)
    v.wait_ge(step, 2 * NT)
    v.tensor_scalar(rstd[:, :], mv[:, :, 1], EPS, None, ALU.add).then_inc(step, 1)


def prologue(nc, d, s, sb, sem):
    xn, xnT = s["xn"], s["xnT"]
    psW, psS, psO = s["psW"], s["psS"], s["psO"]
    loads = sem("pro_loads")
    consts = sem("pro_consts")
    ln = sem("pro_ln")
    root = sem("pro_root")
    xn_ready = sem("pro_xn")
    turned = sem("pro_turned")
    xnT_out = sem("pro_xnT")
    q_full = sem("pro_q")
    q_out = sem("pro_q_out")
    w_hi = sem("pro_w_hi")
    rb_ready = sem("pro_rb")
    near_full = sem("pro_near")
    near_out = sem("pro_near_out")
    dN_full = sem("pro_dN")
    dN_out = sem("pro_dN_out")
    mrow = sem("pro_mrow")
    m_full = sem("pro_m_full")
    m_out = sem("pro_m_out")
    rbT = sb("rbT", [BUCKETS, H], F32)
    rb_far = sb("rb_far", [BUCKETS, H], F32)
    rbd = sb("rbd", [BUCKETS, H], F32)
    onehot = sb("onehot", [BUCKETS, NEAR + TQ - 1], F32)
    m16 = sb("m16", [B, TK], U8)
    m16f = sb("m16f", [B, TK], F32)
    mb16 = sb("mb16", [B, TK], F32)
    any16 = sb("any16", [B, 2], F32)
    stats = sb("stats", [P, NT, 6], F32)
    mv = sb("mv", [P, NT, 2], F32)
    rstd = sb("rstd", [P, NT], F32)
    wq = sb("wq", [P, KT, 4, P], F32)
    wkv = sb("wkv", [P, 2, KT, DM], F32)
    dma_list = [
        (s["x1"][:, :, :], d["x"].rearrange("(n p) f -> p n f", p=P)),
        (s["ident"][:, :], d["c_ident"]),
        (wq[:, :, :, :], d["xWqD"].rearrange("(k p) g f -> p k g f", p=P)),
        (onehot[:, :], d["c_onehot"]),
        (rbT[:, :], d["rbT"]),
        (rb_far[:, :], d["rbT"][BUCKETS - 1:BUCKETS, :].to_broadcast([BUCKETS, H])),
        (m16[:, :], d["mask"]),
        (s["head_rows"][:, :], d["c_head_rows4"]),
        (wkv[:, 0, :, :], d["xWkT"].rearrange("(k p) f -> p k f", p=P)),
        (wkv[:, 1, :, :], d["xWvT"].rearrange("(k p) f -> p k f", p=P)),
        (s["den_rows"][:, :], d["c_den_rows"]),
    ]
    wo_view = d["xWoT"].rearrange("(g j e) n -> j e g n", j=4, e=DK)
    NL = 16 * (len(dma_list) + 4)
    with nc.Block() as block:
        @block.sync
        def _(sp):
            for dst, src in dma_list:
                sp.dma_start(dst, src).then_inc(loads, 16)
            sp.wait_ge(consts, 1)
            for j in range(4):
                sp.dma_start(s["woP"][32 * j:32 * j + DK, :, :], wo_view[j]).then_inc(loads, 16)
            sp.wait_ge(loads, NL)

        @block.gpsimd
        def _(pool):
            pool.memset(s["woP"][:, :, :], 0.0).then_inc(consts, 1)
            pool.memset(s["ctx"][:, 1, :, CSPAN[-1][1]:CSPAN[-1][1] + 1], 0.0).then_inc(consts, 1)
            for par in range(2):
                pool.memset(s["V"][par][:, :, :, DK:DK + 1], 1.0).then_inc(consts, 1)
            pool.wait_ge(loads, NL)
            pool.tensor_copy(s["identb"][:, :], s["ident"][:, :]).then_inc(consts, 1)
            pool.wait_ge(w_hi, 1)
            pool.tensor_tensor(s["wL"][:, :, :, :], wkv[:, :, :, :], s["wH"][:, :, :, :].bitcast(F32), ALU.subtract)\
                .then_inc(consts, 1)

        @block.vector
        def _(v):
            v.memset(psO[:, :], 0.0)
            v.memset(psW[:, 2, :], 0.0).then_inc(mrow, 1)
            v.wait_ge(loads, NL)
            layer_norm_steps(v, s["x1"], stats, mv, rstd, xn, ln)
            v.tensor_copy(m16f[:, :], m16[:, :]).then_inc(mrow, 1)
            v.wait_ge(mrow, 2)
            v.tensor_reduce(any16[:, 0:1], m16f[:, :], AX.X, ALU.max).then_inc(mrow, 1)
            v.wait_ge(mrow, 3)
            v.tensor_scalar(any16[:, 1:2], any16[:, 0:1], NEG, None, ALU.mult).then_inc(mrow, 1)
            v.wait_ge(mrow, 4)
            v.tensor_scalar(mb16[:, :], m16f[:, :], -1.0, any16[:, 1:2], ALU.add, ALU.mult).then_inc(mrow, 1)
            v.tensor_tensor(rbd[:, :], rbT[:, :], rb_far[:, :], ALU.subtract).then_inc(rb_ready, 1)
            v.wait_ge(root, 1)
            v.reciprocal(rstd[:, :], rstd[:, :]).then_inc(ln, 1)
            v.wait_ge(ln, 2 * NT + 2)
            for n in range(NT):
                v.tensor_scalar(xn[:, n, :], s["x1"][:, n, :], mv[:, n, 0:1], rstd[:, n:n + 1],
                                ALU.subtract, ALU.mult).then_inc(xn_ready, 1)
            for i in range(4):
                v.wait_ge(turned, i + 1)
                v.tensor_copy(xnT[:, i // 2, (i % 2) * 512:(i % 2) * 512 + 512], psS[:, i // 2, (i % 2) * 512:(i % 2) * 512 + 512])\
                 .then_inc(xnT_out, 1)
            v.wait_ge(m_full, 1)
            v.tensor_copy(s["mcols"].rearrange("p a t b -> p (a t b)"), psW[:, 2, 0:2 * NKT * B]).then_inc(m_out, 1)
            for i in range(8):
                v.wait_ge(q_full, i + 1)
                g, c = i // 2, slice((i % 2) * 512, (i % 2) * 512 + 512)
                v.tensor_copy(s["qD"][:, g, c], psW[:, i % 2, :]).then_inc(q_out, 1)
            for t in range(2):
                v.wait_ge(near_full, t + 1)
                v.tensor_copy(s["dT"][:, t, :].rearrange("p (h q) -> p h q", q=TQ),
                              psS[:, t, :].rearrange("p (q h) -> p h q", h=H)).then_inc(near_out, 1)
            for i in range(4):
                v.wait_ge(dN_full, i + 1)
                v.tensor_copy(s["dN"][:, 2 * i:2 * i + 2, :], psW[:, i % 2, :].rearrange("p (a k) -> p a k", a=2))\
                 .then_inc(dN_out, 1)

        @block.scalar
        def _(act):
            act.wait_ge(loads, NL)
            act.activation(s["wH"][:, :, :, :], wkv[:, :, :, :], ACT.Copy).then_inc(w_hi, 1)
            act.wait_ge(ln, 2 * NT + 1)
            act.activation(rstd[:, :], rstd[:, :], ACT.Sqrt).then_inc(root, 1)

        @block.tensor
        def _(pe):
            pe.wait_ge(loads, NL)
            pe.wait_ge(mrow, 5)
            for a, rows in enumerate((m16f, mb16)):
                for t, (k0, kw) in enumerate(KTILES):
                    c = (a * NKT + t) * B
                    mm = pe.transpose(psW[0:kw, 2, c:c + B], rows[:, k0:k0 + kw], s["ident"][0:B, 0:B])
            mm.then_inc(m_full, 1)
            for i in range(4):
                for n in range(4):
                    pe.wait_ge(xn_ready, (i % 2) * 4 + n + 1)
                    mm = pe.transpose(psS[:, i // 2, (i % 2) * 512 + n * P:(i % 2) * 512 + n * P + P],
                                      xn[:, (i % 2) * 4 + n, (i // 2) * P:(i // 2) * P + P], s["ident"][:, :])
                mm.then_inc(turned, 1)
            pe.wait_ge(xnT_out, 4)
            for i in range(8):
                if i >= 2:
                    pe.wait_ge(q_out, i - 1)
                for k in range(KT):
                    mm = pe.matmul(psW[:, i % 2, :], wq[:, k, i // 2, :],
                                   xnT[:, k, (i % 2) * 512:(i % 2) * 512 + 512], start=(k == 0), stop=(k == KT - 1))
                mm.then_inc(q_full, 1)
            pe.wait_ge(rb_ready, 1)
            for t in range(2):
                for q in range(TQ):
                    off = t * P - q + TQ - 1
                    mm = pe.matmul(psS[:, t, q * H:q * H + H], onehot[:, off:off + P],
                                   rbd[:, :], start=True, stop=True, skip_group_check=True)
                mm.then_inc(near_full, 1)
            pe.wait_ge(near_out, 2)
            for i in range(4):
                pe.wait_ge(q_out, 8)
                if i >= 2:
                    pe.wait_ge(dN_out, i - 1)
                for a in range(2):
                    for t in range(2):
                        pr = 2 * i + a
                        mm = pe.transpose(psW[:, i % 2, a * NEAR + t * P:a * NEAR + t * P + P],
                                          s["dT"][:, t, pr * P:pr * P + P], s["ident"][:, :])
                mm.then_inc(dN_full, 1)


def cross_attention(nc, d, s, sb, sem):
    psS, psW, psO = s["psS"], s["psW"], s["psO"]
    ctx = s["ctx"]
    V = s["V"]
    HG = 4
    cH = sb("cH", [P, 2, KT, 512], F32R)
    cL = sb("cL", [P, 2, KT, 512], F32R)
    kHL = [sb(f"kHL{i}", [P, HG, TK + 1], F32R) for i in range(2)]
    qb = sb("qb", [P, HG, 4 * TQ], F32)
    qh = [sb(f"qh{i}", [P, HG, 4 * TQ], F32R) for i in range(2)]
    ql = [sb(f"ql{i}", [P, HG, 4 * TQ], F32R) for i in range(2)]
    m8 = [sb(f"m8_{i}", [P, TK], U8) for i in range(2)]
    mneg = [sb(f"mneg{i}", [P, TK], BF16) for i in range(2)]
    near = sb("near", [P, H // 2, NEAR], BF16)
    mc = [sb(f"mc{i}", [P, 2, NKT, 1], F32) for i in range(2)]
    mx = [sb(f"mx{i}", [P, H // 2, NC + 1], F32) for i in range(2)]
    cv = [sb(f"cv{i}", [P, H // 2, 2], BF16) for i in range(2)]
    cm = sb("cm", [P, H // 2], F32)
    cr = sb("cr", [P, H // 2], F32)
    shift = sb("shift", [P, H * TQ], F32)
    PTR = 3
    pT = sb("pT", [P, PTR, H * TQ], F32)
    oT = sb("oT", [P, DM], F32)
    oR = sb("oR", [P, DM], F32)
    oN = oR
    x1 = s["x1"]

    ctx_in = [sem(f"ctx_in{c}") for c in range(NC)]
    mask_in = [sem(f"mask_in{i}") for i in range(2)]
    ctx_hi = sem("ctx_hi")
    ctx_lo = sem("ctx_lo")
    work_full = sem("work_full")
    k_hi = sem("k_hi")
    k_lo = sem("k_lo")
    v_out = sem("v_out")
    maxed = sem("maxed")
    mneg_ready = sem("mneg_ready")
    near_ready = sem("near_ready")
    q_ready = sem("q_ready")
    qb_ready = sem("qb_ready")
    mc_ready = sem("mc_ready")
    c_step = sem("c_step")
    s_full = sem("s_full")
    s_read = sem("s_read")
    added = sem("added")
    pv_done = sem("pv_done")
    o_out = sem("o_out")
    d_full = sem("d_full")
    o_step = sem("o_step")
    y_full = sem("y_full")
    y_out = sem("y_out")
    waited = sem("waited")

    SB = NKT + 1
    HI, LO = s["wH"], s["wL"]
    SLOTS = [((0, 1, 2), (3, 4, 5), (6, 7, 8), (9, 10, 11))] + 3 * [((0, 1, 2, 3), (4, 5, 6, 7), (8, 9, 10, 11))]

    def exps(b, t):
        return SB * b + t + 2

    def adds(b, t):
        return 15 * b + (2 * t + 2 if t < 2 else t + 3)

    def at_least(eng, sm, value):
        if not (isinstance(value, int) and value <= 0):
            eng.wait_ge(sm, value)

    def wait_apart(eng, sm, value):
        eng.wait_ge(sm, value)
        eng.sem_inc(waited, 1)

    def groups(c):
        ts = CHUNKS[c]
        return [ts[0:2], ts[2:]]

    def width(c):
        return CSPAN[c][1] + CSPAN[c][1] % 2

    def pe_use(pe, j, par, c, u):
        n = j * NC + c
        r = c % 2
        k0, w = CSPAN[c][0], width(c)
        bank = psW[:, u % 3, :]
        if u <= 2:
            at_least(pe, maxed, 8 * (n - 1) + 6 + u)
        elif u <= 4:
            pe.wait_ge(k_lo, 4 * n + 2 * (u - 2))
        elif u <= 6:
            pe.wait_ge(v_out, 2 * n + u - 4)
        else:
            pe.wait_ge(maxed, 8 * n + u - 6)
        if u == 0:
            pe.wait_ge(ctx_lo, n + 1)
        if u == 4:
            pe.wait_ge(q_ready, 2 * j + 1)
            pe.wait_ge(v_out, 2 * n + 1)
        if u < 2:
            prods = [(a, b, k) for k in range(KT) for a, b in ((HI, cH), (HI, cL), (LO, cH))]
            for i, (a, b, k) in enumerate(prods):
                mm = pe.matmul(bank[:, 0:w], a[:, 0, k, u * P:u * P + P], b[:, r, k, 0:w],
                               start=(i == 0), stop=(i == len(prods) - 1))
        elif u < 4:
            for i, t in enumerate(groups(c)[u - 2]):
                a0, kw = KTILES[t][0] - k0, KTILES[t][1]
                prods = [(a, b, k) for k in range(KT) for a, b in ((cH, HI), (cH, LO), (cL, HI))]
                for q, (a, b, k) in enumerate(prods):
                    mm = pe.matmul(bank[0:kw, i * DM:i * DM + DM], a[:, r, k, a0:a0 + kw], b[:, 1, k, :],
                                   start=(q == 0), stop=(q == len(prods) - 1))
        else:
            p = u - 4
            mm = pe.matmul(bank[:, 0:w], qh[par][:, p // 2, (p % 2) * P:(p % 2) * P + P], kHL[par][:, p // 2, k0:k0 + w],
                           start=True, stop=True)
        mm.then_inc(work_full, 1)

    def pe_shift(pe, b, par):
        pe.wait_ge(c_step, 5 * (b + 1))
        at_least(pe, s_read, SB * b)
        for p in range(H // 2):
            for i in range(2):
                mm = pe.matmul(psS[:, 1, p * P:p * P + P], cv[par][:, p, i:i + 1].to_broadcast([P, P]), s["identb"][:, :],
                               start=(i == 0), stop=(i == 1), skip_group_check=True)
        mm.then_inc(s_full, 1)

    def buf(t):
        return 0 if t == 0 else (t + 1) % 2

    def pe_scores(pe, b, par, t):
        a, kw = KTILES[t]
        if t == 0:
            pe.wait_ge(q_ready, 2 * b + 2)
            at_least(pe, s_read, SB * b - 1)
        elif t == 2:
            pe.wait_ge(s_read, SB * b + 1)
        else:
            pe.wait_ge(s_read, exps(b, max(t - 2, 0)))
        for g in range(HG):
            o = psS[0:kw, buf(t), g * 256:g * 256 + 256]
            for i, q in enumerate((qh, ql)):
                mm = pe.matmul(o, kHL[par][:, g, a:a + kw], q[par][:, g, :], start=(i == 0), stop=(i == 1),
                               skip_group_check=True)
        mm.then_inc(s_full, 1)

    def pe_values(pe, b, par, t):
        kw = KTILES[t][1]
        pe.wait_ge(s_read, exps(b, t))
        if t == 0:
            at_least(pe, y_out, b)
        for h in range(H):
            r, g = 32 * (h % 4), h // 4
            mm = pe.matmul(psO[r:r + DK + 1, g * TQ:g * TQ + TQ], V[par][0:kw, t, h, :],
                           pT[0:kw, t % PTR, h * TQ:h * TQ + TQ], start=(t == 0 and g == 0), stop=(t == NKT - 1),
                           skip_group_check=True)
        mm.then_inc(pv_done, 1)

    def pe_denominators(pe, b):
        pe.wait_ge(o_out, b + 1)
        pe.matmul(psO[:, 256:512], s["den_rows"][:, :], oT[:, :], start=True, stop=True,
                  skip_group_check=True).then_inc(d_full, 1)

    def pe_project(pe, b, par):
        pe.wait_ge(o_step, 2 * b + 2)
        for g in range(4):
            mm = pe.matmul(psO[tok_rows(par), 256:512], oN[:, g * TQ:g * TQ + TQ], s["woP"][:, g, :],
                           start=(g == 0), stop=(g == 3), skip_group_check=True)
        mm.then_inc(y_full, 1)

    def pe_step(pe, j, par, prep, main, fin, ahead):
        for c in range(NC):
            for i, t in enumerate(CHUNKS[c]):
                if t == 1 and fin:
                    pe_project(pe, j - 2, par)
                if main:
                    pe_scores(pe, j - 1, 1 - par, t)
                    if t == 0:
                        pe_shift(pe, j - 1, 1 - par)
                    else:
                        pe_values(pe, j - 1, 1 - par, t - 1)
                if prep:
                    for u in SLOTS[c][i]:
                        pe_use(pe, j, par, c, u)
                if t == 0 and fin:
                    pe_denominators(pe, j - 2)
        if main:
            pe_values(pe, j - 1, 1 - par, NKT - 1)

    def act_split(act, j, c):
        n = j * NC + c
        w = width(c)
        act.wait_ge(ctx_in[c], 16 * (j + 1))
        at_least(act, work_full, 12 * (n - 2) + 4)
        act.activation(cH[:, c % 2, :, 0:w], ctx[:, c % 2, :, 0:w], ACT.Copy).then_inc(ctx_hi, 1)

    def act_use(act, j, par, c, u):
        n = j * NC + c
        k0, w = CSPAN[c][0], width(c)
        if u < 4:
            act.wait_ge(work_full, 12 * n + u + 1)
        if u < 2:
            for g in range(2):
                rows = slice(64 * g, 64 * g + 64)
                act.activation(kHL[par][rows, 2 * u + g, k0:k0 + w], psW[rows, u, 0:w], ACT.Copy).then_inc(k_hi, 1)
        elif u < 4:
            ts = groups(c)[u - 2]
            kw = KTILES[ts[-1]][1]
            act.activation(V[par][0:kw, ts[0]:ts[-1] + 1, :, 0:DK],
                           psW[0:kw, u % 3, 0:len(ts) * DM].rearrange("p (t h e) -> p t h e", t=len(ts), e=DK),
                           ACT.Copy).then_inc(v_out, 1)

    def act_exp(act, b, par, t):
        kw = KTILES[t][1]
        if t == 0:
            act.wait_ge(mc_ready, b + 1)
        if t >= PTR:
            act.wait_ge(pv_done, NKT * b + t - PTR + 1)
        else:
            at_least(act, pv_done, NKT * (b - 1) + [13, 11, 12][t])
        act.wait_ge(added, adds(b, t))
        act.activation(pT[0:kw, t % PTR, :], psS[0:kw, buf(t), :], ACT.Exp,
                       bias=mc[par][0:kw, 1, t, :], scale=mc[par][0:kw, 0, t, :]).then_inc(s_read, 1)

    def act_step(act, j, par, prep, main, fin, ahead):
        b = j - 1
        if isinstance(j, int) and j == 0:
            act_split(act, 0, 0)
        for c in range(NC):
            for i, t in enumerate(CHUNKS[c]):
                if main and t == 0:
                    act.wait_ge(s_full, SB * b + 2)
                    act.activation(shift[:, :], psS[:, 1, :], ACT.Copy).then_inc(s_read, 1)
                if prep and t == 0 and not (isinstance(j, int) and j < 2):
                    act.wait_ge(pv_done, NKT * (j - 1))
                if prep and t == 0:
                    act_use(act, j, par, c, 0)
                if main:
                    act_exp(act, b, 1 - par, t)
                if prep:
                    for u in SLOTS[c][i]:
                        if not (t == 0 and u == 0):
                            act_use(act, j, par, c, u)
                    if i == 1 and (c < NC - 1 or ahead):
                        act_split(act, j if c < NC - 1 else j + 1, (c + 1) % NC)

    def dve_use(v, j, par, c, u):
        n = j * NC + c
        k0, w = CSPAN[c]
        if u < 2:
            w = width(c)
            for g in range(2):
                rows, other = slice(64 * g, 64 * g + 64), slice(64 - 64 * g, 128 - 64 * g)
                v.wait_ge(k_hi, 4 * n + 2 * u + g + 1)
                v.tensor_tensor(kHL[par][other, 2 * u + g, k0:k0 + w], psW[rows, u, 0:w],
                                kHL[par][rows, 2 * u + g, k0:k0 + w].bitcast(F32), ALU.subtract).then_inc(k_lo, 1)
        elif u >= 4:
            p = u - 4
            bank = psW[:, u % 3, :]
            wait_apart(v, work_full, 12 * n + u + 1)
            if c == 0:
                v.tensor_tensor_reduce(bank[:, 0:NEAR], bank[:, 0:NEAR], near[:, p, :], 1.0, -3e38,
                                       ALU.add, ALU.max, mx[par][:, p, 0:1])
                v.tensor_tensor_reduce(bank[:, NEAR:w], bank[:, NEAR:w], mneg[par][:, NEAR:w], 1.0, -3e38,
                                       ALU.add, ALU.max, mx[par][:, p, 1:2]).then_inc(maxed, 1)
            else:
                v.tensor_tensor_reduce(bank[:, 0:w], bank[:, 0:w], mneg[par][:, k0:k0 + w], 1.0, -3e38,
                                       ALU.add, ALU.max, mx[par][:, p, c + 1:c + 2]).then_inc(maxed, 1)

    def dve_add(v, b, t):
        kw = KTILES[t][1]
        if t == 0:
            v.wait_ge(s_read, SB * b + 1)
        v.wait_ge(s_full, SB * b + (1 if t == 0 else t + 2))
        o = psS[0:kw, buf(t), :]
        v.tensor_tensor(o, o, shift[0:kw, :], ALU.add).then_inc(added, 1)
        if t < 2:
            v.wait_ge(added, 15 * b + 2 * t + 1)
            v.tensor_tensor(o, o, s["dT"][0:kw, t, :], ALU.add).then_inc(added, 1)

    def dve_step(v, j, par, prep, main, fin, ahead, tile):
        f, b = j - 2, j - 1
        if fin:
            v.wait_ge(pv_done, NKT * (f + 1))
            v.tensor_copy(oT[:, :], psO[:, 0:DM]).then_inc(o_out, 1)
        for c in range(NC):
            for i, t in enumerate(CHUNKS[c]):
                if t == 1 and fin:
                    v.wait_ge(d_full, f + 1)
                    v.reciprocal(oR[:, :], psO[:, 256:512]).then_inc(o_step, 1)
                    v.wait_ge(o_step, 2 * f + 1)
                    v.tensor_tensor(oN[:, :], oT[:, :], oR[:, :], ALU.mult).then_inc(o_step, 1)
                    v.wait_ge(y_full, f + 1)
                    v.tensor_tensor(x1[tok_rows(par), tile, :], psO[tok_rows(par), 256:512],
                                    x1[tok_rows(par), tile, :], ALU.add).then_inc(y_out, 1)
                if main:
                    dve_add(v, b, t)
                if prep:
                    if t == 0:
                        v.wait_ge(near_ready, j + 1)
                    for u in SLOTS[c][i]:
                        dve_use(v, j, par, c, u)
        if prep:
            k = 5 * j
            v.wait_ge(maxed, 32 * (j + 1))
            v.tensor_reduce(cm[:, :], mx[par][:, :, :], AX.X, ALU.max).then_inc(c_step, 1)
            v.wait_ge(c_step, k + 1)
            v.tensor_scalar(cm[:, :], cm[:, :], -1.0, None, ALU.mult).then_inc(c_step, 1)
            v.wait_ge(c_step, k + 2)
            v.tensor_copy(cv[par][:, :, 0], cm[:, :]).then_inc(c_step, 1)
            v.wait_ge(c_step, k + 3)
            v.tensor_tensor(cr[:, :], cm[:, :], cv[par][:, :, 0], ALU.subtract).then_inc(c_step, 1)
            v.wait_ge(c_step, k + 4)
            v.tensor_copy(cv[par][:, :, 1], cr[:, :]).then_inc(c_step, 1)

    def pool_split(pool, j, c):
        n = j * NC + c
        w = width(c)
        at_least(pool, work_full, 12 * (n - 2) + 4)
        pool.wait_ge(ctx_hi, n + 1)
        pool.tensor_tensor(cL[:, c % 2, :, 0:w], ctx[:, c % 2, :, 0:w], cH[:, c % 2, :, 0:w].bitcast(F32), ALU.subtract)\
            .then_inc(ctx_lo, 1)

    def pool_step(pool, j, par, ahead, half):
        late = not (isinstance(j, int) and j < 2)
        if isinstance(j, int) and j == 0:
            pool_split(pool, 0, 0)
        at_least(pool, maxed, 32 * (j - 1) + 8 if not isinstance(j, int) or j else 0)
        wait_apart(pool, mask_in[par], 16 * (half + 1))
        pool.tensor_scalar(mneg[par][:, :], m8[par][:, :], -1.0, NEG, ALU.add, ALU.mult).then_inc(mneg_ready, 1)
        pool.wait_ge(mneg_ready, j + 1)
        pool.tensor_tensor(near[:, :, :], s["dN"][:, :, :],
                           mneg[par][:, 0:NEAR].unsqueeze(1).to_broadcast([P, H // 2, NEAR]), ALU.add).then_inc(near_ready, 1)
        if late:
            pool.wait_ge(s_full, SB * (j - 1))
        for g in range(HG):
            op = pool.tensor_tensor(qb[:, g, :].rearrange("p (h q) -> p h q", h=4),
                                    s["qD"][:, g, bass.ds(j * TQ, TQ)].unsqueeze(1).to_broadcast([P, 4, TQ]),
                                    s["head_rows"][:, :].unsqueeze(2).to_broadcast([P, 4, TQ]), ALU.mult)
        op.then_inc(qb_ready, 1)
        wait_apart(pool, qb_ready, j + 1)
        pool.tensor_copy(qh[par][:, :, :], qb[:, :, :]).then_inc(q_ready, 1)
        pool.wait_ge(q_ready, 2 * j + 1)
        pool.tensor_tensor(ql[par][:, :, :], qb[:, :, :], qh[par][:, :, :].bitcast(F32), ALU.subtract).then_inc(q_ready, 1)
        if late:
            wait_apart(pool, s_read, SB * (j - 1))
        pool.tensor_copy(mc[par][:, :, :, :], s["mcols"][:, :, :, bass.ds(j, 1)]).then_inc(mc_ready, 1)
        for c in range(NC):
            if c < NC - 1 or ahead:
                pool_split(pool, j if c < NC - 1 else j + 1, (c + 1) % NC)

    ctx_view = d["ctxT"].rearrange("b (k p) t -> b p k t", p=P)

    def sp_step(sp, j, par):
        late = not (isinstance(j, int) and j < 2)
        if late:
            sp.wait_ge(mneg_ready, j - 1)
        for c in range(NC):
            k0, w = CSPAN[c]
            at_least(sp, ctx_lo, j * NC + c - 1)
            sp.dma_start(ctx[:, c % 2, :, 0:w], ctx_view[bass.ds(j, 1), :, :, k0:k0 + w].rearrange("b p k t -> (b p) k t"))\
              .then_inc(ctx_in[c], 16)
            if c == 0:
                sp.dma_start(m8[par][:, :], d["mask"][bass.ds(j, 1), :].to_broadcast([P, TK])).then_inc(mask_in[par], 16)

    def run(eng, step):
        step(eng, 0, 0, 0)
        step(eng, 1, 1, 0)
        with eng.Fori(0, B // 2 - 2) as i:
            step(eng, 2 * i + 2, 0, i + 1)
            step(eng, 2 * i + 3, 1, i + 1)
        for j in range(B - 2, B + 2):
            step(eng, j, j % 2, j // 2)

    def parts(j):
        if not isinstance(j, int):
            return True, True, True, True
        return j < B, 1 <= j <= B, j >= 2, j < B - 1

    with nc.Block() as block:
        @block.sync
        def _(sp):
            run(sp, lambda e, j, par, half: parts(j)[0] and sp_step(e, j, par))

        @block.gpsimd
        def _(pool):
            run(pool, lambda e, j, par, half: parts(j)[0] and pool_step(e, j, par, parts(j)[3], half))

        @block.scalar
        def _(act):
            run(act, lambda e, j, par, half: act_step(e, j, par, *parts(j)))

        @block.vector
        def _(v):
            run(v, lambda e, j, par, half: dve_step(e, j, par, *parts(j), half - 1))

        @block.tensor
        def _(pe):
            run(pe, lambda e, j, par, half: pe_step(e, j, par, *parts(j)))


def norm_stats(nc, x, mv, rstd, sb, sem, tag):
    stats = sb(f"{tag}_stats", [P, NT, 6], F32)
    step = sem(f"{tag}_norm_step")
    root = sem(f"{tag}_norm_root")
    with nc.Block() as block:
        @block.vector
        def _(v):
            layer_norm_steps(v, x, stats, mv, rstd, None, step)
            v.wait_ge(root, 1)
            v.reciprocal(rstd[:, :], rstd[:, :]).then_inc(step, 1)

        @block.scalar
        def _(act):
            act.wait_ge(step, 2 * NT + 1)
            act.activation(rstd[:, :], rstd[:, :], ACT.Sqrt).then_inc(root, 1)


def self_attention(nc, d, s, sb, ps, sem):
    x1, x2, ident = s["x1"], s["x2"], s["ident"]
    psX = ps("a_psX", [P, 512])
    psQ = ps("a_psQ", [P, 512])
    psK = ps("a_psK", [P, 512])
    psV = ps("a_psV", [P, 512])
    psA = ps("a_psA", [P, 1024])
    psT = ps("a_psT", [P, 2, 512])
    mv = sb("a_mv", [P, NT, 2], F32)
    rstd = sb("a_rstd", [P, NT], F32)
    norm_stats(nc, x1, mv, rstd, sb, sem, "a")
    xn = sb("a_xn", [P, DM], F32)
    xs = sb("a_xs", [P, KT, P], F32)
    qs = sb("a_qs", [P, KT, P], F32)
    kbd = sb("a_kbd", [P, 2, KT, 512], F32)
    V = sb("a_V", [P, H, DK + 1], F32)
    E = sb("a_E", [P, H, TQ], F32)
    mx = sb("a_mx", [P, H], F32)
    pf = sb("a_pf", [P, H, P], F32)
    pT = kbd.rearrange("p b m c -> p (b m c)").rearrange("p (h q) -> p h q", h=H)
    oR = sb("a_oR", [P, 512], F32)
    flat = E.rearrange("p h k -> p (h k)")
    oT, oN = flat[:, 0:512], flat[:, 512:1024]
    w = s["wattn"]

    ready = sem("a_ready")
    xn_ready = sem("a_xn")
    x_turned = sem("a_x_turned")
    xs_ready = sem("a_xs")
    q_full, k_full, v_full = sem("a_q_full"), sem("a_k_full"), sem("a_v_full")
    qv_ready = sem("a_qv")
    kbd_ready = sem("a_kbd_ready")
    s_full = sem("a_s_full")
    e_step = sem("a_e_step")
    p_ready = sem("a_p")
    t_full = sem("a_t_full")
    t_out_act = sem("a_t_out_act")
    t_out_dve = sem("a_t_out_dve")
    o_full = sem("a_o_full")
    o_step = sem("a_o_step")
    d_full = sem("a_d_full")
    y_full = sem("a_y_full")
    y_out = sem("a_y_out")

    with nc.Block() as block:
        @block.gpsimd
        def _(pool):
            pool.memset(pf[:, :, :], 0.0).then_inc(ready, 1)
            pool.memset(V[:, :, :], 1.0).then_inc(ready, 1)

        @block.vector
        def _(v):
            v.memset(psV[:, :], 0.0).then_inc(ready, 1)
            v.wait_ge(s["attn_loads"], s["attn_loads_total"])
            with v.Fori(0, NT) as n:
                xn_n = x1[:, bass.ds(n, 1), :].rearrange("p a f -> p (a f)")
                v.tensor_scalar(xn[:, :], xn_n, mv[:, bass.ds(n, 1), 0:1].rearrange("p a b -> p (a b)"),
                                rstd[:, bass.ds(n, 1)], ALU.subtract, ALU.mult).then_inc(xn_ready, 1)
                v.wait_ge(k_full, n + 1)
                for b in range(2):
                    for m in range(KT):
                        v.tensor_tensor(kbd[:, b, m, :].rearrange("p (h k) -> p h k", h=HT),
                                        psK[:, m * P + b * TQ:m * P + b * TQ + TQ].unsqueeze(1).to_broadcast([P, HT, TQ]),
                                        s["head_rows2"][:, :].unsqueeze(2).to_broadcast([P, HT, TQ]), ALU.mult)\
                         .then_inc(kbd_ready, 1)
                v.wait_ge(s_full, n + 1)
                v.scalar_tensor_tensor(out=E.rearrange("p h k -> p (h k)"), in0=psA[:, :], scalar=DK ** -0.5,
                                       in1=s["alibi"][:, :], op0=ALU.mult, op1=ALU.add).then_inc(e_step, 1)
                v.wait_ge(e_step, 3 * n + 1)
                v.tensor_reduce(mx[:, :], E[:, :, :], AX.X, ALU.max).then_inc(e_step, 1)
                v.wait_ge(e_step, 3 * n + 2)
                v.tensor_tensor(E[:, :, :], E[:, :, :], mx[:, :].unsqueeze(2).to_broadcast([P, H, TQ]), ALU.subtract)\
                 .then_inc(e_step, 1)
                for i in (1, 3):
                    v.wait_ge(t_full, 4 * n + i + 1)
                    v.tensor_copy(pT[:, 4 * i:4 * i + 4, :].rearrange("p h q -> p (h q)"), psT[:, i % 2, :]).then_inc(t_out_dve, 1)
                v.wait_ge(o_full, n + 1)
                v.tensor_copy(oT[:, :], psV[:, :]).then_inc(o_step, 1)
                v.wait_ge(d_full, n + 1)
                v.reciprocal(oR[:, :], psX[:, :]).then_inc(o_step, 1)
                v.wait_ge(o_step, 3 * n + 2)
                v.tensor_tensor(oN[:, :], oT[:, :], oR[:, :], ALU.mult).then_inc(o_step, 1)
                v.wait_ge(y_full, n + 1)
                v.tensor_tensor(x2[:, bass.ds(n, 1), :].rearrange("p a f -> p (a f)"), psQ[:, 0:DM], xn_n, ALU.add)\
                 .then_inc(y_out, 1)

        @block.scalar
        def _(act):
            act.wait_ge(ready, 3)
            with act.Fori(0, NT) as n:
                act.wait_ge(x_turned, n + 1)
                act.activation(xs.rearrange("p k t -> p (k t)"), psX[:, 0:2 * P], ACT.Copy).then_inc(xs_ready, 1)
                act.wait_ge(q_full, n + 1)
                act.activation(qs.rearrange("p k t -> p (k t)"), psQ[:, 0:2 * P], ACT.Copy).then_inc(qv_ready, 1)
                act.wait_ge(v_full, n + 1)
                act.activation(V[:, :, 0:DK], psT[:, 0, 0:DM].rearrange("p (h e) -> p h e", e=DK), ACT.Copy).then_inc(qv_ready, 1)
                act.wait_ge(e_step, 3 * n + 3)
                for b in range(2):
                    act.activation(pf[tok_rows(b), :, b * TQ:b * TQ + TQ], E[tok_rows(b), :, :], ACT.Exp).then_inc(p_ready, 1)
                for i in (0, 2):
                    act.wait_ge(t_full, 4 * n + i + 1)
                    act.activation(pT[:, 4 * i:4 * i + 4, :].rearrange("p h q -> p (h q)"), psT[:, i % 2, :], ACT.Copy)\
                       .then_inc(t_out_act, 1)

        @block.tensor
        def _(pe):
            pe.wait_ge(ready, 3)
            pe.wait_ge(s["attn_loads"], s["attn_loads_total"])
            with pe.Fori(0, NT) as n:
                pe.wait_ge(xn_ready, n + 1)
                for k in range(KT):
                    mm = pe.transpose(psX[:, k * P:k * P + P], xn[:, k * P:k * P + P], ident[:, :])
                mm.then_inc(x_turned, 1)
                pe.wait_ge(xs_ready, n + 1)
                for ps_out, f0, full in ((psQ, 0, q_full), (psK, DM, k_full)):
                    for m in range(KT):
                        for k in range(KT):
                            mm = pe.matmul(ps_out[:, m * P:m * P + P], w[:, k, f0 + m * P:f0 + m * P + P], xs[:, k, :],
                                           start=(k == 0), stop=(k == KT - 1), skip_group_check=True)
                    mm.then_inc(full, 1)
                for k in range(KT):
                    mm = pe.matmul(psT[:, 0, 0:DM], xs[:, k, :], w[:, k, 2 * DM:3 * DM], start=(k == 0), stop=(k == KT - 1))
                mm.then_inc(v_full, 1)
                pe.wait_ge(qv_ready, 2 * n + 2)
                pe.wait_ge(kbd_ready, 4 * n + 4)
                for b in range(2):
                    for m in range(KT):
                        mm = pe.matmul(psA[tok_rows(b), m * 512:m * 512 + 512], qs[:, m, b * TQ:b * TQ + TQ],
                                       kbd[:, b, m, :], start=True, stop=True)
                mm.then_inc(s_full, 1)
                pe.wait_ge(p_ready, 2 * n + 2)
                for i in range(4):
                    if i == 2:
                        pe.wait_ge(t_out_act, 2 * n + 1)
                    if i == 3:
                        pe.wait_ge(t_out_dve, 2 * n + 1)
                    for h in range(4 * i, 4 * i + 4):
                        mm = pe.transpose(psT[:, i % 2, (h % 4) * P:(h % 4) * P + P], pf[:, h, :], ident[:, :])
                    mm.then_inc(t_full, 1)
                pe.wait_ge(t_out_act, 2 * n + 2)
                pe.wait_ge(t_out_dve, 2 * n + 2)
                for h in range(H):
                    r, g = 32 * (h % 4), h // 4
                    mm = pe.matmul(psV[r:r + DK + 1, g * P:g * P + P], V[:, h, :], pT[:, h, :], start=(g == 0), stop=True,
                                   skip_group_check=True)
                mm.then_inc(o_full, 1)
                pe.wait_ge(o_step, 3 * n + 1)
                pe.matmul(psX[:, :], s["den_rows2"][:, :], oT[:, :], start=True, stop=True).then_inc(d_full, 1)
                pe.wait_ge(o_step, 3 * n + 3)
                for g in range(4):
                    mm = pe.matmul(psQ[:, 0:DM], oN[:, g * P:g * P + P], s["wprojP"][:, g, :], start=(g == 0), stop=(g == 3))
                mm.then_inc(y_full, 1)


def switch_head(nc, d, s, sb, ps, sem):
    x2, x3, ident = s["x2"], s["x3"], s["ident"]
    psV = ps("f_psV", [P, 4, 512])
    psU = ps("f_psU", [P, 2, 512])
    psC = ps("f_psC", [P, 2, 512])
    mv = sb("f_mv", [P, NT, 2], F32)
    rstd = sb("f_rstd", [P, NT], F32)
    norm_stats(nc, x2, mv, rstd, sb, sem, "f")
    xn = sb("f_xn", [P, DM], F32)
    xs = sb("f_xs", [P, KT, P], F32)
    qT = sb("f_qT", [P, FH, P], F32)
    kT = sb("f_kT", [P, FH, P], F32)
    E = sb("f_E", [P, FH, TQ], F32)
    mx = sb("f_mx", [P, FH], F32)
    pf = sb("f_pf", [P, FH, P], F32)
    rden = sb("f_rden", [P, FH], F32)
    pT = sb("f_pT", [P, FH, P], F32)
    vh = sb("f_vh", [P, 2, P], F32)
    cT = sb("f_cT", [P, 2, P], F32)
    G = 2 * FH
    ex = sb("f_ex", [P, G, FE], F32)
    pr = sb("f_pr", [P, G, FE], F32)
    eq = sb("f_eq", [P, G, FE], F32)
    one1 = sb("f_one1", [P, G, FE], F32)
    one2 = sb("f_one2", [P, G, FE], F32)
    top1 = sb("f_top1", [P, G], F32)
    top2 = sb("f_top2", [P, G], F32)
    pick = sb("f_pick", [P, G], F32)
    tot = sb("f_tot", [P, G], F32)
    gate = sb("f_gate", [P, G, FE], F32)
    vw, ow, qw, kw, sel = s["vw"], s["ow"], s["qw"], s["kw"], s["sel"]

    ready = sem("f_ready")
    xn_ready = sem("f_xn")
    x_turned = sem("f_x_turned")
    xs_ready = sem("f_xs_ready")
    l_full = sem("f_l_full")
    l_exp = sem("f_l_exp")
    g_step = sem("f_g_step")
    qk_full = sem("f_qk_full")
    qk_out = sem("f_qk_out")
    s_full = sem("f_s_full")
    e_step = sem("f_e_step")
    p_ready = sem("f_p")
    t_full = sem("f_t_full")
    t_out = sem("f_t_out")
    v_full = sem("f_v_full")
    v_step = sem("f_v_step")
    c_full = sem("f_c_full")
    c_out = sem("f_c_out")
    u_full = sem("f_u_full")
    u_step = sem("f_u_step")
    r_step = sem("f_r_step")
    GS = 18
    SCALE = 1.0 / math.sqrt(FP)

    def bc(a):
        return a[:, :].unsqueeze(2).to_broadcast([P, G, FE])

    with nc.Block() as block:
        @block.gpsimd
        def _(pool):
            pool.memset(pf[:, :, :], 0.0).then_inc(ready, 1)

        @block.vector
        def _(v):
            v.wait_ge(s["ffn_loads"], s["ffn_loads_total"])

            def gates(n):
                count = [0]

                def step(op):
                    count[0] += 1
                    op.then_inc(g_step, 1)
                    v.wait_ge(g_step, GS * n + count[0])
                rank = s["rank"][:, :].unsqueeze(1).to_broadcast([P, G, FE])
                v.wait_ge(l_exp, n + 1)
                step(v.tensor_scalar(ex[:, :, :], ex[:, :, :], 1.0, None, ALU.add))
                step(v.reciprocal(pr[:, :, :], ex[:, :, :]))
                step(v.tensor_reduce(top1[:, :], pr[:, :, :], AX.X, ALU.max))
                step(v.tensor_tensor(eq[:, :, :], pr[:, :, :], bc(top1), ALU.is_equal))
                step(v.tensor_tensor(eq[:, :, :], eq[:, :, :], rank, ALU.mult))
                step(v.tensor_reduce(pick[:, :], eq[:, :, :], AX.X, ALU.max))
                step(v.tensor_tensor(one1[:, :, :], bc(pick), rank, ALU.is_equal))
                step(v.scalar_tensor_tensor(out=ex.rearrange("p g e -> p (g e)"), in0=one1.rearrange("p g e -> p (g e)"),
                                            scalar=-2.0, in1=pr.rearrange("p g e -> p (g e)"), op0=ALU.mult, op1=ALU.add))
                step(v.tensor_reduce(top2[:, :], ex[:, :, :], AX.X, ALU.max))
                step(v.tensor_tensor(eq[:, :, :], ex[:, :, :], bc(top2), ALU.is_equal))
                step(v.tensor_tensor(eq[:, :, :], eq[:, :, :], rank, ALU.mult))
                step(v.tensor_reduce(pick[:, :], eq[:, :, :], AX.X, ALU.max))
                step(v.tensor_tensor(one2[:, :, :], bc(pick), rank, ALU.is_equal))
                step(v.tensor_tensor(tot[:, :], top1[:, :], top2[:, :], ALU.add))
                step(v.tensor_scalar(tot[:, :], tot[:, :], 1e-9, None, ALU.max))
                step(v.reciprocal(tot[:, :], tot[:, :]))
                step(v.tensor_tensor(gate[:, :, :], one1[:, :, :], one2[:, :, :], ALU.add))
                step(v.tensor_tensor(gate[:, :, :], gate[:, :, :], pr[:, :, :], ALU.mult))
                return count[0]

            def gate_scale(n):
                v.tensor_scalar(tot[:, :], tot[:, :], s["route"][:, 0:1], None, ALU.mult).then_inc(r_step, 1)
                v.wait_ge(p_ready, 2 * n + 2)
                v.tensor_reduce(rden[:, :], pf[:, :, :], AX.X, ALU.add).then_inc(r_step, 1)
                v.wait_ge(r_step, 5 * n + 2)
                v.reciprocal(rden[:, :], rden[:, :]).then_inc(r_step, 1)
                v.wait_ge(r_step, 5 * n + 3)
                v.tensor_tensor(tot[:, FH:G], tot[:, FH:G], rden[:, :], ALU.mult).then_inc(r_step, 1)
                v.wait_ge(r_step, 5 * n + 4)
                v.tensor_tensor(gate[:, :, :], gate[:, :, :], bc(tot), ALU.mult).then_inc(r_step, 1)
                v.wait_ge(r_step, 5 * n + 5)

            def values(n, h):
                for e in range(FE):
                    k = 64 * n + 8 * h + e
                    if e % 4 == 0:
                        v.wait_ge(v_full, 16 * n + 2 * h + e // 4 + 1)
                    src = psV[:, 2 * (h % 2) + e // 4, (e % 4) * FP:(e % 4) * FP + FP]
                    g = gate[:, h, e:e + 1]
                    if e == 0:
                        if h >= 2:
                            v.wait_ge(c_full, 8 * n + h - 1)
                        v.tensor_scalar(vh[:, h % 2, :], src, g, None, ALU.mult).then_inc(v_step, 1)
                    else:
                        v.wait_ge(v_step, k)
                        v.scalar_tensor_tensor(out=vh[:, h % 2, :], in0=src, scalar=g, in1=vh[:, h % 2, :],
                                               op0=ALU.mult, op1=ALU.add).then_inc(v_step, 1)

            def outputs(n, h):
                acc = x3[:, bass.ds(n, 1), :].rearrange("p a f -> p (a f)")
                for e in range(FE):
                    k = 64 * n + 8 * h + e
                    if e % 2 == 0:
                        v.wait_ge(u_full, 32 * n + 4 * h + e // 2 + 1)
                    if not (h == 0 and e == 0):
                        v.wait_ge(u_step, k)
                    first = x2[:, bass.ds(n, 1), :].rearrange("p a f -> p (a f)") if h == 0 and e == 0 else acc
                    v.scalar_tensor_tensor(out=acc, in0=psU[:, (e // 2) % 2, (e % 2) * DM:(e % 2) * DM + DM],
                                           scalar=gate[:, FH + h, e:e + 1], in1=first,
                                           op0=ALU.mult, op1=ALU.add).then_inc(u_step, 1)

            with v.Fori(0, NT) as n:
                v.tensor_scalar(xn[:, :], x2[:, bass.ds(n, 1), :].rearrange("p a f -> p (a f)"),
                                mv[:, bass.ds(n, 1), 0:1].rearrange("p a b -> p (a b)"),
                                rstd[:, bass.ds(n, 1)], ALU.subtract, ALU.mult).then_inc(xn_ready, 1)
                assert gates(n) == GS
                v.wait_ge(s_full, n + 1)
                v.tensor_reduce(mx[:, :], psC[:, 1, :].rearrange("p (h k) -> p h k", h=FH), AX.X, ALU.max).then_inc(e_step, 1)
                v.wait_ge(e_step, 2 * n + 1)
                v.tensor_tensor(E[:, :, :], psC[:, 1, :].rearrange("p (h k) -> p h k", h=FH),
                                mx[:, :].unsqueeze(2).to_broadcast([P, FH, TQ]), ALU.subtract).then_inc(e_step, 1)
                gate_scale(n)
                values(n, 0)
                for h in range(FH):
                    if h + 1 < FH:
                        values(n, h + 1)
                    outputs(n, h)

        @block.scalar
        def _(act):
            act.wait_ge(ready, 1)
            with act.Fori(0, NT) as n:
                act.wait_ge(x_turned, n + 1)
                act.activation(xs.rearrange("p k t -> p (k t)"), psC[:, 0, 0:2 * P], ACT.Copy).then_inc(xs_ready, 1)
                act.wait_ge(l_full, n + 1)
                act.activation(ex.rearrange("p g e -> p (g e)"), psC[:, 1, 0:P], ACT.Exp, scale=-1.0).then_inc(l_exp, 1)
                for i in range(4):
                    act.wait_ge(qk_full, 4 * n + i + 1)
                    dst = (qT, kT)[i // 2][:, 4 * (i % 2):4 * (i % 2) + 4, :].rearrange("p h t -> p (h t)")
                    act.activation(dst, psV[:, i, :], ACT.Copy).then_inc(qk_out, 1)
                act.wait_ge(e_step, 2 * n + 2)
                for b in range(2):
                    act.activation(pf[tok_rows(b), :, b * TQ:b * TQ + TQ], E[tok_rows(b), :, :], ACT.Exp, scale=SCALE)\
                       .then_inc(p_ready, 1)
                for i in range(2):
                    act.wait_ge(t_full, 2 * n + i + 1)
                    act.activation(pT[:, 4 * i:4 * i + 4, :].rearrange("p h q -> p (h q)"), psC[:, i, :], ACT.Copy)\
                       .then_inc(t_out, 1)
                for h in range(FH):
                    act.wait_ge(c_full, 8 * n + h + 1)
                    act.activation(cT[:, h % 2, :], psC[:, h % 2, 0:P], ACT.Copy).then_inc(c_out, 1)

        @block.tensor
        def _(pe):
            pe.wait_ge(ready, 1)
            pe.wait_ge(s["ffn_loads"], s["ffn_loads_total"])

            def values(n, h):
                for i in range(2):
                    if h >= 2:
                        pe.wait_ge(v_step, 64 * n + 8 * (h - 2) + 4 * i + 4)
                    for k in range(KT):
                        mm = pe.matmul(psV[:, 2 * (h % 2) + i, :], xs[:, k, :], vw[:, k, h, 512 * i:512 * i + 512],
                                       start=(k == 0), stop=(k == KT - 1))
                    mm.then_inc(v_full, 1)

            def context(n, h):
                pe.wait_ge(v_step, 64 * n + 8 * h + 8)
                if h >= 2:
                    pe.wait_ge(c_out, 8 * n + h - 1)
                pe.matmul(psC[:, h % 2, 0:P], vh[:, h % 2, :], pT[:, h, :], start=True, stop=True).then_inc(c_full, 1)

            def outputs(n, h):
                pe.wait_ge(c_out, 8 * n + h + 1)
                for i in range(4):
                    if i >= 2 or h >= 1:
                        pe.wait_ge(u_step, 64 * n + 8 * h + 2 * i - 2)
                    pe.matmul(psU[:, i % 2, :], cT[:, h % 2, :], ow[:, h, 512 * i:512 * i + 512], start=True, stop=True)\
                      .then_inc(u_full, 1)

            with pe.Fori(0, NT) as n:
                pe.wait_ge(xn_ready, n + 1)
                for k in range(KT):
                    mm = pe.transpose(psC[:, 0, k * P:k * P + P], xn[:, k * P:k * P + P], ident[:, :])
                mm.then_inc(x_turned, 1)
                pe.wait_ge(xs_ready, n + 1)
                for k in range(KT):
                    mm = pe.matmul(psC[:, 1, 0:P], xs[:, k, :], sel[:, k, :], start=(k == 0), stop=(k == KT - 1))
                mm.then_inc(l_full, 1)
                for i in range(4):
                    w = (qw, kw)[i // 2]
                    for h in range(4 * (i % 2), 4 * (i % 2) + 4):
                        for k in range(KT):
                            mm = pe.matmul(psV[:, i, (h % 4) * P:(h % 4) * P + P], w[:, k, h * FP:h * FP + FP], xs[:, k, :],
                                           start=(k == 0), stop=(k == KT - 1), skip_group_check=True)
                    mm.then_inc(qk_full, 1)
                pe.wait_ge(qk_out, 4 * n + 4)
                pe.wait_ge(l_exp, n + 1)
                for h in range(FH):
                    for b in range(2):
                        c = slice(b * TQ, b * TQ + TQ)
                        mm = pe.matmul(psC[tok_rows(b), 1, h * TQ:h * TQ + TQ], qT[:, h, c], kT[:, h, c], start=True, stop=True,
                                       skip_group_check=True)
                mm.then_inc(s_full, 1)
                values(n, 0)
                pe.wait_ge(p_ready, 2 * n + 2)
                for i in range(2):
                    for h in range(4 * i, 4 * i + 4):
                        mm = pe.transpose(psC[:, i, (h % 4) * P:(h % 4) * P + P], pf[:, h, :], ident[:, :])
                    mm.then_inc(t_full, 1)
                pe.wait_ge(t_out, 2 * n + 2)
                for h in range(FH):
                    if h + 1 < FH:
                        values(n, h + 1)
                    context(n, h)
                    outputs(n, h)


def build(nc, d, out, stages=3):
    with ExitStack() as whole:
        def sem(name):
            return whole.enter_context(nc.semaphore(name))
        def keep(name, shape, dt):
            return whole.enter_context(nc.sbuf_tensor(name, shape, dt))
        s = {}
        s["ident"] = keep("ident", [P, P], F32)
        s["x1"] = keep("x1", [P, NT, DM], F32)
        with ExitStack() as st:
            def sb(name, shape, dt):
                return st.enter_context(nc.sbuf_tensor(name, shape, dt))
            s["psS"] = st.enter_context(nc.psum_tensor("psS", [P, 2, 1024], F32))
            s["psW"] = st.enter_context(nc.psum_tensor("psW", [P, 3, 512], F32))
            s["psO"] = st.enter_context(nc.psum_tensor("psO", [P, 512], F32))
            s["identb"] = sb("identb", [P, P], BF16)
            s["head_rows"] = sb("head_rows", [P, 4], F32)
            s["den_rows"] = sb("den_rows", [P, P], F32)
            s["wH"] = sb("wH", [P, 2, KT, DM], F32R)
            s["wL"] = sb("wL", [P, 2, KT, DM], F32R)
            s["woP"] = sb("woP", [P, 4, DM], F32)
            s["qD"] = sb("qD", [P, 4, TOK], F32)
            s["dT"] = sb("dT", [P, 2, H * TQ], F32)
            s["dN"] = sb("dN", [P, H // 2, NEAR], BF16)
            s["ctx"] = sb("ctx", [P, 2, KT, 512], F32)
            s["mcols"] = sb("mcols", [P, 2, NKT, B], F32)
            s["V"] = [sb(f"V{i}", [P, NKT, H, DK + 1], F32) for i in range(2)]
            with ExitStack() as pro:
                def sbp(name, shape, dt):
                    return pro.enter_context(nc.sbuf_tensor(name, shape, dt))
                s["xn"] = sbp("xn", [P, NT, DM], F32)
                s["xnT"] = sbp("xnT", [P, KT, TOK], F32)
                prologue(nc, d, s, sbp, sem)
            cross_attention(nc, d, s, sb, sem)
        with ExitStack() as st:
            def sb(name, shape, dt):
                return st.enter_context(nc.sbuf_tensor(name, shape, dt))
            loads = sem("late_loads")
            s["x2"] = sb("x2", [P, NT, DM], F32)
            s["wattn"] = sb("wattn", [P, KT, 3 * DM], F32)
            s["wprojP"] = sb("wprojP", [P, 4, DM], F32)
            s["alibi"] = sb("alibi", [P, H * TQ], F32)
            s["head_rows2"] = sb("head_rows2", [P, HT], F32)
            s["den_rows2"] = sb("den_rows2", [P, P], F32)
            s["vw"] = sb("vw", [P, KT, FH, FE * FP], F32)
            s["ow"] = sb("ow", [P, FH, FE * DM], F32)
            s["qw"] = sb("qw", [P, KT, FH * FP], F32)
            s["kw"] = sb("kw", [P, KT, FH * FP], F32)
            s["sel"] = sb("sel", [P, KT, 2 * FH * FE], F32)
            s["rank"] = sb("rank", [P, FE], F32)
            s["route"] = sb("route", [P, 1], F32)
            zeroed = sem("wproj_zeroed")
            s["attn_loads"], s["ffn_loads"] = sem("attn_loads"), sem("ffn_loads")
            first = [
                (s["wattn"][:, :, :], d["aWT"].rearrange("(k p) f -> p k f", p=P)),
                (s["alibi"][:, :], d["c_alibi"]),
                (s["head_rows2"][:, :], d["c_head_rows"]),
                (s["den_rows2"][:, :], d["c_den_rows"]),
            ]
            wo_view = d["aPT"].rearrange("(g j e) n -> j e g n", j=4, e=DK)
            first += [(s["wprojP"][32 * j:32 * j + DK, :, :], wo_view[j]) for j in range(4)]
            late = [
                (s["sel"][:, :, :], d["selT"].rearrange("(k p) f -> p k f", p=P)),
                (s["rank"][:, :], d["c_rank"].to_broadcast([P, FE])),
                (s["route"][:, :], d["route"].rearrange("(a b) -> a b", a=1).to_broadcast([P, 1])),
                (s["qw"][:, :, :], d["qwT"].rearrange("(k p) f -> p k f", p=P)),
                (s["kw"][:, :, :], d["kwT"].rearrange("(k p) f -> p k f", p=P)),
            ]
            for h in range(FH):
                late.append((s["vw"][:, :, h, :], d["vw"].rearrange("(k p) h f -> h p k f", p=P)[h]))
                late.append((s["ow"][:, h, :], d["ow"].rearrange("h p f -> p h f")[:, h, :]))
            s["attn_loads_total"], s["ffn_loads_total"] = 16 * len(first), 16 * len(late)
            with nc.Block() as block:
                @block.gpsimd
                def _(pool):
                    pool.memset(s["wprojP"][:, :, :], 0.0).then_inc(zeroed, 1)

                @block.sync
                def _(sp):
                    sp.wait_ge(zeroed, 1)
                    for dst, src in first:
                        sp.dma_start(dst, src).then_inc(s["attn_loads"], 16)
                    for dst, src in late:
                        sp.dma_start(dst, src).then_inc(s["ffn_loads"], 16)
            with ExitStack() as sa:
                self_attention(nc, d, s, lambda n, sh, dt: sa.enter_context(nc.sbuf_tensor(n, sh, dt)),
                               lambda n, sh: sa.enter_context(nc.psum_tensor(n, sh, F32)), sem)
            if stages == 3:
                s["x3"] = s["x1"]
                with ExitStack() as sf:
                    switch_head(nc, d, s, lambda n, sh, dt: sf.enter_context(nc.sbuf_tensor(n, sh, dt)),
                                lambda n, sh: sf.enter_context(nc.psum_tensor(n, sh, F32)), sem)
            wrote = sem("wrote")
            with nc.Block() as block:
                @block.sync
                def _(sp):
                    sp.dma_start(out.rearrange("(n p) f -> p n f", p=P), s["x1" if stages == 3 else "x2"][:, :, :])\
                      .then_inc(wrote, 16)
                    sp.wait_ge(wrote, 16)


def layout(i):
    import numpy as _np
    C = _np.ascontiguousarray
    v = _np.asarray(i["L0_ffn_v_w"]).reshape(FH, FE, DM, FP).transpose(2, 0, 1, 3).reshape(DM, FH, FE * FP)
    o = _np.asarray(i["L0_ffn_o_w"]).reshape(FH, FE, FP, DM).transpose(0, 2, 1, 3).reshape(FH, FP, FE * DM)
    sel = _np.concatenate([_np.asarray(i["L0_ffn_sel_v_w"]), _np.asarray(i["L0_ffn_sel_o_w"])])
    ins = {
        "x": _np.asarray(i["x"]).reshape(TOK, DM),
        "ctxT": C(_np.asarray(i["ctx_1024"]).transpose(0, 2, 1)),
        "mask": _np.asarray(i["mask_Bx1x1xS2_bk0"]).reshape(B, TK),
        "xWqD": C(_np.stack(2 * [_np.asarray(i["L0_xattn_Wq"]).T.reshape(DM, 4, 64)], axis=2).reshape(DM, 4, P)),
        "xWkT": C(_np.asarray(i["L0_xattn_Wk"]).T),
        "xWvT": C(_np.asarray(i["L0_xattn_Wv"]).T), "xWoT": C(_np.asarray(i["L0_xattn_Wo"]).T),
        "rbT": C(_np.asarray(i["L0_xattn_rel_bias"]).T),
        "aWT": C(_np.asarray(i["L0_attn_W_attn"]).T), "aPT": C(_np.asarray(i["L0_attn_W_proj"]).T),
        "qwT": C(_np.asarray(i["L0_ffn_q_w"]).T), "kwT": C(_np.asarray(i["L0_ffn_k_w"]).T),
        "vw": C(v), "ow": C(o), "selT": C(sel.T), "route": C(_np.asarray(i["L0_ffn_route_scale"])),
    }
    ins.update(constants())
    return ins


def kernel(**inputs):
    import concourse.bacc as _bacc
    from concourse import mybir as _mybir
    from concourse.bass_utils import run_bass_kernel_spmd as _run

    nc = _bacc.Bacc("TRN2", target_bir_lowering=False, num_devices=1)
    arrays, args = {}, {}
    for name, a in layout(inputs).items():
        arrays[f"in_{name}"] = a
        args[name] = nc.dram_tensor(f"in_{name}", a.shape, _mybir.dt.from_np(a.dtype), kind="ExternalInput").ap()
    out = nc.dram_tensor("out_0", (TOK, DM), F32, kind="ExternalOutput").ap()
    build(nc, args, out)
    r = _run(nc, [arrays], core_ids=[0])
    return r.results[0]["out_0"].reshape(B, TQ, DM)
```

```python
import math
from contextlib import ExitStack

import numpy as np

import concourse.bass as bass
from concourse import mybir

F32 = mybir.dt.float32
F32R = mybir.dt.float32r
BF16 = mybir.dt.bfloat16
U8 = mybir.dt.uint8
ALU = mybir.AluOpType
ACT = mybir.ActivationFunctionType
AX = mybir.AxisListType

P = 128
B, TQ, DM = 16, 64, 256
TOK = B * TQ
NT = TOK // P
KT = DM // P
H, DK = 16, 16
HT = P // DK
TK = 1601
KTILES = [(t * P, min(P, TK - t * P)) for t in range((TK + P - 1) // P)]
NKT = len(KTILES)
CHUNKS = [(0, 1, 2, 3), (4, 5, 6), (7, 8, 9), (10, 11, 12)]
NC = len(CHUNKS)
CSPAN = [(KTILES[c[0]][0], sum(KTILES[t][1] for t in c)) for c in CHUNKS]
NEAR = 256
NEG = 1.0e9
EPS = 1e-5
FH, FE, FP = 8, 8, 128
BUCKETS, MAXDIST = 32, 128


def relative_buckets(rel):
    nb = BUCKETS // 2
    rp = np.abs(rel)
    exact = nb // 2
    large = exact + (np.log(np.maximum(rp, 1).astype(np.float32) / np.float32(exact))
                     / np.float32(math.log(MAXDIST / exact)) * np.float32(nb - exact)).astype(np.int32)
    large = np.minimum(large, nb - 1)
    return (rel > 0).astype(np.int32) * nb + np.where(rp < exact, rp, large)


def constants():
    rel = np.arange(NEAR + TQ - 1) - (TQ - 1)
    onehot = (np.arange(BUCKETS)[:, None] == relative_buckets(rel)[None, :]).astype(np.float32)
    assert relative_buckets(np.arange(NEAR - TQ + 1, TK)).min() == BUCKETS - 1
    part = np.arange(P)
    head_rows = (part[:, None] // DK == np.arange(HT)[None, :]).astype(np.float32)
    den_rows = (part[:, None] == 32 * (part[None, :] // 32) + DK).astype(np.float32)
    start = 2.0 ** (-2.0 ** (-(math.log2(H) - 3)))
    slopes = np.array([start * start ** i for i in range(H)], np.float32)
    pos = np.arange(TQ, dtype=np.float32)
    dist = pos[None, :] - pos[:, None]
    alibi = slopes[None, :, None] * dist[:, None, :]
    alibi = np.where((dist <= 0)[:, None, :], alibi, np.float32(-1e30)).reshape(TQ, H * TQ)
    return {
        "c_onehot": onehot,
        "c_head_rows": head_rows,
        "c_head_rows4": (part[:, None] % 64 // DK == np.arange(4)[None, :]).astype(np.float32),
        "c_den_rows": den_rows,
        "c_rank": (FE - np.arange(FE, dtype=np.float32)).reshape(1, FE),
        "c_ident": np.eye(P, dtype=np.float32),
        "c_alibi": np.concatenate([alibi, alibi]).astype(np.float32),
    }


def tok_rows(par):
    return slice(TQ * par, TQ * par + TQ)


def layer_norm_steps(v, x, stats, mv, rstd, xn, step, nc_scalar=None):
    for n in range(NT):
        v.bn_stats(stats[:, n, :], x[:, n, :]).then_inc(step, 1)
    v.wait_ge(step, NT)
    for n in range(NT):
        v.bn_aggr(mv[:, n, :], stats[:, n, :]).then_inc(step, 1)
    v.wait_ge(step, 2 * NT)
    v.tensor_scalar(rstd[:, :], mv[:, :, 1], EPS, None, ALU.add).then_inc(step, 1)


def prologue(nc, d, s, sb, sem):
    xn, xnT = s["xn"], s["xnT"]
    psW, psS, psO = s["psW"], s["psS"], s["psO"]
    loads = sem("pro_loads")
    consts = sem("pro_consts")
    ln = sem("pro_ln")
    root = sem("pro_root")
    xn_ready = sem("pro_xn")
    turned = sem("pro_turned")
    xnT_out = sem("pro_xnT")
    q_full = sem("pro_q")
    q_out = sem("pro_q_out")
    w_hi = sem("pro_w_hi")
    rb_ready = sem("pro_rb")
    near_full = sem("pro_near")
    near_out = sem("pro_near_out")
    dN_full = sem("pro_dN")
    dN_out = sem("pro_dN_out")
    mrow = sem("pro_mrow")
    m_full = sem("pro_m_full")
    m_out = sem("pro_m_out")
    rbT = sb("rbT", [BUCKETS, H], F32)
    rb_far = sb("rb_far", [BUCKETS, H], F32)
    rbd = sb("rbd", [BUCKETS, H], F32)
    onehot = sb("onehot", [BUCKETS, NEAR + TQ - 1], F32)
    m16 = sb("m16", [B, TK], U8)
    m16f = sb("m16f", [B, TK], F32)
    mb16 = sb("mb16", [B, TK], F32)
    any16 = sb("any16", [B, 2], F32)
    stats = sb("stats", [P, NT, 6], F32)
    mv = sb("mv", [P, NT, 2], F32)
    rstd = sb("rstd", [P, NT], F32)
    wq = sb("wq", [P, KT, 4, P], F32)
    wkv = sb("wkv", [P, 2, KT, DM], F32)
    dma_list = [
        (s["x1"][:, :, :], d["x"].rearrange("(n p) f -> p n f", p=P)),
        (s["ident"][:, :], d["c_ident"]),
        (wq[:, :, :, :], d["xWqD"].rearrange("(k p) g f -> p k g f", p=P)),
        (onehot[:, :], d["c_onehot"]),
        (rbT[:, :], d["rbT"]),
        (rb_far[:, :], d["rbT"][BUCKETS - 1:BUCKETS, :].to_broadcast([BUCKETS, H])),
        (m16[:, :], d["mask"]),
        (s["head_rows"][:, :], d["c_head_rows4"]),
        (wkv[:, 0, :, :], d["xWkT"].rearrange("(k p) f -> p k f", p=P)),
        (wkv[:, 1, :, :], d["xWvT"].rearrange("(k p) f -> p k f", p=P)),
        (s["den_rows"][:, :], d["c_den_rows"]),
    ]
    wo_view = d["xWoT"].rearrange("(g j e) n -> j e g n", j=4, e=DK)
    NL = 16 * (len(dma_list) + 4)
    with nc.Block() as block:
        @block.sync
        def _(sp):
            for dst, src in dma_list:
                sp.dma_start(dst, src).then_inc(loads, 16)
            sp.wait_ge(consts, 1)
            for j in range(4):
                sp.dma_start(s["woP"][32 * j:32 * j + DK, :, :], wo_view[j]).then_inc(loads, 16)
            sp.wait_ge(loads, NL)

        @block.gpsimd
        def _(pool):
            pool.memset(s["woP"][:, :, :], 0.0).then_inc(consts, 1)
            pool.memset(s["ctx"][:, 1, :, CSPAN[-1][1]:CSPAN[-1][1] + 1], 0.0).then_inc(consts, 1)
            for par in range(2):
                pool.memset(s["V"][par][:, :, :, DK:DK + 1], 1.0).then_inc(consts, 1)
            pool.wait_ge(loads, NL)
            pool.tensor_copy(s["identb"][:, :], s["ident"][:, :]).then_inc(consts, 1)
            pool.wait_ge(w_hi, 1)
            pool.tensor_tensor(s["wL"][:, :, :, :], wkv[:, :, :, :], s["wH"][:, :, :, :].bitcast(F32), ALU.subtract)\
                .then_inc(consts, 1)

        @block.vector
        def _(v):
            v.memset(psO[:, :], 0.0)
            v.memset(psW[:, 2, :], 0.0).then_inc(mrow, 1)
            v.wait_ge(loads, NL)
            layer_norm_steps(v, s["x1"], stats, mv, rstd, xn, ln)
            v.tensor_copy(m16f[:, :], m16[:, :]).then_inc(mrow, 1)
            v.wait_ge(mrow, 2)
            v.tensor_reduce(any16[:, 0:1], m16f[:, :], AX.X, ALU.max).then_inc(mrow, 1)
            v.wait_ge(mrow, 3)
            v.tensor_scalar(any16[:, 1:2], any16[:, 0:1], NEG, None, ALU.mult).then_inc(mrow, 1)
            v.wait_ge(mrow, 4)
            v.tensor_scalar(mb16[:, :], m16f[:, :], -1.0, any16[:, 1:2], ALU.add, ALU.mult).then_inc(mrow, 1)
            v.tensor_tensor(rbd[:, :], rbT[:, :], rb_far[:, :], ALU.subtract).then_inc(rb_ready, 1)
            v.wait_ge(root, 1)
            v.reciprocal(rstd[:, :], rstd[:, :]).then_inc(ln, 1)
            v.wait_ge(ln, 2 * NT + 2)
            for n in range(NT):
                v.tensor_scalar(xn[:, n, :], s["x1"][:, n, :], mv[:, n, 0:1], rstd[:, n:n + 1],
                                ALU.subtract, ALU.mult).then_inc(xn_ready, 1)
            for i in range(4):
                v.wait_ge(turned, i + 1)
                v.tensor_copy(xnT[:, i // 2, (i % 2) * 512:(i % 2) * 512 + 512], psS[:, i // 2, (i % 2) * 512:(i % 2) * 512 + 512])\
                 .then_inc(xnT_out, 1)
            v.wait_ge(m_full, 1)
            v.tensor_copy(s["mcols"].rearrange("p a t b -> p (a t b)"), psW[:, 2, 0:2 * NKT * B]).then_inc(m_out, 1)
            for i in range(8):
                v.wait_ge(q_full, i + 1)
                g, c = i // 2, slice((i % 2) * 512, (i % 2) * 512 + 512)
                v.tensor_copy(s["qD"][:, g, c], psW[:, i % 2, :]).then_inc(q_out, 1)
            for t in range(2):
                v.wait_ge(near_full, t + 1)
                v.tensor_copy(s["dT"][:, t, :].rearrange("p (h q) -> p h q", q=TQ),
                              psS[:, t, :].rearrange("p (q h) -> p h q", h=H)).then_inc(near_out, 1)
            for i in range(4):
                v.wait_ge(dN_full, i + 1)
                v.tensor_copy(s["dN"][:, 2 * i:2 * i + 2, :], psW[:, i % 2, :].rearrange("p (a k) -> p a k", a=2))\
                 .then_inc(dN_out, 1)

        @block.scalar
        def _(act):
            act.wait_ge(loads, NL)
            act.activation(s["wH"][:, :, :, :], wkv[:, :, :, :], ACT.Copy).then_inc(w_hi, 1)
            act.wait_ge(ln, 2 * NT + 1)
            act.activation(rstd[:, :], rstd[:, :], ACT.Sqrt).then_inc(root, 1)

        @block.tensor
        def _(pe):
            pe.wait_ge(loads, NL)
            pe.wait_ge(mrow, 5)
            for a, rows in enumerate((m16f, mb16)):
                for t, (k0, kw) in enumerate(KTILES):
                    c = (a * NKT + t) * B
                    mm = pe.transpose(psW[0:kw, 2, c:c + B], rows[:, k0:k0 + kw], s["ident"][0:B, 0:B])
            mm.then_inc(m_full, 1)
            for i in range(4):
                for n in range(4):
                    pe.wait_ge(xn_ready, (i % 2) * 4 + n + 1)
                    mm = pe.transpose(psS[:, i // 2, (i % 2) * 512 + n * P:(i % 2) * 512 + n * P + P],
                                      xn[:, (i % 2) * 4 + n, (i // 2) * P:(i // 2) * P + P], s["ident"][:, :])
                mm.then_inc(turned, 1)
            pe.wait_ge(xnT_out, 4)
            for i in range(8):
                if i >= 2:
                    pe.wait_ge(q_out, i - 1)
                for k in range(KT):
                    mm = pe.matmul(psW[:, i % 2, :], wq[:, k, i // 2, :],
                                   xnT[:, k, (i % 2) * 512:(i % 2) * 512 + 512], start=(k == 0), stop=(k == KT - 1))
                mm.then_inc(q_full, 1)
            pe.wait_ge(rb_ready, 1)
            for t in range(2):
                for q in range(TQ):
                    off = t * P - q + TQ - 1
                    mm = pe.matmul(psS[:, t, q * H:q * H + H], onehot[:, off:off + P],
                                   rbd[:, :], start=True, stop=True, skip_group_check=True)
                mm.then_inc(near_full, 1)
            pe.wait_ge(near_out, 2)
            for i in range(4):
                pe.wait_ge(q_out, 8)
                if i >= 2:
                    pe.wait_ge(dN_out, i - 1)
                for a in range(2):
                    for t in range(2):
                        pr = 2 * i + a
                        mm = pe.transpose(psW[:, i % 2, a * NEAR + t * P:a * NEAR + t * P + P],
                                          s["dT"][:, t, pr * P:pr * P + P], s["ident"][:, :])
                mm.then_inc(dN_full, 1)


def cross_attention(nc, d, s, sb, sem):
    psS, psW, psO = s["psS"], s["psW"], s["psO"]
    ctx = s["ctx"]
    V = s["V"]
    HG = 4
    cH = sb("cH", [P, 2, KT, 512], F32R)
    cL = sb("cL", [P, 2, KT, 512], F32R)
    kHL = [sb(f"kHL{i}", [P, HG, TK + 1], F32R) for i in range(2)]
    qb = sb("qb", [P, HG, 4 * TQ], F32)
    qh = [sb(f"qh{i}", [P, HG, 4 * TQ], F32R) for i in range(2)]
    ql = [sb(f"ql{i}", [P, HG, 4 * TQ], F32R) for i in range(2)]
    m8 = [sb(f"m8_{i}", [P, TK], U8) for i in range(2)]
    mneg = [sb(f"mneg{i}", [P, TK], BF16) for i in range(2)]
    near = sb("near", [P, H // 2, NEAR], BF16)
    mc = [sb(f"mc{i}", [P, 2, NKT, 1], F32) for i in range(2)]
    mx = [sb(f"mx{i}", [P, H // 2, NC + 1], F32) for i in range(2)]
    cv = [sb(f"cv{i}", [P, H // 2, 2], BF16) for i in range(2)]
    cm = sb("cm", [P, H // 2], F32)
    cr = sb("cr", [P, H // 2], F32)
    shift = sb("shift", [P, H * TQ], F32)
    PTR = 3
    pT = sb("pT", [P, PTR, H * TQ], F32)
    oT = sb("oT", [P, DM], F32)
    oR = sb("oR", [P, DM], F32)
    oN = oR
    x1 = s["x1"]

    ctx_in = [sem(f"ctx_in{c}") for c in range(NC)]
    mask_in = [sem(f"mask_in{i}") for i in range(2)]
    ctx_hi = sem("ctx_hi")
    ctx_lo = sem("ctx_lo")
    work_full = sem("work_full")
    k_hi = sem("k_hi")
    k_lo = sem("k_lo")
    v_out = sem("v_out")
    maxed = sem("maxed")
    mneg_ready = sem("mneg_ready")
    near_ready = sem("near_ready")
    q_ready = sem("q_ready")
    qb_ready = sem("qb_ready")
    mc_ready = sem("mc_ready")
    c_step = sem("c_step")
    s_full = sem("s_full")
    s_read = sem("s_read")
    added = sem("added")
    pv_done = sem("pv_done")
    o_out = sem("o_out")
    d_full = sem("d_full")
    o_step = sem("o_step")
    y_full = sem("y_full")
    y_out = sem("y_out")
    waited = sem("waited")

    SB = NKT + 1
    HI, LO = s["wH"], s["wL"]
    SLOTS = [((0, 1, 2), (3, 4, 5), (6, 7, 8), (9, 10, 11))] + 3 * [((0, 1, 2, 3), (4, 5, 6, 7), (8, 9, 10, 11))]

    def exps(b, t):
        return SB * b + t + 2

    def adds(b, t):
        return 15 * b + (2 * t + 2 if t < 2 else t + 3)

    def at_least(eng, sm, value):
        if not (isinstance(value, int) and value <= 0):
            eng.wait_ge(sm, value)

    def wait_apart(eng, sm, value):
        eng.wait_ge(sm, value)
        eng.sem_inc(waited, 1)

    def groups(c):
        ts = CHUNKS[c]
        return [ts[0:2], ts[2:]]

    def width(c):
        return CSPAN[c][1] + CSPAN[c][1] % 2

    def pe_use(pe, j, par, c, u):
        n = j * NC + c
        r = c % 2
        k0, w = CSPAN[c][0], width(c)
        bank = psW[:, u % 3, :]
        if u <= 2:
            at_least(pe, maxed, 8 * (n - 1) + 6 + u)
        elif u <= 4:
            pe.wait_ge(k_lo, 4 * n + 2 * (u - 2))
        elif u <= 6:
            pe.wait_ge(v_out, 2 * n + u - 4)
        else:
            pe.wait_ge(maxed, 8 * n + u - 6)
        if u == 0:
            pe.wait_ge(ctx_lo, n + 1)
        if u == 4:
            pe.wait_ge(q_ready, 2 * j + 1)
            pe.wait_ge(v_out, 2 * n + 1)
        if u < 2:
            prods = [(a, b, k) for k in range(KT) for a, b in ((HI, cH), (HI, cL), (LO, cH))]
            for i, (a, b, k) in enumerate(prods):
                mm = pe.matmul(bank[:, 0:w], a[:, 0, k, u * P:u * P + P], b[:, r, k, 0:w],
                               start=(i == 0), stop=(i == len(prods) - 1))
        elif u < 4:
            for i, t in enumerate(groups(c)[u - 2]):
                a0, kw = KTILES[t][0] - k0, KTILES[t][1]
                prods = [(a, b, k) for k in range(KT) for a, b in ((cH, HI), (cH, LO), (cL, HI))]
                for q, (a, b, k) in enumerate(prods):
                    mm = pe.matmul(bank[0:kw, i * DM:i * DM + DM], a[:, r, k, a0:a0 + kw], b[:, 1, k, :],
                                   start=(q == 0), stop=(q == len(prods) - 1))
        else:
            p = u - 4
            mm = pe.matmul(bank[:, 0:w], qh[par][:, p // 2, (p % 2) * P:(p % 2) * P + P], kHL[par][:, p // 2, k0:k0 + w],
                           start=True, stop=True)
        mm.then_inc(work_full, 1)

    def pe_shift(pe, b, par):
        pe.wait_ge(c_step, 5 * (b + 1))
        at_least(pe, s_read, SB * b)
        for p in range(H // 2):
            for i in range(2):
                mm = pe.matmul(psS[:, 1, p * P:p * P + P], cv[par][:, p, i:i + 1].to_broadcast([P, P]), s["identb"][:, :],
                               start=(i == 0), stop=(i == 1), skip_group_check=True)
        mm.then_inc(s_full, 1)

    def buf(t):
        return 0 if t == 0 else (t + 1) % 2

    def pe_scores(pe, b, par, t):
        a, kw = KTILES[t]
        if t == 0:
            pe.wait_ge(q_ready, 2 * b + 2)
            at_least(pe, s_read, SB * b - 1)
        elif t == 2:
            pe.wait_ge(s_read, SB * b + 1)
        else:
            pe.wait_ge(s_read, exps(b, max(t - 2, 0)))
        for g in range(HG):
            o = psS[0:kw, buf(t), g * 256:g * 256 + 256]
            for i, q in enumerate((qh, ql)):
                mm = pe.matmul(o, kHL[par][:, g, a:a + kw], q[par][:, g, :], start=(i == 0), stop=(i == 1),
                               skip_group_check=True)
        mm.then_inc(s_full, 1)

    def pe_values(pe, b, par, t):
        kw = KTILES[t][1]
        pe.wait_ge(s_read, exps(b, t))
        if t == 0:
            at_least(pe, y_out, b)
        for h in range(H):
            r, g = 32 * (h % 4), h // 4
            mm = pe.matmul(psO[r:r + DK + 1, g * TQ:g * TQ + TQ], V[par][0:kw, t, h, :],
                           pT[0:kw, t % PTR, h * TQ:h * TQ + TQ], start=(t == 0 and g == 0), stop=(t == NKT - 1),
                           skip_group_check=True)
        mm.then_inc(pv_done, 1)

    def pe_denominators(pe, b):
        pe.wait_ge(o_out, b + 1)
        pe.matmul(psO[:, 256:512], s["den_rows"][:, :], oT[:, :], start=True, stop=True,
                  skip_group_check=True).then_inc(d_full, 1)

    def pe_project(pe, b, par):
        pe.wait_ge(o_step, 2 * b + 2)
        for g in range(4):
            mm = pe.matmul(psO[tok_rows(par), 256:512], oN[:, g * TQ:g * TQ + TQ], s["woP"][:, g, :],
                           start=(g == 0), stop=(g == 3), skip_group_check=True)
        mm.then_inc(y_full, 1)

    def pe_step(pe, j, par, prep, main, fin, ahead):
        for c in range(NC):
            for i, t in enumerate(CHUNKS[c]):
                if t == 1 and fin:
                    pe_project(pe, j - 2, par)
                if main:
                    pe_scores(pe, j - 1, 1 - par, t)
                    if t == 0:
                        pe_shift(pe, j - 1, 1 - par)
                    else:
                        pe_values(pe, j - 1, 1 - par, t - 1)
                if prep:
                    for u in SLOTS[c][i]:
                        pe_use(pe, j, par, c, u)
                if t == 0 and fin:
                    pe_denominators(pe, j - 2)
        if main:
            pe_values(pe, j - 1, 1 - par, NKT - 1)

    def act_split(act, j, c):
        n = j * NC + c
        w = width(c)
        act.wait_ge(ctx_in[c], 16 * (j + 1))
        at_least(act, work_full, 12 * (n - 2) + 4)
        act.activation(cH[:, c % 2, :, 0:w], ctx[:, c % 2, :, 0:w], ACT.Copy).then_inc(ctx_hi, 1)

    def act_use(act, j, par, c, u):
        n = j * NC + c
        k0, w = CSPAN[c][0], width(c)
        if u < 4:
            act.wait_ge(work_full, 12 * n + u + 1)
        if u < 2:
            for g in range(2):
                rows = slice(64 * g, 64 * g + 64)
                act.activation(kHL[par][rows, 2 * u + g, k0:k0 + w], psW[rows, u, 0:w], ACT.Copy).then_inc(k_hi, 1)
        elif u < 4:
            ts = groups(c)[u - 2]
            kw = KTILES[ts[-1]][1]
            act.activation(V[par][0:kw, ts[0]:ts[-1] + 1, :, 0:DK],
                           psW[0:kw, u % 3, 0:len(ts) * DM].rearrange("p (t h e) -> p t h e", t=len(ts), e=DK),
                           ACT.Copy).then_inc(v_out, 1)

    def act_exp(act, b, par, t):
        kw = KTILES[t][1]
        if t == 0:
            act.wait_ge(mc_ready, b + 1)
        if t >= PTR:
            act.wait_ge(pv_done, NKT * b + t - PTR + 1)
        else:
            at_least(act, pv_done, NKT * (b - 1) + [13, 11, 12][t])
        act.wait_ge(added, adds(b, t))
        act.activation(pT[0:kw, t % PTR, :], psS[0:kw, buf(t), :], ACT.Exp,
                       bias=mc[par][0:kw, 1, t, :], scale=mc[par][0:kw, 0, t, :]).then_inc(s_read, 1)

    def act_step(act, j, par, prep, main, fin, ahead):
        b = j - 1
        if isinstance(j, int) and j == 0:
            act_split(act, 0, 0)
        for c in range(NC):
            for i, t in enumerate(CHUNKS[c]):
                if main and t == 0:
                    act.wait_ge(s_full, SB * b + 2)
                    act.activation(shift[:, :], psS[:, 1, :], ACT.Copy).then_inc(s_read, 1)
                if prep and t == 0 and not (isinstance(j, int) and j < 2):
                    act.wait_ge(pv_done, NKT * (j - 1))
                if prep and t == 0:
                    act_use(act, j, par, c, 0)
                if main:
                    act_exp(act, b, 1 - par, t)
                if prep:
                    for u in SLOTS[c][i]:
                        if not (t == 0 and u == 0):
                            act_use(act, j, par, c, u)
                    if i == 1 and (c < NC - 1 or ahead):
                        act_split(act, j if c < NC - 1 else j + 1, (c + 1) % NC)

    def dve_use(v, j, par, c, u):
        n = j * NC + c
        k0, w = CSPAN[c]
        if u < 2:
            w = width(c)
            for g in range(2):
                rows, other = slice(64 * g, 64 * g + 64), slice(64 - 64 * g, 128 - 64 * g)
                v.wait_ge(k_hi, 4 * n + 2 * u + g + 1)
                v.tensor_tensor(kHL[par][other, 2 * u + g, k0:k0 + w], psW[rows, u, 0:w],
                                kHL[par][rows, 2 * u + g, k0:k0 + w].bitcast(F32), ALU.subtract).then_inc(k_lo, 1)
        elif u >= 4:
            p = u - 4
            bank = psW[:, u % 3, :]
            wait_apart(v, work_full, 12 * n + u + 1)
            if c == 0:
                v.tensor_tensor_reduce(bank[:, 0:NEAR], bank[:, 0:NEAR], near[:, p, :], 1.0, -3e38,
                                       ALU.add, ALU.max, mx[par][:, p, 0:1])
                v.tensor_tensor_reduce(bank[:, NEAR:w], bank[:, NEAR:w], mneg[par][:, NEAR:w], 1.0, -3e38,
                                       ALU.add, ALU.max, mx[par][:, p, 1:2]).then_inc(maxed, 1)
            else:
                v.tensor_tensor_reduce(bank[:, 0:w], bank[:, 0:w], mneg[par][:, k0:k0 + w], 1.0, -3e38,
                                       ALU.add, ALU.max, mx[par][:, p, c + 1:c + 2]).then_inc(maxed, 1)

    def dve_add(v, b, t):
        kw = KTILES[t][1]
        if t == 0:
            v.wait_ge(s_read, SB * b + 1)
        v.wait_ge(s_full, SB * b + (1 if t == 0 else t + 2))
        o = psS[0:kw, buf(t), :]
        v.tensor_tensor(o, o, shift[0:kw, :], ALU.add).then_inc(added, 1)
        if t < 2:
            v.wait_ge(added, 15 * b + 2 * t + 1)
            v.tensor_tensor(o, o, s["dT"][0:kw, t, :], ALU.add).then_inc(added, 1)

    def dve_step(v, j, par, prep, main, fin, ahead, tile):
        f, b = j - 2, j - 1
        if fin:
            v.wait_ge(pv_done, NKT * (f + 1))
            v.tensor_copy(oT[:, :], psO[:, 0:DM]).then_inc(o_out, 1)
        for c in range(NC):
            for i, t in enumerate(CHUNKS[c]):
                if t == 1 and fin:
                    v.wait_ge(d_full, f + 1)
                    v.reciprocal(oR[:, :], psO[:, 256:512]).then_inc(o_step, 1)
                    v.wait_ge(o_step, 2 * f + 1)
                    v.tensor_tensor(oN[:, :], oT[:, :], oR[:, :], ALU.mult).then_inc(o_step, 1)
                    v.wait_ge(y_full, f + 1)
                    v.tensor_tensor(x1[tok_rows(par), tile, :], psO[tok_rows(par), 256:512],
                                    x1[tok_rows(par), tile, :], ALU.add).then_inc(y_out, 1)
                if main:
                    dve_add(v, b, t)
                if prep:
                    if t == 0:
                        v.wait_ge(near_ready, j + 1)
                    for u in SLOTS[c][i]:
                        dve_use(v, j, par, c, u)
        if prep:
            k = 5 * j
            v.wait_ge(maxed, 32 * (j + 1))
            v.tensor_reduce(cm[:, :], mx[par][:, :, :], AX.X, ALU.max).then_inc(c_step, 1)
            v.wait_ge(c_step, k + 1)
            v.tensor_scalar(cm[:, :], cm[:, :], -1.0, None, ALU.mult).then_inc(c_step, 1)
            v.wait_ge(c_step, k + 2)
            v.tensor_copy(cv[par][:, :, 0], cm[:, :]).then_inc(c_step, 1)
            v.wait_ge(c_step, k + 3)
            v.tensor_tensor(cr[:, :], cm[:, :], cv[par][:, :, 0], ALU.subtract).then_inc(c_step, 1)
            v.wait_ge(c_step, k + 4)
            v.tensor_copy(cv[par][:, :, 1], cr[:, :]).then_inc(c_step, 1)

    def pool_split(pool, j, c):
        n = j * NC + c
        w = width(c)
        at_least(pool, work_full, 12 * (n - 2) + 4)
        pool.wait_ge(ctx_hi, n + 1)
        pool.tensor_tensor(cL[:, c % 2, :, 0:w], ctx[:, c % 2, :, 0:w], cH[:, c % 2, :, 0:w].bitcast(F32), ALU.subtract)\
            .then_inc(ctx_lo, 1)

    def pool_step(pool, j, par, ahead, half):
        late = not (isinstance(j, int) and j < 2)
        if isinstance(j, int) and j == 0:
            pool_split(pool, 0, 0)
        at_least(pool, maxed, 32 * (j - 1) + 8 if not isinstance(j, int) or j else 0)
        wait_apart(pool, mask_in[par], 16 * (half + 1))
        pool.tensor_scalar(mneg[par][:, :], m8[par][:, :], -1.0, NEG, ALU.add, ALU.mult).then_inc(mneg_ready, 1)
        pool.wait_ge(mneg_ready, j + 1)
        pool.tensor_tensor(near[:, :, :], s["dN"][:, :, :],
                           mneg[par][:, 0:NEAR].unsqueeze(1).to_broadcast([P, H // 2, NEAR]), ALU.add).then_inc(near_ready, 1)
        if late:
            pool.wait_ge(s_full, SB * (j - 1))
        for g in range(HG):
            op = pool.tensor_tensor(qb[:, g, :].rearrange("p (h q) -> p h q", h=4),
                                    s["qD"][:, g, bass.ds(j * TQ, TQ)].unsqueeze(1).to_broadcast([P, 4, TQ]),
                                    s["head_rows"][:, :].unsqueeze(2).to_broadcast([P, 4, TQ]), ALU.mult)
        op.then_inc(qb_ready, 1)
        wait_apart(pool, qb_ready, j + 1)
        pool.tensor_copy(qh[par][:, :, :], qb[:, :, :]).then_inc(q_ready, 1)
        pool.wait_ge(q_ready, 2 * j + 1)
        pool.tensor_tensor(ql[par][:, :, :], qb[:, :, :], qh[par][:, :, :].bitcast(F32), ALU.subtract).then_inc(q_ready, 1)
        if late:
            wait_apart(pool, s_read, SB * (j - 1))
        pool.tensor_copy(mc[par][:, :, :, :], s["mcols"][:, :, :, bass.ds(j, 1)]).then_inc(mc_ready, 1)
        for c in range(NC):
            if c < NC - 1 or ahead:
                pool_split(pool, j if c < NC - 1 else j + 1, (c + 1) % NC)

    ctx_view = d["ctxT"].rearrange("b (k p) t -> b p k t", p=P)

    def sp_step(sp, j, par):
        late = not (isinstance(j, int) and j < 2)
        if late:
            sp.wait_ge(mneg_ready, j - 1)
        for c in range(NC):
            k0, w = CSPAN[c]
            at_least(sp, ctx_lo, j * NC + c - 1)
            sp.dma_start(ctx[:, c % 2, :, 0:w], ctx_view[bass.ds(j, 1), :, :, k0:k0 + w].rearrange("b p k t -> (b p) k t"))\
              .then_inc(ctx_in[c], 16)
            if c == 0:
                sp.dma_start(m8[par][:, :], d["mask"][bass.ds(j, 1), :].to_broadcast([P, TK])).then_inc(mask_in[par], 16)

    def run(eng, step):
        step(eng, 0, 0, 0)
        step(eng, 1, 1, 0)
        with eng.Fori(0, B // 2 - 2) as i:
            step(eng, 2 * i + 2, 0, i + 1)
            step(eng, 2 * i + 3, 1, i + 1)
        for j in range(B - 2, B + 2):
            step(eng, j, j % 2, j // 2)

    def parts(j):
        if not isinstance(j, int):
            return True, True, True, True
        return j < B, 1 <= j <= B, j >= 2, j < B - 1

    with nc.Block() as block:
        @block.sync
        def _(sp):
            run(sp, lambda e, j, par, half: parts(j)[0] and sp_step(e, j, par))

        @block.gpsimd
        def _(pool):
            run(pool, lambda e, j, par, half: parts(j)[0] and pool_step(e, j, par, parts(j)[3], half))

        @block.scalar
        def _(act):
            run(act, lambda e, j, par, half: act_step(e, j, par, *parts(j)))

        @block.vector
        def _(v):
            run(v, lambda e, j, par, half: dve_step(e, j, par, *parts(j), half - 1))

        @block.tensor
        def _(pe):
            run(pe, lambda e, j, par, half: pe_step(e, j, par, *parts(j)))


def norm_stats(nc, x, mv, rstd, sb, sem, tag):
    stats = sb(f"{tag}_stats", [P, NT, 6], F32)
    step = sem(f"{tag}_norm_step")
    root = sem(f"{tag}_norm_root")
    with nc.Block() as block:
        @block.vector
        def _(v):
            layer_norm_steps(v, x, stats, mv, rstd, None, step)
            v.wait_ge(root, 1)
            v.reciprocal(rstd[:, :], rstd[:, :]).then_inc(step, 1)

        @block.scalar
        def _(act):
            act.wait_ge(step, 2 * NT + 1)
            act.activation(rstd[:, :], rstd[:, :], ACT.Sqrt).then_inc(root, 1)


def self_attention(nc, d, s, sb, ps, sem):
    x1, x2, ident = s["x1"], s["x2"], s["ident"]
    psX = ps("a_psX", [P, 512])
    psQ = ps("a_psQ", [P, 512])
    psK = ps("a_psK", [P, 512])
    psV = ps("a_psV", [P, 512])
    psA = ps("a_psA", [P, 1024])
    psT = ps("a_psT", [P, 2, 512])
    mv = sb("a_mv", [P, NT, 2], F32)
    rstd = sb("a_rstd", [P, NT], F32)
    norm_stats(nc, x1, mv, rstd, sb, sem, "a")
    xn = sb("a_xn", [P, DM], F32)
    xs = sb("a_xs", [P, KT, P], F32)
    qs = sb("a_qs", [P, KT, P], F32)
    kbd = sb("a_kbd", [P, 2, KT, 512], F32)
    V = sb("a_V", [P, H, DK + 1], F32)
    E = sb("a_E", [P, H, TQ], F32)
    mx = sb("a_mx", [P, H], F32)
    pf = sb("a_pf", [P, H, P], F32)
    pT = kbd.rearrange("p b m c -> p (b m c)").rearrange("p (h q) -> p h q", h=H)
    oR = sb("a_oR", [P, 512], F32)
    flat = E.rearrange("p h k -> p (h k)")
    oT, oN = flat[:, 0:512], flat[:, 512:1024]
    w = s["wattn"]

    ready = sem("a_ready")
    xn_ready = sem("a_xn")
    x_turned = sem("a_x_turned")
    xs_ready = sem("a_xs")
    q_full, k_full, v_full = sem("a_q_full"), sem("a_k_full"), sem("a_v_full")
    qv_ready = sem("a_qv")
    kbd_ready = sem("a_kbd_ready")
    s_full = sem("a_s_full")
    e_step = sem("a_e_step")
    p_ready = sem("a_p")
    t_full = sem("a_t_full")
    t_out_act = sem("a_t_out_act")
    t_out_dve = sem("a_t_out_dve")
    o_full = sem("a_o_full")
    o_step = sem("a_o_step")
    d_full = sem("a_d_full")
    y_full = sem("a_y_full")
    y_out = sem("a_y_out")

    with nc.Block() as block:
        @block.gpsimd
        def _(pool):
            pool.memset(pf[:, :, :], 0.0).then_inc(ready, 1)
            pool.memset(V[:, :, :], 1.0).then_inc(ready, 1)

        @block.vector
        def _(v):
            v.memset(psV[:, :], 0.0).then_inc(ready, 1)
            v.wait_ge(s["attn_loads"], s["attn_loads_total"])
            with v.Fori(0, NT) as n:
                xn_n = x1[:, bass.ds(n, 1), :].rearrange("p a f -> p (a f)")
                v.tensor_scalar(xn[:, :], xn_n, mv[:, bass.ds(n, 1), 0:1].rearrange("p a b -> p (a b)"),
                                rstd[:, bass.ds(n, 1)], ALU.subtract, ALU.mult).then_inc(xn_ready, 1)
                v.wait_ge(k_full, n + 1)
                for b in range(2):
                    for m in range(KT):
                        v.tensor_tensor(kbd[:, b, m, :].rearrange("p (h k) -> p h k", h=HT),
                                        psK[:, m * P + b * TQ:m * P + b * TQ + TQ].unsqueeze(1).to_broadcast([P, HT, TQ]),
                                        s["head_rows2"][:, :].unsqueeze(2).to_broadcast([P, HT, TQ]), ALU.mult)\
                         .then_inc(kbd_ready, 1)
                v.wait_ge(s_full, n + 1)
                v.scalar_tensor_tensor(out=E.rearrange("p h k -> p (h k)"), in0=psA[:, :], scalar=DK ** -0.5,
                                       in1=s["alibi"][:, :], op0=ALU.mult, op1=ALU.add).then_inc(e_step, 1)
                v.wait_ge(e_step, 3 * n + 1)
                v.tensor_reduce(mx[:, :], E[:, :, :], AX.X, ALU.max).then_inc(e_step, 1)
                v.wait_ge(e_step, 3 * n + 2)
                v.tensor_tensor(E[:, :, :], E[:, :, :], mx[:, :].unsqueeze(2).to_broadcast([P, H, TQ]), ALU.subtract)\
                 .then_inc(e_step, 1)
                for i in (1, 3):
                    v.wait_ge(t_full, 4 * n + i + 1)
                    v.tensor_copy(pT[:, 4 * i:4 * i + 4, :].rearrange("p h q -> p (h q)"), psT[:, i % 2, :]).then_inc(t_out_dve, 1)
                v.wait_ge(o_full, n + 1)
                v.tensor_copy(oT[:, :], psV[:, :]).then_inc(o_step, 1)
                v.wait_ge(d_full, n + 1)
                v.reciprocal(oR[:, :], psX[:, :]).then_inc(o_step, 1)
                v.wait_ge(o_step, 3 * n + 2)
                v.tensor_tensor(oN[:, :], oT[:, :], oR[:, :], ALU.mult).then_inc(o_step, 1)
                v.wait_ge(y_full, n + 1)
                v.tensor_tensor(x2[:, bass.ds(n, 1), :].rearrange("p a f -> p (a f)"), psQ[:, 0:DM], xn_n, ALU.add)\
                 .then_inc(y_out, 1)

        @block.scalar
        def _(act):
            act.wait_ge(ready, 3)
            with act.Fori(0, NT) as n:
                act.wait_ge(x_turned, n + 1)
                act.activation(xs.rearrange("p k t -> p (k t)"), psX[:, 0:2 * P], ACT.Copy).then_inc(xs_ready, 1)
                act.wait_ge(q_full, n + 1)
                act.activation(qs.rearrange("p k t -> p (k t)"), psQ[:, 0:2 * P], ACT.Copy).then_inc(qv_ready, 1)
                act.wait_ge(v_full, n + 1)
                act.activation(V[:, :, 0:DK], psT[:, 0, 0:DM].rearrange("p (h e) -> p h e", e=DK), ACT.Copy).then_inc(qv_ready, 1)
                act.wait_ge(e_step, 3 * n + 3)
                for b in range(2):
                    act.activation(pf[tok_rows(b), :, b * TQ:b * TQ + TQ], E[tok_rows(b), :, :], ACT.Exp).then_inc(p_ready, 1)
                for i in (0, 2):
                    act.wait_ge(t_full, 4 * n + i + 1)
                    act.activation(pT[:, 4 * i:4 * i + 4, :].rearrange("p h q -> p (h q)"), psT[:, i % 2, :], ACT.Copy)\
                       .then_inc(t_out_act, 1)

        @block.tensor
        def _(pe):
            pe.wait_ge(ready, 3)
            pe.wait_ge(s["attn_loads"], s["attn_loads_total"])
            with pe.Fori(0, NT) as n:
                pe.wait_ge(xn_ready, n + 1)
                for k in range(KT):
                    mm = pe.transpose(psX[:, k * P:k * P + P], xn[:, k * P:k * P + P], ident[:, :])
                mm.then_inc(x_turned, 1)
                pe.wait_ge(xs_ready, n + 1)
                for ps_out, f0, full in ((psQ, 0, q_full), (psK, DM, k_full)):
                    for m in range(KT):
                        for k in range(KT):
                            mm = pe.matmul(ps_out[:, m * P:m * P + P], w[:, k, f0 + m * P:f0 + m * P + P], xs[:, k, :],
                                           start=(k == 0), stop=(k == KT - 1), skip_group_check=True)
                    mm.then_inc(full, 1)
                for k in range(KT):
                    mm = pe.matmul(psT[:, 0, 0:DM], xs[:, k, :], w[:, k, 2 * DM:3 * DM], start=(k == 0), stop=(k == KT - 1))
                mm.then_inc(v_full, 1)
                pe.wait_ge(qv_ready, 2 * n + 2)
                pe.wait_ge(kbd_ready, 4 * n + 4)
                for b in range(2):
                    for m in range(KT):
                        mm = pe.matmul(psA[tok_rows(b), m * 512:m * 512 + 512], qs[:, m, b * TQ:b * TQ + TQ],
                                       kbd[:, b, m, :], start=True, stop=True)
                mm.then_inc(s_full, 1)
                pe.wait_ge(p_ready, 2 * n + 2)
                for i in range(4):
                    if i == 2:
                        pe.wait_ge(t_out_act, 2 * n + 1)
                    if i == 3:
                        pe.wait_ge(t_out_dve, 2 * n + 1)
                    for h in range(4 * i, 4 * i + 4):
                        mm = pe.transpose(psT[:, i % 2, (h % 4) * P:(h % 4) * P + P], pf[:, h, :], ident[:, :])
                    mm.then_inc(t_full, 1)
                pe.wait_ge(t_out_act, 2 * n + 2)
                pe.wait_ge(t_out_dve, 2 * n + 2)
                for h in range(H):
                    r, g = 32 * (h % 4), h // 4
                    mm = pe.matmul(psV[r:r + DK + 1, g * P:g * P + P], V[:, h, :], pT[:, h, :], start=(g == 0), stop=True,
                                   skip_group_check=True)
                mm.then_inc(o_full, 1)
                pe.wait_ge(o_step, 3 * n + 1)
                pe.matmul(psX[:, :], s["den_rows2"][:, :], oT[:, :], start=True, stop=True).then_inc(d_full, 1)
                pe.wait_ge(o_step, 3 * n + 3)
                for g in range(4):
                    mm = pe.matmul(psQ[:, 0:DM], oN[:, g * P:g * P + P], s["wprojP"][:, g, :], start=(g == 0), stop=(g == 3))
                mm.then_inc(y_full, 1)


def load_experts(sp, d, s, h, par):
    sp.dma_start(s["vraw"][par][:, :, :], d["vw"].rearrange("(k p) h f -> p k h f", p=P)[:, :, bass.ds(h, 1), :]
                 .rearrange("p k a f -> p (k a) f")).then_inc(s["v_in"][par], 16)
    sp.dma_start(s["oraw"][par][:, :], d["ow"][bass.ds(h, 1), :, :].rearrange("a p f -> (a p) f")).then_inc(s["o_in"][par], 16)


def switch_head(nc, d, s, sb, ps, sem):
    x, ident = s["x2"], s["ident"]
    psV = ps("f_psV", [P, 4, 512])
    psU = ps("f_psU", [P, 2, 512])
    psC = ps("f_psC", [P, 2, 512])
    bankU = [psU[:, 0, :], psU[:, 1, :], psC[:, 0, :]]
    bankC = psC[:, 1, 0:P]
    mv = sb("f_mv", [P, NT, 2], F32)
    rstd = sb("f_rstd", [P, NT], F32)
    norm_stats(nc, x, mv, rstd, sb, sem, "f")
    pT = sb("f_pT", [P, FH, NT, P], F32)
    xH = sb("f_xH", [P, KT, TOK], F32R)
    xL = sb("f_xL", [P, KT, TOK], F32R)
    NG = 2 * NT * 2
    gate = sb("f_gate", [P, FH, NT, 2, FE], F32)
    qkw, sel = s["qkw"], s["sel"]
    SCALE = 1.0 / math.sqrt(FP)

    vH, vL = [[sb(f"f_v{n}0", [P, KT, FE * FP], F32R)] for n in "HL"]
    oH, oL = [[sb(f"f_o{n}0", [P, FE * DM], F32R)] for n in "HL"]
    whi_v, whi_o = sem("f_whi_v"), sem("f_whi_o")
    wlo_v, wlo_o = sem("f_wlo_v"), sem("f_wlo_o")

    def piece(kind, par, q):
        if kind == "v":
            k, c = q // 2, slice(512 * (q % 2), 512 * (q % 2) + 512)
            return vH[par][:, k, c], vL[par][:, k, c], s["vraw"][par][:, k, c]
        c = slice(512 * q, 512 * q + 512)
        return oH[par][:, c], oL[par][:, c], s["oraw"][par][:, c]

    def act_cut(act, h, par, kind, q):
        if q == 0:
            act.wait_ge(s[f"{kind}_in"][par], 16 * (h // 2 + 1) if isinstance(h, int) else 8 * (h - par) + 16)
            if not (isinstance(h, int) and h < 2):
                act.wait_ge({"v": v_full, "o": u_full}[kind], {"v": 16, "o": 32}[kind] * (h - 1))
        hi, lo, raw = piece(kind, par, q)
        act.activation(hi, raw, ACT.Copy).then_inc({"v": whi_v, "o": whi_o}[kind], 1)

    def pool_cut(pool, h, par, kind, q):
        pool.wait_ge({"v": whi_v, "o": whi_o}[kind], 4 * h + q + 1)
        hi, lo, raw = piece(kind, par, q)
        pool.tensor_tensor(lo, raw, hi.bitcast(F32), ALU.subtract).then_inc({"v": wlo_v, "o": wlo_o}[kind], 1)

    xn_ready = sem("f_xn")
    x_turned = sem("f_x_turned")
    xs_ready = sem("f_xs_ready")
    xh_ready = sem("f_xh")
    xl_ready = sem("f_xl")
    l_full = sem("f_l_full")
    l_exp = sem("f_l_exp")
    zeroed = sem("f_zeroed")
    qkw_hi = sem("f_qkw_hi")
    qkw_lo = sem("f_qkw_lo")
    qk_full = sem("f_qk_full")
    qk_out = sem("f_qk_out")
    s_full = sem("f_s_full")
    e_step = sem("f_e_step")
    p_ready = sem("f_p")
    den_read = sem("f_den_read")
    g_step = sem("f_g_step")
    t_full = sem("f_t_full")
    t_out = sem("f_t_out")
    GS = 22

    with ExitStack() as first:
        def sbf(name, shape, dt=F32):
            return first.enter_context(nc.sbuf_tensor(name, shape, dt))
        xn = sbf("f_xn_rows", [P, NT, DM])
        xs = sbf("f_xs", [P, KT, TOK])
        wH = [sbf(f"f_qkH{i}", [P, KT, 2 * FP], F32R) for i in range(2)]
        wL = [sbf(f"f_qkL{i}", [P, KT, 2 * FP], F32R) for i in range(2)]
        qkT = sbf("f_qkT", [P, 2, TOK])
        E = sbf("f_E", [P, NT, TQ])
        pf = [sbf(f"f_pf{i}", [P, NT, P]) for i in range(2)]
        mx = sbf("f_mx", [P, NT])
        rden = sbf("f_rden", [P, 2 * NT])
        lex = sbf("f_lex", [P, FH, NT, 2 * FE])
        ex, pr, eq, one1, one2 = [sbf(f"f_g{n}", [P, NG, FE]) for n in ("ex", "pr", "eq", "one1", "one2")]
        top1, top2, pick, tot = [sbf(f"f_g{n}", [P, NG]) for n in ("top1", "top2", "pick", "tot")]

        def bc(a):
            return a[:, :].unsqueeze(2).to_broadcast([P, NG, FE])

        def flat(a):
            return a.rearrange("p g e -> p (g e)")

        with nc.Block() as block:
            @block.gpsimd
            def _(pool):
                for i in range(2):
                    pool.memset(pf[i][:, :, :], 0.0).then_inc(zeroed, 1)

                def weights(h, par):
                    pool.wait_ge(qkw_hi, h + 1)
                    pool.tensor_tensor(wL[par][:, :, :], qkw[:, :, bass.ds(h, 1), :].rearrange("p k a f -> p (k a) f"),
                                       wH[par][:, :, :].bitcast(F32), ALU.subtract).then_inc(qkw_lo, 1)
                for i in range(4):
                    k, c = i // 2, slice(512 * (i % 2), 512 * (i % 2) + 512)
                    pool.wait_ge(xh_ready, i + 1)
                    pool.tensor_tensor(xL[:, k, c], xs[:, k, c], xH[:, k, c].bitcast(F32), ALU.subtract).then_inc(xl_ready, 1)
                weights(0, 0)
                weights(1, 1)
                for kind in "vo":
                    for q in range(4):
                        pool_cut(pool, 0, 0, kind, q)
                with pool.Fori(0, FH // 2 - 1) as i:
                    weights(2 * i + 2, 0)
                    weights(2 * i + 3, 1)

            @block.vector
            def _(v):
                for n in range(NT):
                    v.tensor_scalar(xn[:, n, :], x[:, n, :], mv[:, n, 0:1], rstd[:, n:n + 1], ALU.subtract, ALU.mult)\
                     .then_inc(xn_ready, 1)
                v.wait_ge(s["ffn_loads"], s["ffn_loads_total"])
                v.wait_ge(l_exp, NT)

                def softmax(h, par):
                    v.wait_ge(s_full, h + 1)
                    sc = psC[:, par, :].rearrange("p (n k) -> p n k", n=NT)
                    v.tensor_reduce(mx[:, :], sc, AX.X, ALU.max).then_inc(e_step, 1)
                    v.wait_ge(e_step, 2 * h + 1)
                    v.tensor_tensor(E[:, :, :], sc, mx[:, :].unsqueeze(2).to_broadcast([P, NT, TQ]), ALU.subtract)\
                     .then_inc(e_step, 1)

                def denominators(h, par):
                    v.wait_ge(p_ready, 2 * h + 2)
                    v.tensor_reduce(rden[:, NT * par:NT * par + NT], pf[par][:, :, :], AX.X, ALU.add).then_inc(den_read, 1)

                def gates(i, part):
                    count = [0 if part == 0 else 9]

                    def step(op):
                        count[0] += 1
                        op.then_inc(g_step, 1)
                        v.wait_ge(g_step, GS * i + count[0])
                    rank = s["rank"][:, :].unsqueeze(1).to_broadcast([P, NG, FE])
                    if part == 0:
                        step(v.tensor_scalar(flat(ex), lex[:, bass.ds(2 * i, 2), :, :].rearrange("p a n e -> p (a n e)"),
                                             1.0, None, ALU.add))
                        step(v.reciprocal(pr[:, :, :], ex[:, :, :]))
                        step(v.tensor_reduce(top1[:, :], pr[:, :, :], AX.X, ALU.max))
                        step(v.tensor_tensor(eq[:, :, :], pr[:, :, :], bc(top1), ALU.is_equal))
                        step(v.tensor_tensor(eq[:, :, :], eq[:, :, :], rank, ALU.mult))
                        step(v.tensor_reduce(pick[:, :], eq[:, :, :], AX.X, ALU.max))
                        step(v.tensor_tensor(one1[:, :, :], bc(pick), rank, ALU.is_equal))
                        step(v.scalar_tensor_tensor(out=flat(ex), in0=flat(one1), scalar=-2.0, in1=flat(pr),
                                                    op0=ALU.mult, op1=ALU.add))
                        step(v.tensor_reduce(top2[:, :], ex[:, :, :], AX.X, ALU.max))
                        return
                    step(v.tensor_tensor(eq[:, :, :], ex[:, :, :], bc(top2), ALU.is_equal))
                    step(v.tensor_tensor(eq[:, :, :], eq[:, :, :], rank, ALU.mult))
                    step(v.tensor_reduce(pick[:, :], eq[:, :, :], AX.X, ALU.max))
                    step(v.tensor_tensor(one2[:, :, :], bc(pick), rank, ALU.is_equal))
                    step(v.tensor_tensor(tot[:, :], top1[:, :], top2[:, :], ALU.add))
                    step(v.tensor_scalar(tot[:, :], tot[:, :], 1e-9, None, ALU.max))
                    step(v.reciprocal(tot[:, :], tot[:, :]))
                    step(v.tensor_scalar(tot[:, :], tot[:, :], s["route"][:, 0:1], None, ALU.mult))
                    step(v.tensor_tensor(eq[:, :, :], one1[:, :, :], one2[:, :, :], ALU.add))
                    step(v.tensor_tensor(eq[:, :, :], eq[:, :, :], pr[:, :, :], ALU.mult))
                    denominators(2 * i + 1, 1)
                    v.wait_ge(den_read, 2 * i + 2)
                    step(v.reciprocal(rden[:, :], rden[:, :]))
                    o_tot = tot.rearrange("p (n w) -> p n w", w=2)[:, :, 1]
                    step(v.tensor_tensor(o_tot, o_tot, rden[:, :], ALU.mult))
                    step(v.tensor_tensor(gate[:, bass.ds(2 * i, 2), :, :, :].rearrange("p a n w e -> p (a n w) e"), eq[:, :, :],
                                         bc(tot), ALU.mult))
                    assert count[0] == GS
                with v.Fori(0, FH // 2) as i:
                    softmax(2 * i, 0)
                    gates(i, 0)
                    denominators(2 * i, 0)
                    softmax(2 * i + 1, 1)
                    gates(i, 1)

            @block.scalar
            def _(act):
                act.wait_ge(s["ffn_loads"], s["ffn_loads_total"])

                def weights(h, par):
                    if not (isinstance(h, int) and h < 2):
                        act.wait_ge(qk_full, 4 * (h - 1))
                    act.activation(wH[par][:, :, :], qkw[:, :, bass.ds(h, 1), :].rearrange("p k a f -> p (k a) f"), ACT.Copy)\
                       .then_inc(qkw_hi, 1)
                weights(0, 0)
                for i in range(4):
                    k, c = i // 2, slice(512 * (i % 2), 512 * (i % 2) + 512)
                    act.wait_ge(x_turned, i + 1)
                    act.activation(xs[:, k, c], psV[:, i, :], ACT.Copy).then_inc(xs_ready, 1)
                    act.wait_ge(xs_ready, i + 1)
                    act.activation(xH[:, k, c], xs[:, k, c], ACT.Copy).then_inc(xh_ready, 1)
                for n in range(NT):
                    if n % 4 == 0:
                        act.wait_ge(l_full, n // 4 + 1)
                    act.activation(lex[:, :, n, :], psC[:, n // 4, (n % 4) * P:(n % 4) * P + P]
                                   .rearrange("p (h e) -> p h e", h=FH), ACT.Exp, scale=-1.0).then_inc(l_exp, 1)
                act.wait_ge(zeroed, 2)

                def heads(h, par, begun, more):
                    for i in range(4):
                        if i == 2 and begun:
                            act.wait_ge(e_step, 2 * h)
                            if not (isinstance(h, int) and h < 3):
                                act.wait_ge(t_full, 2 * (h - 2))
                                act.wait_ge(den_read, h - 2)
                            for b in range(2):
                                act.activation(pf[1 - par][tok_rows(b), :, b * TQ:b * TQ + TQ], E[tok_rows(b), :, :], ACT.Exp,
                                               scale=SCALE).then_inc(p_ready, 1)
                        if more is None:
                            continue
                        act.wait_ge(qk_full, 4 * h + i + 1)
                        if i == 0 and begun:
                            act.wait_ge(s_full, h)
                        act.activation(qkT[:, i // 2, 512 * (i % 2):512 * (i % 2) + 512], psV[:, i, :], ACT.Copy).then_inc(qk_out, 1)
                    if begun:
                        for i in range(2):
                            act.wait_ge(t_full, 2 * (h - 1) + i + 1)
                            act.activation(pT[:, bass.ds(h - 1, 1), 4 * i:4 * i + 4, :].rearrange("p a n q -> p (a n q)"),
                                           psU[:, i, :], ACT.Copy).then_inc(t_out, 1)
                    if more:
                        weights(h + 2 - 1, 1 - par)
                heads(0, 0, False, True)
                for q in range(4):
                    act_cut(act, 0, 0, "v", q)
                heads(1, 1, True, True)
                for q in range(4):
                    act_cut(act, 0, 0, "o", q)
                with act.Fori(0, FH // 2 - 2) as i:
                    heads(2 * i + 2, 0, True, True)
                    heads(2 * i + 3, 1, True, True)
                heads(FH - 2, 0, True, True)
                heads(FH - 1, 1, True, False)
                heads(FH, 0, True, None)

            @block.tensor
            def _(pe):
                for i in range(4):
                    for n in range(4):
                        t = 4 * (i % 2) + n
                        if i < 2:
                            pe.wait_ge(xn_ready, t + 1)
                        mm = pe.transpose(psV[:, i, n * P:n * P + P], xn[:, t, (i // 2) * P:(i // 2) * P + P], ident[:, :])
                    mm.then_inc(x_turned, 1)
                pe.wait_ge(s["ffn_loads"], s["ffn_loads_total"])
                pe.wait_ge(xs_ready, 4)
                for n in range(NT):
                    for k in range(KT):
                        mm = pe.matmul(psC[:, n // 4, (n % 4) * P:(n % 4) * P + P], xs[:, k, n * P:n * P + P], sel[:, k, :],
                                       start=(k == 0), stop=(k == KT - 1), skip_group_check=True)
                    if n % 4 == 3:
                        mm.then_inc(l_full, 1)
                pe.wait_ge(xl_ready, 4)

                def queries_keys(h, par):
                    pe.wait_ge(qkw_lo, h + 1)
                    for i in range(4):
                        if not (isinstance(h, int) and h == 0):
                            pe.wait_ge(qk_out, 4 * (h - 1) + i + 1)
                        f, c = slice((i // 2) * FP, (i // 2) * FP + FP), slice(512 * (i % 2), 512 * (i % 2) + 512)
                        prods = [(a, b, k) for k in range(KT) for a, b in ((wH, xH), (wH, xL), (wL, xH))]
                        for q, (a, b, k) in enumerate(prods):
                            mm = pe.matmul(psV[:, i, :], a[par][:, k, f], b[:, k, c], start=(q == 0), stop=(q == 5))
                        mm.then_inc(qk_full, 1)

                def turn(h, par):
                    pe.wait_ge(p_ready, 2 * h + 2)
                    for i in range(2):
                        if not (isinstance(h, int) and h == 0):
                            pe.wait_ge(t_out, 2 * (h - 1) + i + 1)
                        for n in range(4):
                            mm = pe.transpose(psU[:, i, n * P:n * P + P], pf[par][:, 4 * i + n, :], ident[:, :])
                        mm.then_inc(t_full, 1)

                def scores(h, par):
                    pe.wait_ge(qk_out, 4 * h + 4)
                    if isinstance(h, int) and h < 2:
                        pe.wait_ge(l_exp, NT)
                    else:
                        pe.wait_ge(e_step, 2 * (h - 1))
                    for n in range(NT):
                        for b in range(2):
                            c = slice(n * P + b * TQ, n * P + b * TQ + TQ)
                            mm = pe.matmul(psC[tok_rows(b), par, n * TQ:n * TQ + TQ], qkT[:, 0, c], qkT[:, 1, c],
                                           start=True, stop=True, skip_group_check=True)
                    mm.then_inc(s_full, 1)

                def head(h, par, begun):
                    queries_keys(h, par)
                    if begun:
                        turn(h - 1, 1 - par)
                    scores(h, par)
                head(0, 0, False)
                head(1, 1, True)
                with pe.Fori(0, FH // 2 - 1) as i:
                    head(2 * i + 2, 0, True)
                    head(2 * i + 3, 1, True)
                turn(FH - 1, 1)

    for n, parts in (("vH", vH), ("vL", vL)):
        parts.append(sb(f"f_{n}1", [P, KT, FE * FP], F32R))
    for n, parts in (("oH", oH), ("oL", oL)):
        parts.append(sb(f"f_{n}1", [P, FE * DM], F32R))
    vh = sb("f_vh", [P, 2, P], F32)
    cf = sb("f_c", [P, 2, P], F32)
    cH = sb("f_cH", [P, 2, P], F32R)
    cL = sb("f_cL", [P, 2, P], F32R)
    part = sb("f_part", [P, 2, 2, DM], F32)
    acc = sb("f_acc", [P, NT, 2, DM], F32)
    v_full = sem("f_v_full")
    v_step = sem("f_v_step")
    c_full = sem("f_c_full")
    c_hi = sem("f_c_hi")
    c_lo = sem("f_c_lo")
    u_full = sem("f_u_full")
    u_step = sem("f_u_step")
    part_ready = sem("f_part_ready")
    acc_step = sem("f_acc_step")
    summed = sem("f_summed")
    PIECES = [[], [("v", 0)], [("v", 1)], [("v", 2)], [("v", 3), ("o", 0)], [("o", 1)], [("o", 2)], [("o", 3)]]
    assert len(PIECES) == NT
    x2 = s["x2"]

    def known(i, least):
        return not isinstance(i, int) or i >= least

    def heads(eng, head):
        head(0, 0, True)
        head(1, 1, True)
        with eng.Fori(0, FH // 2 - 2) as i:
            head(2 * i + 2, 0, True)
            head(2 * i + 3, 1, True)
        head(FH - 2, 0, True)
        head(FH - 1, 1, False)

    def follower(h, par, t):
        return (h, par, t + 1) if t + 1 < NT else (h + 1, 1 - par, 0)

    def gate_of(h, t, w, e):
        return gate[:, bass.ds(h, 1), t, w, e:e + 1].rearrange("p a e -> p (a e)")

    with nc.Block() as block:
        @block.sync
        def _(sp):
            def reload(h, par):
                sp.wait_ge(wlo_v, 4 * (h - 1))
                sp.wait_ge(wlo_o, 4 * (h - 1))
                load_experts(sp, d, s, h, par)
            with sp.Fori(0, FH // 2 - 1) as i:
                reload(2 * i + 2, 0)
                reload(2 * i + 3, 1)

        @block.gpsimd
        def _(pool):
            pool.memset(acc[:, :, :, :], 0.0).then_inc(acc_step, 1)

            def add(i, t, x):
                pool.wait_ge(part_ready, 4 * i + 2 * x + 2)
                pool.wait_ge(acc_step, 2 * i + x + 1)
                pool.tensor_tensor(acc[:, t, :, :], acc[:, t, :, :], part[:, x, :, :], ALU.add).then_inc(acc_step, 1)

            def head(h, par, more):
                for t in range(NT):
                    i, r = NT * h + t, t % 2
                    pool.wait_ge(c_hi, 2 * i + 2)
                    if known(i, 2):
                        pool.wait_ge(u_full, 4 * (i - 1))
                    pool.tensor_tensor(cL[:, r, :], cf[:, r, :], cH[:, r, :].bitcast(F32), ALU.subtract).then_inc(c_lo, 1)
                    if known(i, 1):
                        add(i - 1, (t - 1) % NT, 1)
                    if more:
                        for kind, q in PIECES[t]:
                            pool_cut(pool, h + 1, 1 - par, kind, q)
                    add(i, t, 0)
            heads(pool, head)
            add(NT * FH - 1, NT - 1, 1)

        @block.scalar
        def _(act):
            def head(h, par, more):
                for t in range(NT):
                    i, r = NT * h + t, t % 2
                    act.wait_ge(c_full, i + 1)
                    if known(i, 2):
                        act.wait_ge(u_full, 4 * (i - 1))
                    act.activation(cH[:, r, :], bankC, ACT.Copy).then_inc(c_hi, 1)
                    if known(i, 2):
                        act.wait_ge(c_lo, i - 1)
                    act.activation(cf[:, r, :], bankC, ACT.Copy).then_inc(c_hi, 1)
                    if more:
                        for kind, q in PIECES[t]:
                            act_cut(act, h + 1, 1 - par, kind, q)
                    for x in range(2):
                        k = 2 * x + 1
                        act.wait_ge(u_full, 4 * i + k + 1)
                        if known(i, 1):
                            act.wait_ge(acc_step, 2 * (i - 1) + x + 2)
                        for e in range(2):
                            act.activation(part[:, x, e, :], bankU[k % 3][:, e * DM:e * DM + DM], ACT.Copy,
                                           scale=gate_of(h, t, 1, 2 * k + e)).then_inc(part_ready, 1)
            heads(act, head)

        @block.vector
        def _(v):
            def value(h, t, e):
                i, r = NT * h + t, t % 2
                if e % 4 == 0:
                    v.wait_ge(v_full, 2 * i + e // 4 + 1)
                src = psV[:, 2 * r + e // 4, (e % 4) * FP:(e % 4) * FP + FP]
                if e == 0:
                    if known(i, 2):
                        v.wait_ge(c_full, i - 1)
                    v.tensor_scalar(vh[:, r, :], src, gate_of(h, t, 0, e), None, ALU.mult).then_inc(v_step, 1)
                else:
                    v.wait_ge(v_step, 8 * i + e)
                    v.scalar_tensor_tensor(out=vh[:, r, :], in0=src, scalar=gate_of(h, t, 0, e), in1=vh[:, r, :],
                                           op0=ALU.mult, op1=ALU.add).then_inc(v_step, 1)

            def output(h, t, x, e):
                i = NT * h + t
                if e == 0:
                    v.wait_ge(u_full, 4 * i + 2 * x + 1)
                if known(i, NT) or x or e:
                    v.wait_ge(u_step, 4 * i + 2 * x + e if x or e else 4 * (i - NT + 1))
                v.scalar_tensor_tensor(out=x2[:, t, :], in0=bankU[2 * x % 3][:, e * DM:e * DM + DM],
                                       scalar=gate_of(h, t, 1, 4 * x + e), in1=x2[:, t, :],
                                       op0=ALU.mult, op1=ALU.add).then_inc(u_step, 1)

            def head(h, par, more):
                for t in range(NT):
                    i = NT * h + t
                    nh, npar, nt = follower(h, par, t)
                    go = t + 1 < NT or more
                    before = known(i, 1)
                    bh, bt = (h, t - 1) if t else (h - 1, NT - 1)
                    if go:
                        value(nh, nt, 0)
                    if before:
                        output(bh, bt, 1, 0)
                    if go:
                        value(nh, nt, 1)
                    if before:
                        output(bh, bt, 1, 1)
                    if go:
                        value(nh, nt, 2)
                        value(nh, nt, 3)
                        value(nh, nt, 4)
                    output(h, t, 0, 0)
                    if go:
                        value(nh, nt, 5)
                    output(h, t, 0, 1)
                    if go:
                        value(nh, nt, 6)
                        value(nh, nt, 7)
                    if not more and t >= 2:
                        total(t - 2)

            def total(t):
                i = NT * (FH - 1) + t
                for e in range(2):
                    v.wait_ge(acc_step, 2 * i + 3)
                    v.wait_ge(u_step, 4 * i + 4)
                    if e:
                        v.wait_ge(summed, 2 * t + 1)
                    v.tensor_tensor(x2[:, t, :], x2[:, t, :], acc[:, t, e, :], ALU.add).then_inc(summed, 1)

            for e in range(FE):
                value(0, 0, e)
            heads(v, head)
            for e in range(2):
                output(FH - 1, NT - 1, 1, e)
            total(NT - 2)
            total(NT - 1)

        @block.tensor
        def _(pe):
            def values(h, par, t, x):
                i, r = NT * h + t, t % 2
                if t == 0 and x == 0:
                    pe.wait_ge(wlo_v, 4 * h + 4)
                if known(i, 2):
                    pe.wait_ge(v_step, 8 * (i - 2) + 4 * x + 4)
                prods = [(a, b, k) for k in range(KT) for a, b in ((xH, vH), (xH, vL), (xL, vH))]
                for q, (a, b, k) in enumerate(prods):
                    mm = pe.matmul(psV[:, 2 * r + x, :], a[:, k, t * P:t * P + P], b[par][:, k, 512 * x:512 * x + 512],
                                   start=(q == 0), stop=(q == 5))
                mm.then_inc(v_full, 1)

            def context(h, t):
                i, r = NT * h + t, t % 2
                pe.wait_ge(v_step, 8 * i + 8)
                if known(i, 1):
                    pe.wait_ge(c_hi, 2 * i)
                pe.matmul(bankC, vh[:, r, :], pT[:, bass.ds(h, 1), t, :].rearrange("p a q -> p (a q)"),
                          start=True, stop=True).then_inc(c_full, 1)

            def outputs(h, par, t):
                i = NT * h + t
                pe.wait_ge(c_lo, i + 1)
                if t == 0:
                    pe.wait_ge(wlo_o, 4 * h + 4)
                for k in range(4):
                    if k == 0 and known(i, 1):
                        pe.wait_ge(part_ready, 4 * i)
                    elif k == 1 and known(i, 1):
                        pe.wait_ge(part_ready, 4 * i - 2)
                    elif k == 2 and known(i, 1):
                        pe.wait_ge(u_step, 4 * i)
                    elif k == 3:
                        pe.wait_ge(u_step, 4 * i + 2)
                    for q, (a, b) in enumerate(((cH, oH), (cH, oL), (cL, oH))):
                        mm = pe.matmul(bankU[k % 3], a[:, t % 2, :], b[par][:, 512 * k:512 * k + 512],
                                       start=(q == 0), stop=(q == 2))
                    mm.then_inc(u_full, 1)

            def head(h, par, more):
                for t in range(NT):
                    nh, npar, nt = follower(h, par, t)
                    go = t + 1 < NT or more
                    if go:
                        values(nh, npar, nt, 0)
                    context(h, t)
                    if go:
                        values(nh, npar, nt, 1)
                    outputs(h, par, t)
            values(0, 0, 0, 0)
            values(0, 0, 0, 1)
            heads(pe, head)


def build(nc, d, out, stages=3):
    with ExitStack() as whole:
        def sem(name):
            return whole.enter_context(nc.semaphore(name))
        def keep(name, shape, dt):
            return whole.enter_context(nc.sbuf_tensor(name, shape, dt))
        s = {}
        s["ident"] = keep("ident", [P, P], F32)
        s["x1"] = keep("x1", [P, NT, DM], F32)
        with ExitStack() as st:
            def sb(name, shape, dt):
                return st.enter_context(nc.sbuf_tensor(name, shape, dt))
            s["psS"] = st.enter_context(nc.psum_tensor("psS", [P, 2, 1024], F32))
            s["psW"] = st.enter_context(nc.psum_tensor("psW", [P, 3, 512], F32))
            s["psO"] = st.enter_context(nc.psum_tensor("psO", [P, 512], F32))
            s["identb"] = sb("identb", [P, P], BF16)
            s["head_rows"] = sb("head_rows", [P, 4], F32)
            s["den_rows"] = sb("den_rows", [P, P], F32)
            s["wH"] = sb("wH", [P, 2, KT, DM], F32R)
            s["wL"] = sb("wL", [P, 2, KT, DM], F32R)
            s["woP"] = sb("woP", [P, 4, DM], F32)
            s["qD"] = sb("qD", [P, 4, TOK], F32)
            s["dT"] = sb("dT", [P, 2, H * TQ], F32)
            s["dN"] = sb("dN", [P, H // 2, NEAR], BF16)
            s["ctx"] = sb("ctx", [P, 2, KT, 512], F32)
            s["mcols"] = sb("mcols", [P, 2, NKT, B], F32)
            s["V"] = [sb(f"V{i}", [P, NKT, H, DK + 1], F32) for i in range(2)]
            with ExitStack() as pro:
                def sbp(name, shape, dt):
                    return pro.enter_context(nc.sbuf_tensor(name, shape, dt))
                s["xn"] = sbp("xn", [P, NT, DM], F32)
                s["xnT"] = sbp("xnT", [P, KT, TOK], F32)
                prologue(nc, d, s, sbp, sem)
            cross_attention(nc, d, s, sb, sem)
        with ExitStack() as st:
            def sb(name, shape, dt):
                return st.enter_context(nc.sbuf_tensor(name, shape, dt))
            loads = sem("late_loads")
            s["x2"] = sb("x2", [P, NT, DM], F32)
            s["vraw"] = [sb(f"vraw{i}", [P, KT, FE * FP], F32) for i in range(2)]
            s["oraw"] = [sb(f"oraw{i}", [P, FE * DM], F32) for i in range(2)]
            s["qkw"] = sb("qkw", [P, KT, FH, 2 * FP], F32)
            s["sel"] = sb("sel", [P, KT, 2 * FH * FE], F32)
            s["rank"] = sb("rank", [P, FE], F32)
            s["route"] = sb("route", [P, 1], F32)
            sa = ExitStack()

            def sba(name, shape, dt):
                return sa.enter_context(nc.sbuf_tensor(name, shape, dt))
            s["wattn"] = sba("wattn", [P, KT, 3 * DM], F32)
            s["wprojP"] = sba("wprojP", [P, 4, DM], F32)
            s["alibi"] = sba("alibi", [P, H * TQ], F32)
            s["head_rows2"] = sba("head_rows2", [P, HT], F32)
            s["den_rows2"] = sba("den_rows2", [P, P], F32)
            zeroed = sem("wproj_zeroed")
            s["attn_loads"], s["ffn_loads"] = sem("attn_loads"), sem("ffn_loads")
            s["v_in"], s["o_in"] = [[sem(f"{n}_in{i}") for i in range(2)] for n in "vo"]
            first = [
                (s["wattn"][:, :, :], d["aWT"].rearrange("(k p) f -> p k f", p=P)),
                (s["alibi"][:, :], d["c_alibi"]),
                (s["head_rows2"][:, :], d["c_head_rows"]),
                (s["den_rows2"][:, :], d["c_den_rows"]),
            ]
            wo_view = d["aPT"].rearrange("(g j e) n -> j e g n", j=4, e=DK)
            first += [(s["wprojP"][32 * j:32 * j + DK, :, :], wo_view[j]) for j in range(4)]
            late = [
                (s["sel"][:, :, :], d["selT"].rearrange("(k p) f -> p k f", p=P)),
                (s["rank"][:, :], d["c_rank"].to_broadcast([P, FE])),
                (s["route"][:, :], d["route"].rearrange("(a b) -> a b", a=1).to_broadcast([P, 1])),
                (s["qkw"][:, :, :, :], d["qkT"].rearrange("(k p) h f -> p k h f", p=P)),
            ]
            s["attn_loads_total"], s["ffn_loads_total"] = 16 * len(first), 16 * len(late)
            with nc.Block() as block:
                @block.gpsimd
                def _(pool):
                    pool.memset(s["wprojP"][:, :, :], 0.0).then_inc(zeroed, 1)

                @block.sync
                def _(sp):
                    sp.wait_ge(zeroed, 1)
                    for dst, src in first:
                        sp.dma_start(dst, src).then_inc(s["attn_loads"], 16)
                    for dst, src in late:
                        sp.dma_start(dst, src).then_inc(s["ffn_loads"], 16)
                    for h in range(2):
                        load_experts(sp, d, s, h, h)
            with sa:
                self_attention(nc, d, s, sba, lambda n, sh: sa.enter_context(nc.psum_tensor(n, sh, F32)), sem)
            if stages == 3:
                with ExitStack() as sf:
                    switch_head(nc, d, s, lambda n, sh, dt: sf.enter_context(nc.sbuf_tensor(n, sh, dt)),
                                lambda n, sh: sf.enter_context(nc.psum_tensor(n, sh, F32)), sem)
            wrote = sem("wrote")
            with nc.Block() as block:
                @block.sync
                def _(sp):
                    sp.dma_start(out.rearrange("(n p) f -> p n f", p=P), s["x2"][:, :, :])\
                      .then_inc(wrote, 16)
                    sp.wait_ge(wrote, 16)


def layout(i):
    import numpy as _np
    C = _np.ascontiguousarray
    v = _np.asarray(i["L0_ffn_v_w"]).reshape(FH, FE, DM, FP).transpose(2, 0, 1, 3).reshape(DM, FH, FE * FP)
    o = _np.asarray(i["L0_ffn_o_w"]).reshape(FH, FE, FP, DM).transpose(0, 2, 1, 3).reshape(FH, FP, FE * DM)
    sel = _np.stack([_np.asarray(i[f"L0_ffn_sel_{n}_w"]).reshape(FH, FE, DM) for n in "vo"], axis=1).reshape(2 * FH * FE, DM)
    qk = _np.concatenate([_np.asarray(i[f"L0_ffn_{n}_w"]).reshape(FH, FP, DM) for n in "qk"], axis=1)
    ins = {
        "x": _np.asarray(i["x"]).reshape(TOK, DM),
        "ctxT": C(_np.asarray(i["ctx_1024"]).transpose(0, 2, 1)),
        "mask": _np.asarray(i["mask_Bx1x1xS2_bk0"]).reshape(B, TK),
        "xWqD": C(_np.stack(2 * [_np.asarray(i["L0_xattn_Wq"]).T.reshape(DM, 4, 64)], axis=2).reshape(DM, 4, P)),
        "xWkT": C(_np.asarray(i["L0_xattn_Wk"]).T),
        "xWvT": C(_np.asarray(i["L0_xattn_Wv"]).T), "xWoT": C(_np.asarray(i["L0_xattn_Wo"]).T),
        "rbT": C(_np.asarray(i["L0_xattn_rel_bias"]).T),
        "aWT": C(_np.asarray(i["L0_attn_W_attn"]).T), "aPT": C(_np.asarray(i["L0_attn_W_proj"]).T),
        "qkT": C(qk.transpose(2, 0, 1)),
        "vw": C(v), "ow": C(o), "selT": C(sel.T), "route": C(_np.asarray(i["L0_ffn_route_scale"])),
    }
    ins.update(constants())
    return ins


def kernel(**inputs):
    import concourse.bacc as _bacc
    from concourse import mybir as _mybir
    from concourse.bass_utils import run_bass_kernel_spmd as _run

    nc = _bacc.Bacc("TRN2", target_bir_lowering=False, num_devices=1)
    arrays, args = {}, {}
    for name, a in layout(inputs).items():
        arrays[f"in_{name}"] = a
        args[name] = nc.dram_tensor(f"in_{name}", a.shape, _mybir.dt.from_np(a.dtype), kind="ExternalInput").ap()
    out = nc.dram_tensor("out_0", (TOK, DM), F32, kind="ExternalOutput").ap()
    build(nc, args, out)
    r = _run(nc, [arrays], core_ids=[0])
    return r.results[0]["out_0"].reshape(B, TQ, DM)
```

```python
import math
from contextlib import ExitStack

import numpy as np

import concourse.bass as bass
from concourse import mybir

F32 = mybir.dt.float32
F32R = mybir.dt.float32r
BF16 = mybir.dt.bfloat16
U8 = mybir.dt.uint8
ALU = mybir.AluOpType
ACT = mybir.ActivationFunctionType
AX = mybir.AxisListType

P = 128
B, TQ, DM = 16, 64, 256
TOK = B * TQ
NT = TOK // P
KT = DM // P
H, DK = 16, 16
HT = P // DK
TK = 1601
KTILES = [(t * P, min(P, TK - t * P)) for t in range((TK + P - 1) // P)]
NKT = len(KTILES)
CHUNKS = [(0, 1, 2, 3), (4, 5, 6), (7, 8, 9), (10, 11, 12)]
NC = len(CHUNKS)
CSPAN = [(KTILES[c[0]][0], sum(KTILES[t][1] for t in c)) for c in CHUNKS]
NEAR = 256
NEG = 1.0e9
EPS = 1e-5
FH, FE, FP = 8, 8, 128
BUCKETS, MAXDIST = 32, 128


def relative_buckets(rel):
    nb = BUCKETS // 2
    rp = np.abs(rel)
    exact = nb // 2
    large = exact + (np.log(np.maximum(rp, 1).astype(np.float32) / np.float32(exact))
                     / np.float32(math.log(MAXDIST / exact)) * np.float32(nb - exact)).astype(np.int32)
    large = np.minimum(large, nb - 1)
    return (rel > 0).astype(np.int32) * nb + np.where(rp < exact, rp, large)


def constants():
    rel = np.arange(NEAR + TQ - 1) - (TQ - 1)
    onehot = (np.arange(BUCKETS)[:, None] == relative_buckets(rel)[None, :]).astype(np.float32)
    assert relative_buckets(np.arange(NEAR - TQ + 1, TK)).min() == BUCKETS - 1
    part = np.arange(P)
    head_rows = (part[:, None] // DK == np.arange(HT)[None, :]).astype(np.float32)
    den_rows = (part[:, None] == 32 * (part[None, :] // 32) + DK).astype(np.float32)
    start = 2.0 ** (-2.0 ** (-(math.log2(H) - 3)))
    slopes = np.array([start * start ** i for i in range(H)], np.float32)
    pos = np.arange(TQ, dtype=np.float32)
    dist = pos[None, :] - pos[:, None]
    alibi = slopes[None, :, None] * dist[:, None, :]
    alibi = np.where((dist <= 0)[:, None, :], alibi, np.float32(-1e30)).reshape(TQ, H * TQ)
    return {
        "c_onehot": np.concatenate(3 * [onehot]),
        "c_head_rows": head_rows,
        "c_head_rows4": (part[:, None] % 64 // DK == np.arange(4)[None, :]).astype(np.float32),
        "c_den_rows": den_rows,
        "c_rank": (FE - np.arange(FE, dtype=np.float32)).reshape(1, FE),
        "c_ident": np.eye(P, dtype=np.float32),
        "c_alibi": np.concatenate([alibi, alibi]).astype(np.float32),
    }


def tok_rows(par):
    return slice(TQ * par, TQ * par + TQ)


def layer_norm_steps(v, x, stats, mv, rstd, step):
    for n in range(NT):
        v.bn_stats(stats[:, n, :], x[:, n, :]).then_inc(step, 1)
    v.wait_ge(step, NT)
    for n in range(NT):
        v.bn_aggr(mv[:, n, :], stats[:, n, :]).then_inc(step, 1)
    v.wait_ge(step, 2 * NT)
    v.tensor_scalar(rstd[:, :], mv[:, :, 1], EPS, None, ALU.add).then_inc(step, 1)


def prologue(nc, d, s, sb, sem):
    xn, xnT = s["xn"], s["xnT"]
    psW, psS, psO = s["psW"], s["psS"], s["psO"]
    loads = sem("pro_loads")
    consts = sem("pro_consts")
    ln = sem("pro_ln")
    root = sem("pro_root")
    xn_ready = sem("pro_xn")
    turned = sem("pro_turned")
    xnT_out = sem("pro_xnT")
    q_full = sem("pro_q")
    q_out = sem("pro_q_out")
    w_hi = sem("pro_w_hi")
    rb_ready = sem("pro_rb")
    near_full = sem("pro_near")
    near_out = sem("pro_near_out")
    dN_full = sem("pro_dN")
    dN_out = sem("pro_dN_out")
    mrow = sem("pro_mrow")
    m_full = sem("pro_m_full")
    m_out = sem("pro_m_out")
    PARTS = 3
    rbT = sb("rbT", [PARTS * BUCKETS, H], F32)
    rb_far = sb("rb_far", [PARTS * BUCKETS, H], F32)
    rb_part = sb("rb_part", [PARTS * BUCKETS, H], BF16)
    rb_parts = sb("rb_parts", [PARTS * BUCKETS, H], BF16)
    onehot = sb("onehot", [PARTS * BUCKETS, NEAR + TQ - 1], F32)
    onehotb = sb("onehotb", [PARTS * BUCKETS, NEAR + TQ - 1], BF16)
    m16 = sb("m16", [B, TK], U8)
    m16f = sb("m16f", [B, TK], F32)
    mb16 = sb("mb16", [B, TK], F32)
    any16 = sb("any16", [B, 2], F32)
    stats = sb("stats", [P, NT, 6], F32)
    mv = sb("mv", [P, NT, 2], F32)
    rstd = sb("rstd", [P, NT], F32)
    wq = sb("wq", [P, KT, 4, P], F32)
    wkv = sb("wkv", [P, 2, KT, DM], F32)
    dma_list = [
        (s["x1"][:, :, :], d["x"].rearrange("(n p) f -> p n f", p=P)),
        (s["ident"][:, :], d["c_ident"]),
        (wq[:, :, :, :], d["xWqD"].rearrange("(k p) g f -> p k g f", p=P)),
        (onehot[:, :], d["c_onehot"]),
        *[(rbT[BUCKETS * i:BUCKETS * i + BUCKETS, :], d["rbT"]) for i in range(PARTS)],
        (rb_far[:, :], d["rbT"][BUCKETS - 1:BUCKETS, :].to_broadcast([PARTS * BUCKETS, H])),
        (m16[:, :], d["mask"]),
        (s["head_rows"][:, :], d["c_head_rows4"]),
        (wkv[:, 0, :, :], d["xWkT"].rearrange("(k p) f -> p k f", p=P)),
        (wkv[:, 1, :, :], d["xWvT"].rearrange("(k p) f -> p k f", p=P)),
        (s["den_rows"][:, :], d["c_den_rows"]),
    ]
    wo_view = d["xWoT"].rearrange("(g j e) n -> j e g n", j=4, e=DK)
    NL = 16 * (len(dma_list) + 4)
    with nc.Block() as block:
        @block.sync
        def _(sp):
            for dst, src in dma_list:
                sp.dma_start(dst, src).then_inc(loads, 16)
            sp.wait_ge(consts, 1)
            for j in range(4):
                sp.dma_start(s["woP"][32 * j:32 * j + DK, :, :], wo_view[j]).then_inc(loads, 16)
            sp.wait_ge(loads, NL)

        @block.gpsimd
        def _(pool):
            pool.memset(s["woP"][:, :, :], 0.0).then_inc(consts, 1)
            pool.memset(s["ctx"][:, 1, :, CSPAN[-1][1]:CSPAN[-1][1] + 1], 0.0).then_inc(consts, 1)
            for par in range(2):
                pool.memset(s["V"][par][:, :, :, DK:DK + 1], 1.0).then_inc(consts, 1)
            pool.wait_ge(loads, NL)
            pool.tensor_copy(s["identb"][:, :], s["ident"][:, :]).then_inc(consts, 1)
            pool.wait_ge(w_hi, 1)
            pool.tensor_tensor(s["wL"][:, :, :, :], wkv[:, :, :, :], s["wH"][:, :, :, :].bitcast(F32), ALU.subtract)\
                .then_inc(consts, 1)

        @block.vector
        def _(v):
            v.memset(psO[:, :], 0.0)
            v.memset(psW[:, 2, :], 0.0).then_inc(mrow, 1)
            v.wait_ge(loads, NL)
            layer_norm_steps(v, s["x1"], stats, mv, rstd, ln)
            v.tensor_copy(m16f[:, :], m16[:, :]).then_inc(mrow, 1)
            v.wait_ge(mrow, 2)
            v.tensor_reduce(any16[:, 0:1], m16f[:, :], AX.X, ALU.max).then_inc(mrow, 1)
            v.wait_ge(mrow, 3)
            v.tensor_scalar(any16[:, 1:2], any16[:, 0:1], NEG, None, ALU.mult).then_inc(mrow, 1)
            v.wait_ge(mrow, 4)
            v.tensor_scalar(mb16[:, :], m16f[:, :], -1.0, any16[:, 1:2], ALU.add, ALU.mult).then_inc(mrow, 1)
            v.tensor_copy(onehotb[:, :], onehot[:, :])
            v.tensor_tensor(rbT[:, :], rbT[:, :], rb_far[:, :], ALU.subtract).then_inc(rb_ready, 1)
            for i in range(PARTS):
                v.wait_ge(rb_ready, 3 * i + 1)
                v.tensor_copy(rb_part[:, :], rbT[:, :]).then_inc(rb_ready, 1)
                v.wait_ge(rb_ready, 3 * i + 2)
                rows = slice(BUCKETS * i, BUCKETS * i + BUCKETS)
                v.tensor_copy(rb_parts[rows, :], rb_part[rows, :]).then_inc(rb_ready, 1)
                v.tensor_tensor(rbT[:, :], rbT[:, :], rb_part[:, :], ALU.subtract).then_inc(rb_ready, 1)
            v.wait_ge(root, 1)
            v.reciprocal(rstd[:, :], rstd[:, :]).then_inc(ln, 1)
            v.wait_ge(ln, 2 * NT + 2)
            for n in range(NT):
                v.tensor_scalar(xn[:, n, :], s["x1"][:, n, :], mv[:, n, 0:1], rstd[:, n:n + 1],
                                ALU.subtract, ALU.mult).then_inc(xn_ready, 1)
            for i in range(4):
                v.wait_ge(turned, i + 1)
                v.tensor_copy(xnT[:, i // 2, (i % 2) * 512:(i % 2) * 512 + 512], psS[:, i // 2, (i % 2) * 512:(i % 2) * 512 + 512])\
                 .then_inc(xnT_out, 1)
            v.wait_ge(m_full, 1)
            v.tensor_copy(s["mcols"].rearrange("p a t b -> p (a t b)"), psW[:, 2, 0:2 * NKT * B]).then_inc(m_out, 1)
            for i in range(8):
                v.wait_ge(q_full, i + 1)
                g, c = i // 2, slice((i % 2) * 512, (i % 2) * 512 + 512)
                v.tensor_copy(s["qD"][:, g, c], psW[:, i % 2, :]).then_inc(q_out, 1)
            for t in range(2):
                v.wait_ge(near_full, t + 1)
                v.tensor_copy(s["dT"][:, t, :].rearrange("p (h q) -> p h q", q=TQ),
                              psS[:, t, :].rearrange("p (q h) -> p h q", h=H)).then_inc(near_out, 1)
            for i in range(4):
                v.wait_ge(dN_full, i + 1)
                v.tensor_copy(s["dN"][:, 2 * i:2 * i + 2, :], psW[:, i % 2, :].rearrange("p (a k) -> p a k", a=2))\
                 .then_inc(dN_out, 1)

        @block.scalar
        def _(act):
            act.wait_ge(loads, NL)
            act.activation(s["wH"][:, :, :, :], wkv[:, :, :, :], ACT.Copy).then_inc(w_hi, 1)
            act.wait_ge(ln, 2 * NT + 1)
            act.activation(rstd[:, :], rstd[:, :], ACT.Sqrt).then_inc(root, 1)

        @block.tensor
        def _(pe):
            pe.wait_ge(loads, NL)
            pe.wait_ge(mrow, 5)
            for a, rows in enumerate((m16f, mb16)):
                for t, (k0, kw) in enumerate(KTILES):
                    c = (a * NKT + t) * B
                    mm = pe.transpose(psW[0:kw, 2, c:c + B], rows[:, k0:k0 + kw], s["ident"][0:B, 0:B])
            mm.then_inc(m_full, 1)
            for i in range(4):
                for n in range(4):
                    pe.wait_ge(xn_ready, (i % 2) * 4 + n + 1)
                    mm = pe.transpose(psS[:, i // 2, (i % 2) * 512 + n * P:(i % 2) * 512 + n * P + P],
                                      xn[:, (i % 2) * 4 + n, (i // 2) * P:(i // 2) * P + P], s["ident"][:, :])
                mm.then_inc(turned, 1)
            pe.wait_ge(xnT_out, 4)
            for i in range(8):
                if i >= 2:
                    pe.wait_ge(q_out, i - 1)
                for k in range(KT):
                    mm = pe.matmul(psW[:, i % 2, :], wq[:, k, i // 2, :],
                                   xnT[:, k, (i % 2) * 512:(i % 2) * 512 + 512], start=(k == 0), stop=(k == KT - 1))
                mm.then_inc(q_full, 1)
            pe.wait_ge(rb_ready, 3 * PARTS + 1)
            for t in range(2):
                for q in range(TQ):
                    off = t * P - q + TQ - 1
                    mm = pe.matmul(psS[:, t, q * H:q * H + H], onehotb[:, off:off + P],
                                   rb_parts[:, :], start=True, stop=True, skip_group_check=True)
                mm.then_inc(near_full, 1)
            pe.wait_ge(near_out, 2)
            for i in range(4):
                pe.wait_ge(q_out, 8)
                if i >= 2:
                    pe.wait_ge(dN_out, i - 1)
                for a in range(2):
                    for t in range(2):
                        pr = 2 * i + a
                        mm = pe.transpose(psW[:, i % 2, a * NEAR + t * P:a * NEAR + t * P + P],
                                          s["dT"][:, t, pr * P:pr * P + P], s["ident"][:, :])
                mm.then_inc(dN_full, 1)


def cross_attention(nc, d, s, sb, sem):
    psS, psW, psO = s["psS"], s["psW"], s["psO"]
    ctx = s["ctx"]
    V = s["V"]
    HG = 4
    cH = sb("cH", [P, 2, KT, 512], F32R)
    cL = sb("cL", [P, 2, KT, 512], F32R)
    kHL = [sb(f"kHL{i}", [P, HG, TK + 1], F32R) for i in range(2)]
    qb = sb("qb", [P, HG, 4 * TQ], F32)
    qh = [sb(f"qh{i}", [P, HG, 4 * TQ], F32R) for i in range(2)]
    ql = [sb(f"ql{i}", [P, HG, 4 * TQ], F32R) for i in range(2)]
    m8 = [sb(f"m8_{i}", [P, TK], U8) for i in range(2)]
    mneg = [sb(f"mneg{i}", [P, TK], BF16) for i in range(2)]
    near = sb("near", [P, H // 2, NEAR], BF16)
    mc = [sb(f"mc{i}", [P, 2, NKT, 1], F32) for i in range(2)]
    mx = [sb(f"mx{i}", [P, H // 2, NC + 1], F32) for i in range(2)]
    cv = [sb(f"cv{i}", [P, H // 2, 2], BF16) for i in range(2)]
    cm = sb("cm", [P, H // 2], F32)
    cr = sb("cr", [P, H // 2], F32)
    shift = sb("shift", [P, H * TQ], F32)
    PTR = 3
    pT = sb("pT", [P, PTR, H * TQ], F32)
    oT = sb("oT", [P, DM], F32)
    oR = sb("oR", [P, DM], F32)
    oN = oR
    x1 = s["x1"]

    ctx_in = [sem(f"ctx_in{c}") for c in range(NC)]
    mask_in = [sem(f"mask_in{i}") for i in range(2)]
    ctx_hi = sem("ctx_hi")
    ctx_lo = sem("ctx_lo")
    work_full = sem("work_full")
    k_hi = sem("k_hi")
    k_lo = sem("k_lo")
    v_out = sem("v_out")
    maxed = sem("maxed")
    mneg_ready = sem("mneg_ready")
    near_ready = sem("near_ready")
    q_ready = sem("q_ready")
    qb_ready = sem("qb_ready")
    mc_ready = sem("mc_ready")
    c_step = sem("c_step")
    s_full = sem("s_full")
    s_read = sem("s_read")
    added = sem("added")
    pv_done = sem("pv_done")
    o_out = sem("o_out")
    d_full = sem("d_full")
    o_step = sem("o_step")
    y_full = sem("y_full")
    y_out = sem("y_out")
    rows_done = sem("rows_done")
    waited = sem("waited")

    SB = NKT + 1
    HI, LO = s["wH"], s["wL"]
    USES = [("K", 0), ("V", 0), ("A", 0), ("A", 1), ("K", 1), ("A", 2), ("A", 3), ("V", 1), ("A", 4), ("A", 5), ("A", 6), ("A", 7)]
    NU = len(USES)
    LAST_KV = max(i for i, use in enumerate(USES) if use[0] != "A") + 1
    SLOTS = [(((0,), (1, 2, 3, 4, 5, 6)), ((7,), (8,)), ((9,), (10,)), ((11,), ()))] + 3 * [(((0,), (1, 2, 3)), ((4,), (5, 6)), ((7, 8, 9), (10, 11)))]

    def bank_read(n, u):
        kind, i = USES[u]
        return {"K": (k_lo, 4 * n + 2 * i + 2), "V": (v_out, 2 * n + i + 1), "A": (maxed, 8 * n + i + 1)}[kind]

    def exps(b, t):
        return SB * b + t + 2

    def adds(b, t):
        return 15 * b + (2 * t + 2 if t < 2 else t + 3)

    def slot(c, i):
        return SLOTS[c][i][0] + SLOTS[c][i][1]

    def at_least(eng, sm, value):
        if not (isinstance(value, int) and value <= 0):
            eng.wait_ge(sm, value)

    def wait_apart(eng, sm, value):
        eng.wait_ge(sm, value)
        eng.sem_inc(waited, 1)

    def groups(c):
        ts = CHUNKS[c]
        return [ts[0:2], ts[2:]]

    def width(c):
        return CSPAN[c][1] + CSPAN[c][1] % 2

    def pe_use(pe, j, par, c, u):
        n = j * NC + c
        r = c % 2
        k0, w = CSPAN[c][0], width(c)
        bank = psW[:, u % 3, :]
        kind, i = USES[u]
        at_least(pe, *(bank_read(n, u - 3) if u >= 3 else bank_read(n - 1, u + NU - 3)))
        if u == 0:
            pe.wait_ge(ctx_lo, n + 1)
        if kind == "A" and i % 4 == 0:
            pe.wait_ge(k_lo, 4 * n + 2 * (i // 4) + 2)
            pe.wait_ge(q_ready, 2 * j + 1)
        if kind == "K":
            prods = [(a, b, k) for k in range(KT) for a, b in ((HI, cH), (HI, cL), (LO, cH))]
            for q, (a, b, k) in enumerate(prods):
                mm = pe.matmul(bank[:, 0:w], a[:, 0, k, i * P:i * P + P], b[:, r, k, 0:w],
                               start=(q == 0), stop=(q == len(prods) - 1))
        elif kind == "V":
            for z, t in enumerate(groups(c)[i]):
                a0, kw = KTILES[t][0] - k0, KTILES[t][1]
                prods = [(a, b, k) for k in range(KT) for a, b in ((cH, HI), (cH, LO), (cL, HI))]
                for q, (a, b, k) in enumerate(prods):
                    mm = pe.matmul(bank[0:kw, z * DM:z * DM + DM], a[:, r, k, a0:a0 + kw], b[:, 1, k, :],
                                   start=(q == 0), stop=(q == len(prods) - 1))
        else:
            mm = pe.matmul(bank[:, 0:w], qh[par][:, i // 2, (i % 2) * P:(i % 2) * P + P], kHL[par][:, i // 2, k0:k0 + w],
                           start=True, stop=True)
        mm.then_inc(work_full, 1)

    def pe_shift(pe, b, par):
        pe.wait_ge(c_step, 5 * (b + 1))
        at_least(pe, s_read, SB * b)
        for p in range(H // 2):
            for i in range(2):
                mm = pe.matmul(psS[:, 1, p * P:p * P + P], cv[par][:, p, i:i + 1].to_broadcast([P, P]), s["identb"][:, :],
                               start=(i == 0), stop=(i == 1), skip_group_check=True)
        mm.then_inc(s_full, 1)

    def buf(t):
        return 0 if t == 0 else (t + 1) % 2

    def pe_scores(pe, b, par, t):
        a, kw = KTILES[t]
        if t == 0:
            pe.wait_ge(q_ready, 2 * b + 2)
            at_least(pe, s_read, SB * b - 1)
        elif t == 2:
            pe.wait_ge(s_read, SB * b + 1)
        else:
            pe.wait_ge(s_read, exps(b, max(t - 2, 0)))
        for g in range(HG):
            o = psS[0:kw, buf(t), g * 256:g * 256 + 256]
            for i, q in enumerate((qh, ql)):
                mm = pe.matmul(o, kHL[par][:, g, a:a + kw], q[par][:, g, :], start=(i == 0), stop=(i == 1),
                               skip_group_check=True)
        mm.then_inc(s_full, 1)

    def pe_values(pe, b, par, t):
        kw = KTILES[t][1]
        pe.wait_ge(s_read, exps(b, t))
        if t == 0:
            at_least(pe, y_out, b)
        for h in range(H):
            r, g = 32 * (h % 4), h // 4
            mm = pe.matmul(psO[r:r + DK + 1, g * TQ:g * TQ + TQ], V[par][0:kw, t, h, :],
                           pT[0:kw, t % PTR, h * TQ:h * TQ + TQ], start=(t == 0 and g == 0), stop=(t == NKT - 1),
                           skip_group_check=True)
        mm.then_inc(pv_done, 1)

    def pe_denominators(pe, b):
        pe.wait_ge(o_out, b + 1)
        pe.matmul(psO[:, 256:512], s["den_rows"][:, :], oT[:, :], start=True, stop=True,
                  skip_group_check=True).then_inc(d_full, 1)

    def pe_project(pe, b, par):
        pe.wait_ge(o_step, 2 * b + 2)
        for g in range(4):
            mm = pe.matmul(psO[tok_rows(par), 256:512], oN[:, g * TQ:g * TQ + TQ], s["woP"][:, g, :],
                           start=(g == 0), stop=(g == 3), skip_group_check=True)
        mm.then_inc(y_full, 1)

    def pe_step(pe, j, par, prep, main, fin, ahead):
        for c in range(NC):
            for i, t in enumerate(CHUNKS[c]):
                if main:
                    pe_scores(pe, j - 1, 1 - par, t)
                if t == 0 and fin:
                    pe_denominators(pe, j - 2)
                if prep:
                    for u in SLOTS[c][i][0]:
                        pe_use(pe, j, par, c, u)
                if main and t == 0:
                    pe_shift(pe, j - 1, 1 - par)
                elif main:
                    pe_values(pe, j - 1, 1 - par, t - 1)
                if prep:
                    for u in SLOTS[c][i][1]:
                        pe_use(pe, j, par, c, u)
                if t == 0 and fin:
                    pe_project(pe, j - 2, par)
        if main:
            pe_values(pe, j - 1, 1 - par, NKT - 1)

    def act_split(act, j, c):
        n = j * NC + c
        w = width(c)
        act.wait_ge(ctx_in[c], 16 * (j + 1))
        at_least(act, work_full, NU * (n - 2) + LAST_KV)
        act.activation(cH[:, c % 2, :, 0:w], ctx[:, c % 2, :, 0:w], ACT.Copy).then_inc(ctx_hi, 1)

    def act_use(act, j, par, c, u):
        n = j * NC + c
        k0, w = CSPAN[c][0], width(c)
        kind, i = USES[u]
        if kind != "A":
            act.wait_ge(work_full, NU * n + u + 1)
        if kind == "K":
            for g in range(2):
                rows = slice(64 * g, 64 * g + 64)
                act.activation(kHL[par][rows, 2 * i + g, k0:k0 + w], psW[rows, u % 3, 0:w], ACT.Copy).then_inc(k_hi, 1)
        elif kind == "V":
            ts = groups(c)[i]
            kw = KTILES[ts[-1]][1]
            act.activation(V[par][0:kw, ts[0]:ts[-1] + 1, :, 0:DK],
                           psW[0:kw, u % 3, 0:len(ts) * DM].rearrange("p (t h e) -> p t h e", t=len(ts), e=DK),
                           ACT.Copy).then_inc(v_out, 1)

    def act_exp(act, b, par, t):
        kw = KTILES[t][1]
        if t == 0:
            act.wait_ge(mc_ready, b + 1)
        if t >= PTR:
            act.wait_ge(pv_done, NKT * b + t - PTR + 1)
        else:
            at_least(act, pv_done, NKT * (b - 1) + [13, 11, 12][t])
        act.wait_ge(added, adds(b, t))
        act.activation(pT[0:kw, t % PTR, :], psS[0:kw, buf(t), :], ACT.Exp,
                       bias=mc[par][0:kw, 1, t, :], scale=mc[par][0:kw, 0, t, :]).then_inc(s_read, 1)

    def act_step(act, j, par, prep, main, fin, ahead):
        b = j - 1
        if isinstance(j, int) and j == 0:
            act_split(act, 0, 0)
        for c in range(NC):
            for i, t in enumerate(CHUNKS[c]):
                if prep and t == 0 and not (isinstance(j, int) and j < 2):
                    act.wait_ge(pv_done, NKT * (j - 1))
                if prep:
                    act_use(act, j, par, c, slot(c, i)[0])
                if main and t == 0:
                    act.wait_ge(s_full, SB * b + 2)
                    act.activation(shift[:, :], psS[:, 1, :], ACT.Copy).then_inc(s_read, 1)
                if prep and t == 0:
                    for u in slot(c, i)[1:]:
                        act_use(act, j, par, c, u)
                if main:
                    act_exp(act, b, 1 - par, t)
                if prep and t:
                    for u in slot(c, i):
                        if u != slot(c, i)[0]:
                            act_use(act, j, par, c, u)
                    if i == 1 and (c < NC - 1 or ahead):
                        act_split(act, j if c < NC - 1 else j + 1, (c + 1) % NC)

    def dve_use(v, j, par, c, u):
        n = j * NC + c
        k0, w = CSPAN[c]
        kind, p = USES[u]
        if kind == "K":
            w = width(c)
            for g in range(2):
                rows, other = slice(64 * g, 64 * g + 64), slice(64 - 64 * g, 128 - 64 * g)
                v.wait_ge(k_hi, 4 * n + 2 * p + g + 1)
                v.tensor_tensor(kHL[par][other, 2 * p + g, k0:k0 + w], psW[rows, u % 3, 0:w],
                                kHL[par][rows, 2 * p + g, k0:k0 + w].bitcast(F32), ALU.subtract).then_inc(k_lo, 1)
        elif kind == "A":
            bank = psW[:, u % 3, :]
            if c == 0 and p == 0:
                v.wait_ge(near_ready, j + 1)
            wait_apart(v, work_full, NU * n + u + 1)
            if c == 0:
                v.tensor_tensor_reduce(bank[:, 0:NEAR], bank[:, 0:NEAR], near[:, p, :], 1.0, -3e38,
                                       ALU.add, ALU.max, mx[par][:, p, 0:1])
                v.tensor_tensor_reduce(bank[:, NEAR:w], bank[:, NEAR:w], mneg[par][:, NEAR:w], 1.0, -3e38,
                                       ALU.add, ALU.max, mx[par][:, p, 1:2]).then_inc(maxed, 1)
            else:
                v.tensor_tensor_reduce(bank[:, 0:w], bank[:, 0:w], mneg[par][:, k0:k0 + w], 1.0, -3e38,
                                       ALU.add, ALU.max, mx[par][:, p, c + 1:c + 2]).then_inc(maxed, 1)

    def dve_add_near(v, b, t):
        v.wait_ge(s_full, SB * b + (1 if t == 0 else t + 2))
        o = psS[:, buf(t), :]
        v.tensor_tensor(o, o, s["dT"][:, t, :], ALU.add).then_inc(added, 1)

    def dve_add(v, b, t):
        kw = KTILES[t][1]
        if t == 0:
            v.wait_ge(s_read, SB * b + 1)
        if t < 2:
            v.wait_ge(added, 15 * b + 2 * t + 1)
        else:
            v.wait_ge(s_full, SB * b + t + 2)
        o = psS[0:kw, buf(t), :]
        v.tensor_tensor(o, o, shift[0:kw, :], ALU.add).then_inc(added, 1)

    def dve_step(v, j, par, prep, main, fin, ahead, tile):
        f, b = j - 2, j - 1
        if fin:
            v.wait_ge(pv_done, NKT * (f + 1))
            v.tensor_copy(oT[:, :], psO[:, 0:DM]).then_inc(o_out, 1)
        for c in range(NC):
            for i, t in enumerate(CHUNKS[c]):
                if t == 0 and main:
                    dve_add_near(v, b, t)
                if t == 0 and fin:
                    v.wait_ge(d_full, f + 1)
                    v.reciprocal(oR[:, :], psO[:, 256:512]).then_inc(o_step, 1)
                    v.wait_ge(o_step, 2 * f + 1)
                    v.tensor_tensor(oN[:, :], oT[:, :], oR[:, :], ALU.mult).then_inc(o_step, 1)
                if prep and t == 0:
                    dve_use(v, j, par, c, 0)
                if main and t == 1:
                    dve_add_near(v, b, t)
                if main:
                    dve_add(v, b, t)
                if prep and t == 0:
                    for u in slot(c, i)[1:]:
                        dve_use(v, j, par, c, u)
                if t == 0 and fin:
                    v.wait_ge(y_full, f + 1)
                    v.tensor_tensor(x1[tok_rows(par), tile, :], psO[tok_rows(par), 256:512],
                                    x1[tok_rows(par), tile, :], ALU.add).then_inc(y_out, 1)
                    if par == 1:
                        v.wait_ge(y_out, f + 1)
                        v.bn_stats(s["stats1"][:, bass.ds(tile, 1), :].rearrange("p a f -> p (a f)"),
                                   x1[:, bass.ds(tile, 1), :].rearrange("p a f -> p (a f)")).then_inc(rows_done, 1)
                if prep and t:
                    for u in slot(c, i):
                        dve_use(v, j, par, c, u)
        if prep:
            k = 5 * j
            v.wait_ge(maxed, 32 * (j + 1))
            v.tensor_reduce(cm[:, :], mx[par][:, :, :], AX.X, ALU.max).then_inc(c_step, 1)
            v.wait_ge(c_step, k + 1)
            v.tensor_scalar(cm[:, :], cm[:, :], -1.0, None, ALU.mult).then_inc(c_step, 1)
            v.wait_ge(c_step, k + 2)
            v.tensor_copy(cv[par][:, :, 0], cm[:, :]).then_inc(c_step, 1)
            v.wait_ge(c_step, k + 3)
            v.tensor_tensor(cr[:, :], cm[:, :], cv[par][:, :, 0], ALU.subtract).then_inc(c_step, 1)
            v.wait_ge(c_step, k + 4)
            v.tensor_copy(cv[par][:, :, 1], cr[:, :]).then_inc(c_step, 1)

    def pool_split(pool, j, c):
        n = j * NC + c
        w = width(c)
        at_least(pool, work_full, NU * (n - 2) + LAST_KV)
        pool.wait_ge(ctx_hi, n + 1)
        pool.tensor_tensor(cL[:, c % 2, :, 0:w], ctx[:, c % 2, :, 0:w], cH[:, c % 2, :, 0:w].bitcast(F32), ALU.subtract)\
            .then_inc(ctx_lo, 1)

    def pool_mask(pool, j, par, half):
        if not (isinstance(j, int) and j == 0):
            pool.wait_ge(maxed, 32 * (j - 1) + 8)
        wait_apart(pool, mask_in[par], 16 * (half + 1))
        pool.tensor_scalar(mneg[par][:, :], m8[par][:, :], -1.0, NEG, ALU.add, ALU.mult).then_inc(mneg_ready, 1)
        pool.wait_ge(mneg_ready, j + 1)
        pool.tensor_tensor(near[:, :, :], s["dN"][:, :, :],
                           mneg[par][:, 0:NEAR].unsqueeze(1).to_broadcast([P, H // 2, NEAR]), ALU.add).then_inc(near_ready, 1)
        if not (isinstance(j, int) and j == 0):
            pool.wait_ge(q_ready, 2 * j)
        for g in range(HG):
            op = pool.tensor_tensor(qb[:, g, :].rearrange("p (h q) -> p h q", h=4),
                                    s["qD"][:, g, bass.ds(j * TQ, TQ)].unsqueeze(1).to_broadcast([P, 4, TQ]),
                                    s["head_rows"][:, :].unsqueeze(2).to_broadcast([P, 4, TQ]), ALU.mult)
        op.then_inc(qb_ready, 1)

    def pool_step(pool, j, par, ahead, half):
        late = not (isinstance(j, int) and j < 2)
        if isinstance(j, int) and j == 0:
            pool_split(pool, 0, 0)
            pool_mask(pool, 0, 0, 0)
        if late:
            wait_apart(pool, s_full, SB * (j - 1))
        wait_apart(pool, qb_ready, j + 1)
        pool.tensor_copy(qh[par][:, :, :], qb[:, :, :]).then_inc(q_ready, 1)
        pool.wait_ge(q_ready, 2 * j + 1)
        pool.tensor_tensor(ql[par][:, :, :], qb[:, :, :], qh[par][:, :, :].bitcast(F32), ALU.subtract).then_inc(q_ready, 1)
        if late:
            wait_apart(pool, s_read, SB * (j - 1))
        pool.tensor_copy(mc[par][:, :, :, :], s["mcols"][:, :, :, bass.ds(j, 1)]).then_inc(mc_ready, 1)
        for c in range(NC):
            if c == 2 and ahead:
                pool_mask(pool, j + 1, 1 - par, half if isinstance(par, int) and par == 0 else half + 1)
            if c < NC - 1 or ahead:
                pool_split(pool, j if c < NC - 1 else j + 1, (c + 1) % NC)

    ctx_view = d["ctxT"].rearrange("b (k p) t -> b p k t", p=P)

    def sp_mask(sp, j, par):
        sp.dma_start(m8[par][:, :], d["mask"][bass.ds(j, 1), :].to_broadcast([P, TK])).then_inc(mask_in[par], 16)

    def sp_step(sp, j, par, ahead):
        if isinstance(j, int) and j == 0:
            sp_mask(sp, 0, 0)
        for c in range(NC):
            k0, w = CSPAN[c]
            at_least(sp, ctx_lo, j * NC + c - 1)
            sp.dma_start(ctx[:, c % 2, :, 0:w], ctx_view[bass.ds(j, 1), :, :, k0:k0 + w].rearrange("b p k t -> (b p) k t"))\
              .then_inc(ctx_in[c], 16)
            if c == 0 and ahead:
                at_least(sp, mneg_ready, j)
                sp_mask(sp, j + 1, 1 - par)

    def run(eng, step):
        step(eng, 0, 0, 0)
        step(eng, 1, 1, 0)
        with eng.Fori(0, B // 2 - 2) as i:
            step(eng, 2 * i + 2, 0, i + 1)
            step(eng, 2 * i + 3, 1, i + 1)
        for j in range(B - 2, B + 2):
            step(eng, j, j % 2, j // 2)

    def parts(j):
        if not isinstance(j, int):
            return True, True, True, True
        return j < B, 1 <= j <= B, j >= 2, j < B - 1

    with nc.Block() as block:
        @block.sync
        def _(sp):
            run(sp, lambda e, j, par, half: parts(j)[0] and sp_step(e, j, par, parts(j)[3]))

        @block.gpsimd
        def _(pool):
            run(pool, lambda e, j, par, half: parts(j)[0] and pool_step(e, j, par, parts(j)[3], half))

        @block.scalar
        def _(act):
            run(act, lambda e, j, par, half: act_step(e, j, par, *parts(j)))

        @block.vector
        def _(v):
            run(v, lambda e, j, par, half: dve_step(e, j, par, *parts(j), half - 1))

        @block.tensor
        def _(pe):
            run(pe, lambda e, j, par, half: pe_step(e, j, par, *parts(j)))


def norm_finish(nc, stats, mv, rstd, sem, tag):
    step = sem(f"{tag}_norm_step")
    root = sem(f"{tag}_norm_root")
    with nc.Block() as block:
        @block.vector
        def _(v):
            for n in range(NT):
                v.bn_aggr(mv[:, n, :], stats[:, n, :]).then_inc(step, 1)
            v.wait_ge(step, NT)
            v.tensor_scalar(rstd[:, :], mv[:, :, 1], EPS, None, ALU.add).then_inc(step, 1)
            v.wait_ge(root, 1)
            v.reciprocal(rstd[:, :], rstd[:, :]).then_inc(step, 1)

        @block.scalar
        def _(act):
            act.wait_ge(step, NT + 1)
            act.activation(rstd[:, :], rstd[:, :], ACT.Sqrt).then_inc(root, 1)


def known(i, least):
    return not isinstance(i, int) or i >= least


def self_attention(nc, d, s, sb, ps, sem):
    x1, x2, ident = s["x1"], s["x2"], s["ident"]
    psP = ps("a_ps", [P, 8, 512])
    mv = sb("a_mv", [P, NT, 2], F32)
    rstd = sb("a_rstd", [P, NT], F32)
    norm_finish(nc, s["stats1"], mv, rstd, sem, "a")
    PAIRS = H // 2
    xn = sb("a_xn", [P, NT, DM], F32)
    xs = sb("a_xs", [P, KT, TOK], F32)
    qT = sb("a_qT", [P, KT, TOK], F32)
    kT = sb("a_kT", [P, KT, TOK], F32)
    Vc = sb("a_Vc", [P, NT, 2, P], F32)
    VB = sb("a_VB", [P, 2, 2, PAIRS, 2 * DK], F32)
    w, wproj = s["wattn"], s["wproj"]

    zeroed = sem("a_zeroed")
    xn_ready = sem("a_xn")
    x_turned = sem("a_x_turned")
    xs_act, xs_dve = sem("a_xs_act"), sem("a_xs_dve")
    qk_full = sem("a_qk_full")
    q_out, k_out = sem("a_q_out"), sem("a_k_out")
    v_full = sem("a_v_full")
    v_act, v_dve = sem("a_v_act"), sem("a_v_dve")

    with nc.Block() as block:
        @block.gpsimd
        def _(pool):
            pool.memset(VB[:, :, :, :, :], 0.0).then_inc(zeroed, 1)

        @block.vector
        def _(v):
            for n in range(NT):
                v.tensor_scalar(xn[:, n, :], x1[:, n, :], mv[:, n, 0:1], rstd[:, n:n + 1], ALU.subtract, ALU.mult)\
                 .then_inc(xn_ready, 1)
            for i in (1, 3):
                v.wait_ge(x_turned, i + 1)
                v.tensor_copy(xs[:, i // 2, 512:1024], psP[:, i, :]).then_inc(xs_dve, 1)
            for i in range(4):
                v.wait_ge(qk_full, 4 + i + 1)
                v.tensor_copy(kT[:, i // 2, 512 * (i % 2):512 * (i % 2) + 512], psP[:, i, :]).then_inc(k_out, 1)
            for n in range(1, NT, 2):
                v.wait_ge(v_full, n + 1)
                v.tensor_copy(Vc[:, n, :, :].rearrange("p b f -> p (b f)"), psP[:, (4 + n) % 8, 0:DM]).then_inc(v_dve, 1)

        @block.scalar
        def _(act):
            for i in (0, 2):
                act.wait_ge(x_turned, i + 1)
                act.activation(xs[:, i // 2, 0:512], psP[:, i, :], ACT.Copy).then_inc(xs_act, 1)
            for i in range(4):
                act.wait_ge(qk_full, i + 1)
                act.activation(qT[:, i // 2, 512 * (i % 2):512 * (i % 2) + 512], psP[:, 4 + i, :], ACT.Copy).then_inc(q_out, 1)
            for n in range(0, NT, 2):
                act.wait_ge(v_full, n + 1)
                act.activation(Vc[:, n, :, :].rearrange("p b f -> p (b f)"), psP[:, (4 + n) % 8, 0:DM], ACT.Copy).then_inc(v_act, 1)

        @block.tensor
        def _(pe):
            for i in range(4):
                for n in range(4):
                    t = 4 * (i % 2) + n
                    if i < 2:
                        pe.wait_ge(xn_ready, t + 1)
                    mm = pe.transpose(psP[:, i, n * P:n * P + P], xn[:, t, (i // 2) * P:(i // 2) * P + P], ident[:, :])
                mm.then_inc(x_turned, 1)
            pe.wait_ge(s["attn_loads"], s["attn_loads_total"])
            pe.wait_ge(xs_act, 2)
            pe.wait_ge(xs_dve, 2)
            for g in range(8):
                f0, c = (g // 2) * P, slice(512 * (g % 2), 512 * (g % 2) + 512)
                for k in range(KT):
                    mm = pe.matmul(psP[:, (4 + g) % 8, :], w[:, k, f0:f0 + P], xs[:, k, c], start=(k == 0), stop=(k == KT - 1))
                mm.then_inc(qk_full, 1)
            for n in range(NT):
                if n < 4:
                    pe.wait_ge(q_out, n + 1)
                else:
                    pe.wait_ge(k_out, n - 3)
                for b in range(2):
                    for r in range(2):
                        for k in range(KT):
                            mm = pe.matmul(psP[tok_rows(r), (4 + n) % 8, b * P:b * P + P], xs[:, k, n * P + b * TQ:n * P + b * TQ + TQ],
                                           w[:, k, 2 * DM + r * P:2 * DM + r * P + P], start=(k == 0), stop=(k == KT - 1),
                                           skip_group_check=True)
                mm.then_inc(v_full, 1)

    psA = psP[:, 0:2, :].rearrange("p a c -> p (a c)")
    psT, psO, psY = psP[:, 2:4, :], psP[:, 4, 0:2 * P], psP[:, 5, 0:DM]
    qs = sb("a_qs", [P, 2, KT, P], F32)
    kbd = [sb(f"a_kbd{i}", [P, 2, KT, 512], F32) for i in range(2)]
    E = sb("a_E", [P, 2, H, TQ], F32)
    mx = sb("a_mx", [P, H], F32)
    rs = sb("a_rs", [P, 2, H], F32)
    pT = sb("a_pT", [P, 2, PAIRS, P], F32)
    oT = sb("a_oT", [P, 2, KT, P], F32)
    kbd_ready = sem("a_kbd_ready")
    qs_ready = sem("a_qs")
    vb_ready = sem("a_vb")
    s_full = sem("a_s_full")
    e_step = sem("a_e_step")
    p_ready = sem("a_p")
    r_step = sem("a_r_step")
    n_ready = sem("a_n")
    t_full = sem("a_t_full")
    t_out = sem("a_t_out")
    o_full = sem("a_o_full")
    o_out = sem("a_o_out")
    y_full = sem("a_y_full")
    y_out = sem("a_y_out")

    def run(eng, step):
        step(0, 0)
        step(1, 1)
        with eng.Fori(0, NT // 2 - 2) as i:
            step(2 * i + 2, 0)
            step(2 * i + 3, 1)
        for n in range(NT - 2, NT + 2):
            step(n, n % 2)

    def has(n, back):
        return not isinstance(n, int) or 0 <= n - back < NT

    def row(a, n):
        return a[:, bass.ds(n, 1), :].rearrange("p a f -> p (a f)")

    with nc.Block() as block:
        @block.gpsimd
        def _(pool):
            def keys(n, r):
                if known(n, 2):
                    pool.wait_ge(s_full, n - 1)
                for b in range(2):
                    for m in range(KT):
                        op = pool.tensor_tensor(kbd[r][:, b, m, :].rearrange("p (h k) -> p h k", h=HT),
                                                kT[:, m, bass.ds(n * P + b * TQ, TQ)].unsqueeze(1).to_broadcast([P, HT, TQ]),
                                                s["head_rows2"][:, :].unsqueeze(2).to_broadcast([P, HT, TQ]), ALU.mult)
                op.then_inc(kbd_ready, 1)

            def step(n, r):
                if has(n, 1):
                    pool.wait_ge(r_step, 2 * n)
                    e = E[:, 1 - r, :, :]
                    pool.tensor_tensor(e, e, rs[:, 1 - r, :].unsqueeze(2).to_broadcast([P, H, TQ]), ALU.mult).then_inc(n_ready, 1)
                if has(n, -1):
                    keys(n + 1, 1 - r)
            keys(0, 0)
            run(pool, step)

        @block.vector
        def _(v):
            def step(n, r):
                if has(n, 1):
                    v.wait_ge(p_ready, n)
                    v.tensor_reduce(rs[:, 1 - r, :], E[:, 1 - r, :, :], AX.X, ALU.add).then_inc(r_step, 1)
                    v.wait_ge(r_step, 2 * n - 1)
                    v.reciprocal(rs[:, 1 - r, :], rs[:, 1 - r, :]).then_inc(r_step, 1)
                if has(n, 0):
                    v.wait_ge(s_full, n + 1)
                    if known(n, 2):
                        v.wait_ge(t_full, 2 * n - 2)
                    v.scalar_tensor_tensor(out=E[:, r, :, :].rearrange("p h k -> p (h k)"), in0=psA, scalar=DK ** -0.5,
                                           in1=s["alibi"][:, :], op0=ALU.mult, op1=ALU.add).then_inc(e_step, 1)
                    v.wait_ge(e_step, 3 * n + 1)
                    v.tensor_reduce(mx[:, :], E[:, r, :, :], AX.X, ALU.max).then_inc(e_step, 1)
                    v.wait_ge(e_step, 3 * n + 2)
                    v.tensor_tensor(E[:, r, :, :], E[:, r, :, :], mx[:, :].unsqueeze(2).to_broadcast([P, H, TQ]), ALU.subtract)\
                     .then_inc(e_step, 1)
                if has(n, 2):
                    v.wait_ge(y_full, n - 1)
                    v.tensor_tensor(row(x2, n - 2), psY, row(x1, n - 2), ALU.add).then_inc(y_out, 1)
                    v.wait_ge(y_out, n)
                    v.bn_stats(row(s["stats2"], n - 2), row(x2, n - 2))
            v.wait_ge(s["attn_loads"], s["attn_loads_total"])
            v.sem_inc(y_out, 1)
            run(v, step)

        @block.scalar
        def _(act):
            def queries(n, r):
                if known(n, 2):
                    act.wait_ge(s_full, n - 1)
                act.activation(qs[:, r, :, :], qT[:, :, bass.ds(n * P, P)], ACT.Copy).then_inc(qs_ready, 1)

            def step(n, r):
                if has(n, -1):
                    queries(n + 1, 1 - r)
                if has(n, 0):
                    if known(n, 2):
                        act.wait_ge(o_full, n - 1)
                    for h in range(2):
                        act.activation(VB[tok_rows(h), r, :, :, h * DK:h * DK + DK],
                                       Vc[tok_rows(h), bass.ds(n, 1), :, :].rearrange("p a b (g e) -> p (a b) g e", e=DK),
                                       ACT.Copy).then_inc(vb_ready, 1)
                if has(n, 2):
                    act.wait_ge(o_full, n - 1)
                    act.activation(oT[:, r, :, :].rearrange("p m q -> p (m q)"), psO, ACT.Copy).then_inc(o_out, 1)
                if has(n, 1):
                    for i in range(2):
                        act.wait_ge(t_full, 2 * n - 1 + i)
                        act.activation(pT[:, 1 - r, 4 * i:4 * i + 4, :].rearrange("p g q -> p (g q)"), psT[:, i, :], ACT.Copy)\
                           .then_inc(t_out, 1)
                if has(n, 0):
                    act.wait_ge(e_step, 3 * n + 3)
                    e = E[:, r, :, :].rearrange("p h k -> p (h k)")
                    act.activation(e, e, ACT.Exp).then_inc(p_ready, 1)
            act.wait_ge(zeroed, 1)
            queries(0, 0)
            run(act, step)

        @block.tensor
        def _(pe):
            def step(n, r):
                if has(n, 0):
                    pe.wait_ge(kbd_ready, n + 1)
                    pe.wait_ge(qs_ready, n + 1)
                    if known(n, 1):
                        pe.wait_ge(e_step, 3 * n - 2)
                    for b in range(2):
                        for m in range(KT):
                            mm = pe.matmul(psA[tok_rows(b), m * 512:m * 512 + 512], qs[:, r, m, b * TQ:b * TQ + TQ],
                                           kbd[r][:, b, m, :], start=True, stop=True, skip_group_check=True)
                    mm.then_inc(s_full, 1)
                if has(n, 2):
                    pe.wait_ge(t_out, 2 * n - 2)
                    pe.wait_ge(vb_ready, 2 * n - 2)
                    for b in range(2):
                        for p in range(PAIRS):
                            row0 = 2 * DK * (p % 4)
                            c = (p // 4) * P + b * TQ
                            mm = pe.matmul(psO[row0:row0 + 2 * DK, c:c + TQ], VB[:, r, b, p, :], pT[:, r, p, b * TQ:b * TQ + TQ],
                                           start=True, stop=True, skip_group_check=True)
                    mm.then_inc(o_full, 1)
                if has(n, 1):
                    pe.wait_ge(n_ready, n)
                    for i in range(2):
                        if known(n, 2):
                            pe.wait_ge(t_out, 2 * n - 3 + i)
                        for p in range(4 * i, 4 * i + 4):
                            mm = pe.transpose(psT[:, i, (p % 4) * P:(p % 4) * P + P],
                                              E[:, 1 - r, 2 * p:2 * p + 2, :].rearrange("p h k -> p (h k)"), ident[:, :])
                        mm.then_inc(t_full, 1)
                if has(n, 2):
                    pe.wait_ge(o_out, n - 1)
                    pe.wait_ge(y_out, n - 1)
                    for m in range(KT):
                        mm = pe.matmul(psY, oT[:, r, m, :], wproj[:, m, :], start=(m == 0), stop=(m == KT - 1))
                    mm.then_inc(y_full, 1)
            run(pe, step)


def load_experts(sp, d, s, h, par):
    sp.dma_start(s["vraw"][par][:, :, :], d["vw"].rearrange("(k p) h f -> p k h f", p=P)[:, :, bass.ds(h, 1), :]
                 .rearrange("p k a f -> p (k a) f")).then_inc(s["v_in"][par], 16)
    sp.dma_start(s["oraw"][par][:, :], d["ow"][bass.ds(h, 1), :, :].rearrange("a p f -> (a p) f")).then_inc(s["o_in"][par], 16)


def switch_head(nc, d, s, sb, ps, sem):
    x, ident = s["x2"], s["ident"]
    psV = ps("f_psV", [P, 4, 512])
    psU = ps("f_psU", [P, 2, 512])
    psC = ps("f_psC", [P, 2, 512])
    bankU = [psU[:, 0, :], psU[:, 1, :], psC[:, 0, :]]
    bankC = psC[:, 1, 0:P]
    mv = sb("f_mv", [P, NT, 2], F32)
    rstd = sb("f_rstd", [P, NT], F32)
    norm_finish(nc, s["stats2"], mv, rstd, sem, "f")
    pT = sb("f_pT", [P, FH, NT, P], F32)
    xH = sb("f_xH", [P, KT, TOK], F32R)
    xL = sb("f_xL", [P, KT, TOK], F32R)
    NG = 2 * NT * 2
    gate = sb("f_gate", [P, FH, NT, 2, FE], F32)
    qkw, sel = s["qkw"], s["sel"]
    SCALE = 1.0 / math.sqrt(FP)

    vH, vL = [[sb(f"f_v{n}0", [P, KT, FE * FP], F32R)] for n in "HL"]
    oH, oL = [[sb(f"f_o{n}0", [P, FE * DM], F32R)] for n in "HL"]
    whi_v, whi_o = sem("f_whi_v"), sem("f_whi_o")
    wlo_v, wlo_o = sem("f_wlo_v"), sem("f_wlo_o")

    def piece(kind, par, q):
        if kind == "v":
            k, c = q // 2, slice(512 * (q % 2), 512 * (q % 2) + 512)
            return vH[par][:, k, c], vL[par][:, k, c], s["vraw"][par][:, k, c]
        c = slice(512 * q, 512 * q + 512)
        return oH[par][:, c], oL[par][:, c], s["oraw"][par][:, c]

    def act_cut(act, h, par, kind, q):
        if q == 0:
            act.wait_ge(s[f"{kind}_in"][par], 16 * (h // 2 + 1) if isinstance(h, int) else 8 * (h - par) + 16)
            if not (isinstance(h, int) and h < 2):
                act.wait_ge({"v": v_full, "o": u_full}[kind], {"v": 16, "o": 32}[kind] * (h - 1))
        hi, lo, raw = piece(kind, par, q)
        act.activation(hi, raw, ACT.Copy).then_inc({"v": whi_v, "o": whi_o}[kind], 1)

    def pool_cut(pool, h, par, kind, q):
        pool.wait_ge({"v": whi_v, "o": whi_o}[kind], 4 * h + q + 1)
        hi, lo, raw = piece(kind, par, q)
        pool.tensor_tensor(lo, raw, hi.bitcast(F32), ALU.subtract).then_inc({"v": wlo_v, "o": wlo_o}[kind], 1)

    xn_ready = sem("f_xn")
    x_turned = sem("f_x_turned")
    xs_ready = sem("f_xs_ready")
    xh_ready = sem("f_xh")
    xl_ready = sem("f_xl")
    l_full = sem("f_l_full")
    l_exp = sem("f_l_exp")
    zeroed = sem("f_zeroed")
    qkw_hi = sem("f_qkw_hi")
    qkw_lo = sem("f_qkw_lo")
    qk_full = sem("f_qk_full")
    qk_out = sem("f_qk_out")
    s_full = sem("f_s_full")
    e_step = sem("f_e_step")
    p_ready = sem("f_p")
    den_read = sem("f_den_read")
    g_step = sem("f_g_step")
    t_full = sem("f_t_full")
    t_out = sem("f_t_out")
    GS = 22

    with ExitStack() as first:
        def sbf(name, shape, dt=F32):
            return first.enter_context(nc.sbuf_tensor(name, shape, dt))
        xn = sbf("f_xn_rows", [P, NT, DM])
        xs = sbf("f_xs", [P, KT, TOK])
        wH = [sbf(f"f_qkH{i}", [P, KT, 2 * FP], F32R) for i in range(2)]
        wL = [sbf(f"f_qkL{i}", [P, KT, 2 * FP], F32R) for i in range(2)]
        qkT = sbf("f_qkT", [P, 2, TOK])
        E = sbf("f_E", [P, NT, TQ])
        pf = [sbf(f"f_pf{i}", [P, NT, P]) for i in range(2)]
        mx = sbf("f_mx", [P, NT])
        rden = sbf("f_rden", [P, 2 * NT])
        lex = sbf("f_lex", [P, FH, NT, 2 * FE])
        ex, pr, eq, one1, one2 = [sbf(f"f_g{n}", [P, NG, FE]) for n in ("ex", "pr", "eq", "one1", "one2")]
        top1, top2, pick, tot = [sbf(f"f_g{n}", [P, NG]) for n in ("top1", "top2", "pick", "tot")]

        def bc(a):
            return a[:, :].unsqueeze(2).to_broadcast([P, NG, FE])

        def flat(a):
            return a.rearrange("p g e -> p (g e)")

        with nc.Block() as block:
            @block.gpsimd
            def _(pool):
                for i in range(2):
                    pool.memset(pf[i][:, :, :], 0.0).then_inc(zeroed, 1)

                def weights(h, par):
                    pool.wait_ge(qkw_hi, h + 1)
                    pool.tensor_tensor(wL[par][:, :, :], qkw[:, :, bass.ds(h, 1), :].rearrange("p k a f -> p (k a) f"),
                                       wH[par][:, :, :].bitcast(F32), ALU.subtract).then_inc(qkw_lo, 1)
                for i in range(4):
                    k, c = i // 2, slice(512 * (i % 2), 512 * (i % 2) + 512)
                    pool.wait_ge(xh_ready, i + 1)
                    pool.tensor_tensor(xL[:, k, c], xs[:, k, c], xH[:, k, c].bitcast(F32), ALU.subtract).then_inc(xl_ready, 1)
                weights(0, 0)
                weights(1, 1)
                for q in range(4):
                    pool_cut(pool, 0, 0, "v", q)
                with pool.Fori(0, FH // 2 - 1) as i:
                    weights(2 * i + 2, 0)
                    weights(2 * i + 3, 1)
                for q in range(4):
                    pool_cut(pool, 0, 0, "o", q)

            @block.vector
            def _(v):
                for n in range(NT):
                    v.tensor_scalar(xn[:, n, :], x[:, n, :], mv[:, n, 0:1], rstd[:, n:n + 1], ALU.subtract, ALU.mult)\
                     .then_inc(xn_ready, 1)
                v.wait_ge(s["ffn_loads"], s["ffn_loads_total"])
                v.wait_ge(l_exp, NT)

                def softmax(h, par):
                    v.wait_ge(s_full, h + 1)
                    sc = psC[:, par, :].rearrange("p (n k) -> p n k", n=NT)
                    v.tensor_reduce(mx[:, :], sc, AX.X, ALU.max).then_inc(e_step, 1)
                    v.wait_ge(e_step, 2 * h + 1)
                    v.tensor_tensor(E[:, :, :], sc, mx[:, :].unsqueeze(2).to_broadcast([P, NT, TQ]), ALU.subtract)\
                     .then_inc(e_step, 1)

                def denominators(h, par):
                    v.wait_ge(p_ready, 2 * h + 2)
                    v.tensor_reduce(rden[:, NT * par:NT * par + NT], pf[par][:, :, :], AX.X, ALU.add).then_inc(den_read, 1)

                def gates(i, part):
                    count = [0 if part == 0 else 9]

                    def step(op):
                        count[0] += 1
                        op.then_inc(g_step, 1)
                        v.wait_ge(g_step, GS * i + count[0])
                    rank = s["rank"][:, :].unsqueeze(1).to_broadcast([P, NG, FE])
                    if part == 0:
                        step(v.tensor_scalar(flat(ex), lex[:, bass.ds(2 * i, 2), :, :].rearrange("p a n e -> p (a n e)"),
                                             1.0, None, ALU.add))
                        step(v.reciprocal(pr[:, :, :], ex[:, :, :]))
                        step(v.tensor_reduce(top1[:, :], pr[:, :, :], AX.X, ALU.max))
                        step(v.tensor_tensor(eq[:, :, :], pr[:, :, :], bc(top1), ALU.is_equal))
                        step(v.tensor_tensor(eq[:, :, :], eq[:, :, :], rank, ALU.mult))
                        step(v.tensor_reduce(pick[:, :], eq[:, :, :], AX.X, ALU.max))
                        step(v.tensor_tensor(one1[:, :, :], bc(pick), rank, ALU.is_equal))
                        step(v.scalar_tensor_tensor(out=flat(ex), in0=flat(one1), scalar=-2.0, in1=flat(pr),
                                                    op0=ALU.mult, op1=ALU.add))
                        step(v.tensor_reduce(top2[:, :], ex[:, :, :], AX.X, ALU.max))
                        return
                    step(v.tensor_tensor(eq[:, :, :], ex[:, :, :], bc(top2), ALU.is_equal))
                    step(v.tensor_tensor(eq[:, :, :], eq[:, :, :], rank, ALU.mult))
                    step(v.tensor_reduce(pick[:, :], eq[:, :, :], AX.X, ALU.max))
                    step(v.tensor_tensor(one2[:, :, :], bc(pick), rank, ALU.is_equal))
                    step(v.tensor_tensor(tot[:, :], top1[:, :], top2[:, :], ALU.add))
                    step(v.tensor_scalar(tot[:, :], tot[:, :], 1e-9, None, ALU.max))
                    step(v.reciprocal(tot[:, :], tot[:, :]))
                    step(v.tensor_scalar(tot[:, :], tot[:, :], s["route"][:, 0:1], None, ALU.mult))
                    step(v.tensor_tensor(eq[:, :, :], one1[:, :, :], one2[:, :, :], ALU.add))
                    step(v.tensor_tensor(eq[:, :, :], eq[:, :, :], pr[:, :, :], ALU.mult))
                    denominators(2 * i + 1, 1)
                    v.wait_ge(den_read, 2 * i + 2)
                    step(v.reciprocal(rden[:, :], rden[:, :]))
                    o_tot = tot.rearrange("p (n w) -> p n w", w=2)[:, :, 1]
                    step(v.tensor_tensor(o_tot, o_tot, rden[:, :], ALU.mult))
                    step(v.tensor_tensor(gate[:, bass.ds(2 * i, 2), :, :, :].rearrange("p a n w e -> p (a n w) e"), eq[:, :, :],
                                         bc(tot), ALU.mult))
                    assert count[0] == GS
                with v.Fori(0, FH // 2) as i:
                    softmax(2 * i, 0)
                    gates(i, 0)
                    denominators(2 * i, 0)
                    softmax(2 * i + 1, 1)
                    gates(i, 1)

            @block.scalar
            def _(act):
                act.wait_ge(s["ffn_loads"], s["ffn_loads_total"])

                def weights(h, par):
                    if not (isinstance(h, int) and h < 2):
                        act.wait_ge(qk_full, 4 * (h - 1))
                    act.activation(wH[par][:, :, :], qkw[:, :, bass.ds(h, 1), :].rearrange("p k a f -> p (k a) f"), ACT.Copy)\
                       .then_inc(qkw_hi, 1)
                weights(0, 0)
                for i in range(4):
                    k, c = i // 2, slice(512 * (i % 2), 512 * (i % 2) + 512)
                    act.wait_ge(x_turned, i + 1)
                    act.activation(xs[:, k, c], psV[:, i, :], ACT.Copy).then_inc(xs_ready, 1)
                    act.wait_ge(xs_ready, i + 1)
                    act.activation(xH[:, k, c], xs[:, k, c], ACT.Copy).then_inc(xh_ready, 1)
                for n in range(NT):
                    if n % 4 == 0:
                        act.wait_ge(l_full, n // 4 + 1)
                    act.activation(lex[:, :, n, :], psC[:, n // 4, (n % 4) * P:(n % 4) * P + P]
                                   .rearrange("p (h e) -> p h e", h=FH), ACT.Exp, scale=-1.0).then_inc(l_exp, 1)
                act.wait_ge(zeroed, 2)

                def heads(h, par, begun, more):
                    for i in range(4):
                        if i == 1 and begun:
                            act.wait_ge(e_step, 2 * h)
                            if not (isinstance(h, int) and h < 3):
                                act.wait_ge(t_full, 2 * (h - 2))
                                act.wait_ge(den_read, h - 2)
                            for b in range(2):
                                act.activation(pf[1 - par][tok_rows(b), :, b * TQ:b * TQ + TQ], E[tok_rows(b), :, :], ACT.Exp,
                                               scale=SCALE).then_inc(p_ready, 1)
                        if more is None:
                            continue
                        act.wait_ge(qk_full, 4 * h + i + 1)
                        if i == 0 and begun:
                            act.wait_ge(s_full, h)
                        act.activation(qkT[:, i // 2, 512 * (i % 2):512 * (i % 2) + 512], psV[:, i, :], ACT.Copy).then_inc(qk_out, 1)
                        if i == 0 and more:
                            weights(h + 1, 1 - par)
                    if begun:
                        for i in range(2):
                            act.wait_ge(t_full, 2 * (h - 1) + i + 1)
                            act.activation(pT[:, bass.ds(h - 1, 1), 4 * i:4 * i + 4, :].rearrange("p a n q -> p (a n q)"),
                                           psU[:, i, :], ACT.Copy).then_inc(t_out, 1)
                heads(0, 0, False, True)
                act_cut(act, 0, 0, "v", 0)
                act_cut(act, 0, 0, "v", 1)
                heads(1, 1, True, True)
                act_cut(act, 0, 0, "v", 2)
                act_cut(act, 0, 0, "v", 3)
                with act.Fori(0, FH // 2 - 2) as i:
                    heads(2 * i + 2, 0, True, True)
                    heads(2 * i + 3, 1, True, True)
                heads(FH - 2, 0, True, True)
                act_cut(act, 0, 0, "o", 0)
                act_cut(act, 0, 0, "o", 1)
                heads(FH - 1, 1, True, False)
                act_cut(act, 0, 0, "o", 2)
                act_cut(act, 0, 0, "o", 3)
                heads(FH, 0, True, None)

            @block.tensor
            def _(pe):
                for i in range(4):
                    for n in range(4):
                        t = 4 * (i % 2) + n
                        if i < 2:
                            pe.wait_ge(xn_ready, t + 1)
                        mm = pe.transpose(psV[:, i, n * P:n * P + P], xn[:, t, (i // 2) * P:(i // 2) * P + P], ident[:, :])
                    mm.then_inc(x_turned, 1)
                pe.wait_ge(s["ffn_loads"], s["ffn_loads_total"])
                pe.wait_ge(xs_ready, 4)
                for n in range(NT):
                    for k in range(KT):
                        mm = pe.matmul(psC[:, n // 4, (n % 4) * P:(n % 4) * P + P], xs[:, k, n * P:n * P + P], sel[:, k, :],
                                       start=(k == 0), stop=(k == KT - 1), skip_group_check=True)
                    if n % 4 == 3:
                        mm.then_inc(l_full, 1)
                pe.wait_ge(xl_ready, 4)

                def queries_keys(h, par):
                    pe.wait_ge(qkw_lo, h + 1)
                    for i in range(4):
                        if not (isinstance(h, int) and h == 0):
                            pe.wait_ge(qk_out, 4 * (h - 1) + i + 1)
                        f, c = slice((i // 2) * FP, (i // 2) * FP + FP), slice(512 * (i % 2), 512 * (i % 2) + 512)
                        prods = [(a, b, k) for k in range(KT) for a, b in ((wH, xH), (wH, xL), (wL, xH))]
                        for q, (a, b, k) in enumerate(prods):
                            mm = pe.matmul(psV[:, i, :], a[par][:, k, f], b[:, k, c], start=(q == 0), stop=(q == 5))
                        mm.then_inc(qk_full, 1)

                def turn(h, par):
                    pe.wait_ge(p_ready, 2 * h + 2)
                    for i in range(2):
                        if not (isinstance(h, int) and h == 0):
                            pe.wait_ge(t_out, 2 * (h - 1) + i + 1)
                        for n in range(4):
                            mm = pe.transpose(psU[:, i, n * P:n * P + P], pf[par][:, 4 * i + n, :], ident[:, :])
                        mm.then_inc(t_full, 1)

                def scores(h, par):
                    pe.wait_ge(qk_out, 4 * h + 4)
                    if isinstance(h, int) and h < 2:
                        pe.wait_ge(l_exp, NT)
                    else:
                        pe.wait_ge(e_step, 2 * (h - 1))
                    for n in range(NT):
                        for b in range(2):
                            c = slice(n * P + b * TQ, n * P + b * TQ + TQ)
                            mm = pe.matmul(psC[tok_rows(b), par, n * TQ:n * TQ + TQ], qkT[:, 0, c], qkT[:, 1, c],
                                           start=True, stop=True, skip_group_check=True)
                    mm.then_inc(s_full, 1)

                def head(h, par, begun):
                    queries_keys(h, par)
                    if begun:
                        turn(h - 1, 1 - par)
                    scores(h, par)
                head(0, 0, False)
                head(1, 1, True)
                with pe.Fori(0, FH // 2 - 1) as i:
                    head(2 * i + 2, 0, True)
                    head(2 * i + 3, 1, True)
                turn(FH - 1, 1)

    for n, parts in (("vH", vH), ("vL", vL)):
        parts.append(sb(f"f_{n}1", [P, KT, FE * FP], F32R))
    for n, parts in (("oH", oH), ("oL", oL)):
        parts.append(sb(f"f_{n}1", [P, FE * DM], F32R))
    vh = sb("f_vh", [P, 2, P], F32)
    cf = sb("f_c", [P, 2, P], F32)
    cH = sb("f_cH", [P, 2, P], F32R)
    cL = sb("f_cL", [P, 2, P], F32R)
    part = sb("f_part", [P, 2, 2, DM], F32)
    acc = sb("f_acc", [P, NT, 2, DM], F32)
    v_full = sem("f_v_full")
    v_step = sem("f_v_step")
    c_full = sem("f_c_full")
    c_hi = sem("f_c_hi")
    c_lo = sem("f_c_lo")
    u_full = sem("f_u_full")
    u_step = sem("f_u_step")
    part_ready = sem("f_part_ready")
    acc_step = sem("f_acc_step")
    summed = sem("f_summed")
    PIECES = [[], [("v", 0)], [("v", 1)], [("v", 2)], [("v", 3), ("o", 0)], [("o", 1)], [("o", 2)], [("o", 3)]]
    assert len(PIECES) == NT
    x2 = s["x2"]

    def heads(eng, head):
        head(0, 0, True)
        head(1, 1, True)
        with eng.Fori(0, FH // 2 - 2) as i:
            head(2 * i + 2, 0, True)
            head(2 * i + 3, 1, True)
        head(FH - 2, 0, True)
        head(FH - 1, 1, False)

    def follower(h, par, t):
        return (h, par, t + 1) if t + 1 < NT else (h + 1, 1 - par, 0)

    def gate_of(h, t, w, e):
        return gate[:, bass.ds(h, 1), t, w, e:e + 1].rearrange("p a e -> p (a e)")

    with nc.Block() as block:
        @block.sync
        def _(sp):
            def reload(h, par):
                sp.wait_ge(wlo_v, 4 * (h - 1))
                sp.wait_ge(wlo_o, 4 * (h - 1))
                load_experts(sp, d, s, h, par)
            with sp.Fori(0, FH // 2 - 1) as i:
                reload(2 * i + 2, 0)
                reload(2 * i + 3, 1)

        @block.gpsimd
        def _(pool):
            pool.memset(acc[:, :, :, :], 0.0).then_inc(acc_step, 1)

            def add(i, t, x):
                pool.wait_ge(part_ready, 4 * i + 2 * x + 2)
                pool.wait_ge(acc_step, 2 * i + x + 1)
                pool.tensor_tensor(acc[:, t, :, :], acc[:, t, :, :], part[:, x, :, :], ALU.add).then_inc(acc_step, 1)

            def head(h, par, more):
                for t in range(NT):
                    i, r = NT * h + t, t % 2
                    pool.wait_ge(c_hi, 2 * i + 2)
                    if known(i, 2):
                        pool.wait_ge(u_full, 4 * (i - 1))
                    pool.tensor_tensor(cL[:, r, :], cf[:, r, :], cH[:, r, :].bitcast(F32), ALU.subtract).then_inc(c_lo, 1)
                    if known(i, 1):
                        add(i - 1, (t - 1) % NT, 1)
                    if more:
                        for kind, q in PIECES[t]:
                            pool_cut(pool, h + 1, 1 - par, kind, q)
                    add(i, t, 0)
            heads(pool, head)
            add(NT * FH - 1, NT - 1, 1)

        @block.scalar
        def _(act):
            def head(h, par, more):
                for t in range(NT):
                    i, r = NT * h + t, t % 2
                    act.wait_ge(c_full, i + 1)
                    if known(i, 2):
                        act.wait_ge(u_full, 4 * (i - 1))
                    act.activation(cH[:, r, :], bankC, ACT.Copy).then_inc(c_hi, 1)
                    if known(i, 2):
                        act.wait_ge(c_lo, i - 1)
                    act.activation(cf[:, r, :], bankC, ACT.Copy).then_inc(c_hi, 1)
                    if more:
                        for kind, q in PIECES[t]:
                            act_cut(act, h + 1, 1 - par, kind, q)
                    for x in range(2):
                        k = 2 * x + 1
                        act.wait_ge(u_full, 4 * i + k + 1)
                        if known(i, 1):
                            act.wait_ge(acc_step, 2 * (i - 1) + x + 2)
                        for e in range(2):
                            act.activation(part[:, x, e, :], bankU[k % 3][:, e * DM:e * DM + DM], ACT.Copy,
                                           scale=gate_of(h, t, 1, 2 * k + e)).then_inc(part_ready, 1)
            heads(act, head)

        @block.vector
        def _(v):
            def value(h, t, e):
                i, r = NT * h + t, t % 2
                if e % 4 == 0:
                    v.wait_ge(v_full, 2 * i + e // 4 + 1)
                src = psV[:, 2 * r + e // 4, (e % 4) * FP:(e % 4) * FP + FP]
                if e == 0:
                    if known(i, 2):
                        v.wait_ge(c_full, i - 1)
                    v.tensor_scalar(vh[:, r, :], src, gate_of(h, t, 0, e), None, ALU.mult).then_inc(v_step, 1)
                else:
                    v.wait_ge(v_step, 8 * i + e)
                    v.scalar_tensor_tensor(out=vh[:, r, :], in0=src, scalar=gate_of(h, t, 0, e), in1=vh[:, r, :],
                                           op0=ALU.mult, op1=ALU.add).then_inc(v_step, 1)

            def output(h, t, x, e):
                i = NT * h + t
                if e == 0:
                    v.wait_ge(u_full, 4 * i + 2 * x + 1)
                if known(i, NT) or x or e:
                    v.wait_ge(u_step, 4 * i + 2 * x + e if x or e else 4 * (i - NT + 1))
                v.scalar_tensor_tensor(out=x2[:, t, :], in0=bankU[2 * x % 3][:, e * DM:e * DM + DM],
                                       scalar=gate_of(h, t, 1, 4 * x + e), in1=x2[:, t, :],
                                       op0=ALU.mult, op1=ALU.add).then_inc(u_step, 1)

            def head(h, par, more):
                for t in range(NT):
                    i = NT * h + t
                    nh, npar, nt = follower(h, par, t)
                    go = t + 1 < NT or more
                    before = known(i, 1)
                    bh, bt = (h, t - 1) if t else (h - 1, NT - 1)
                    if go:
                        value(nh, nt, 0)
                    if before:
                        output(bh, bt, 1, 0)
                    if go:
                        value(nh, nt, 1)
                    if before:
                        output(bh, bt, 1, 1)
                    if go:
                        value(nh, nt, 2)
                    output(h, t, 0, 0)
                    if go:
                        value(nh, nt, 3)
                    output(h, t, 0, 1)
                    if go:
                        for e in range(4, FE):
                            value(nh, nt, e)
                    if not more and t >= 2:
                        total(t - 2)

            def total(t):
                i = NT * (FH - 1) + t
                for e in range(2):
                    v.wait_ge(acc_step, 2 * i + 3)
                    v.wait_ge(u_step, 4 * i + 4)
                    if e:
                        v.wait_ge(summed, 2 * t + 1)
                    v.tensor_tensor(x2[:, t, :], x2[:, t, :], acc[:, t, e, :], ALU.add).then_inc(summed, 1)

            for e in range(FE):
                value(0, 0, e)
            heads(v, head)
            for e in range(2):
                output(FH - 1, NT - 1, 1, e)
            total(NT - 2)
            total(NT - 1)

        @block.tensor
        def _(pe):
            def values(h, par, t, x):
                i, r = NT * h + t, t % 2
                if t == 0 and x == 0:
                    pe.wait_ge(wlo_v, 4 * h + 4)
                if known(i, 2):
                    pe.wait_ge(v_step, 8 * (i - 2) + 4 * x + 4)
                prods = [(a, b, k) for k in range(KT) for a, b in ((xH, vH), (xH, vL), (xL, vH))]
                for q, (a, b, k) in enumerate(prods):
                    mm = pe.matmul(psV[:, 2 * r + x, :], a[:, k, t * P:t * P + P], b[par][:, k, 512 * x:512 * x + 512],
                                   start=(q == 0), stop=(q == 5))
                mm.then_inc(v_full, 1)

            def context(h, t):
                i, r = NT * h + t, t % 2
                pe.wait_ge(v_step, 8 * i + 8)
                if known(i, 1):
                    pe.wait_ge(c_hi, 2 * i)
                pe.matmul(bankC, vh[:, r, :], pT[:, bass.ds(h, 1), t, :].rearrange("p a q -> p (a q)"),
                          start=True, stop=True).then_inc(c_full, 1)

            def outputs(h, par, t):
                i = NT * h + t
                pe.wait_ge(c_lo, i + 1)
                if t == 0:
                    pe.wait_ge(wlo_o, 4 * h + 4)
                for k in range(4):
                    if k == 0 and known(i, 1):
                        pe.wait_ge(part_ready, 4 * i)
                    elif k == 1 and known(i, 1):
                        pe.wait_ge(part_ready, 4 * i - 2)
                    elif k == 2 and known(i, 1):
                        pe.wait_ge(u_step, 4 * i)
                    elif k == 3:
                        pe.wait_ge(u_step, 4 * i + 2)
                    for q, (a, b) in enumerate(((cH, oH), (cH, oL), (cL, oH))):
                        mm = pe.matmul(bankU[k % 3], a[:, t % 2, :], b[par][:, 512 * k:512 * k + 512],
                                       start=(q == 0), stop=(q == 2))
                    mm.then_inc(u_full, 1)

            def head(h, par, more):
                for t in range(NT):
                    nh, npar, nt = follower(h, par, t)
                    go = t + 1 < NT or more
                    if go:
                        values(nh, npar, nt, 0)
                    context(h, t)
                    if go:
                        values(nh, npar, nt, 1)
                    outputs(h, par, t)
            values(0, 0, 0, 0)
            values(0, 0, 0, 1)
            heads(pe, head)


def build(nc, d, out, stages=3):
    with ExitStack() as whole:
        def sem(name):
            return whole.enter_context(nc.semaphore(name))
        def keep(name, shape, dt):
            return whole.enter_context(nc.sbuf_tensor(name, shape, dt))
        s = {}
        s["ident"] = keep("ident", [P, P], F32)
        s["x1"] = keep("x1", [P, NT, DM], F32)
        s["stats1"] = keep("stats1", [P, NT, 6], F32)
        s["stats2"] = keep("stats2", [P, NT, 6], F32)
        with ExitStack() as st:
            def sb(name, shape, dt):
                return st.enter_context(nc.sbuf_tensor(name, shape, dt))
            s["psS"] = st.enter_context(nc.psum_tensor("psS", [P, 2, 1024], F32))
            s["psW"] = st.enter_context(nc.psum_tensor("psW", [P, 3, 512], F32))
            s["psO"] = st.enter_context(nc.psum_tensor("psO", [P, 512], F32))
            s["identb"] = sb("identb", [P, P], BF16)
            s["head_rows"] = sb("head_rows", [P, 4], F32)
            s["den_rows"] = sb("den_rows", [P, P], F32)
            s["wH"] = sb("wH", [P, 2, KT, DM], F32R)
            s["wL"] = sb("wL", [P, 2, KT, DM], F32R)
            s["woP"] = sb("woP", [P, 4, DM], F32)
            s["qD"] = sb("qD", [P, 4, TOK], F32)
            s["dT"] = sb("dT", [P, 2, H * TQ], F32)
            s["dN"] = sb("dN", [P, H // 2, NEAR], BF16)
            s["ctx"] = sb("ctx", [P, 2, KT, 512], F32)
            s["mcols"] = sb("mcols", [P, 2, NKT, B], F32)
            s["V"] = [sb(f"V{i}", [P, NKT, H, DK + 1], F32) for i in range(2)]
            with ExitStack() as pro:
                def sbp(name, shape, dt):
                    return pro.enter_context(nc.sbuf_tensor(name, shape, dt))
                s["xn"] = sbp("xn", [P, NT, DM], F32)
                s["xnT"] = sbp("xnT", [P, KT, TOK], F32)
                prologue(nc, d, s, sbp, sem)
            cross_attention(nc, d, s, sb, sem)
        with ExitStack() as st:
            def sb(name, shape, dt):
                return st.enter_context(nc.sbuf_tensor(name, shape, dt))
            loads = sem("late_loads")
            s["x2"] = sb("x2", [P, NT, DM], F32)
            s["vraw"] = [sb(f"vraw{i}", [P, KT, FE * FP], F32) for i in range(2)]
            s["oraw"] = [sb(f"oraw{i}", [P, FE * DM], F32) for i in range(2)]
            s["qkw"] = sb("qkw", [P, KT, FH, 2 * FP], F32)
            s["sel"] = sb("sel", [P, KT, 2 * FH * FE], F32)
            s["rank"] = sb("rank", [P, FE], F32)
            s["route"] = sb("route", [P, 1], F32)
            sa = ExitStack()

            def sba(name, shape, dt):
                return sa.enter_context(nc.sbuf_tensor(name, shape, dt))
            s["wattn"] = sba("wattn", [P, KT, 3 * DM], F32)
            s["wproj"] = sba("wproj", [P, KT, DM], F32)
            s["alibi"] = sba("alibi", [P, H * TQ], F32)
            s["head_rows2"] = sba("head_rows2", [P, HT], F32)
            s["attn_loads"], s["ffn_loads"] = sem("attn_loads"), sem("ffn_loads")
            s["v_in"], s["o_in"] = [[sem(f"{n}_in{i}") for i in range(2)] for n in "vo"]
            first = [
                (s["wattn"][:, :, :], d["aWT"].rearrange("(k p) f -> p k f", p=P)),
                (s["alibi"][:, :], d["c_alibi"]),
                (s["head_rows2"][:, :], d["c_head_rows"]),
                (s["wproj"][:, :, :], d["aPT"].rearrange("(k p) n -> p k n", p=P)),
            ]
            late = [
                (s["sel"][:, :, :], d["selT"].rearrange("(k p) f -> p k f", p=P)),
                (s["rank"][:, :], d["c_rank"].to_broadcast([P, FE])),
                (s["route"][:, :], d["route"].rearrange("(a b) -> a b", a=1).to_broadcast([P, 1])),
                (s["qkw"][:, :, :, :], d["qkT"].rearrange("(k p) h f -> p k h f", p=P)),
            ]
            s["attn_loads_total"], s["ffn_loads_total"] = 16 * len(first), 16 * len(late)
            with nc.Block() as block:
                @block.sync
                def _(sp):
                    for dst, src in first:
                        sp.dma_start(dst, src).then_inc(s["attn_loads"], 16)
                    for dst, src in late:
                        sp.dma_start(dst, src).then_inc(s["ffn_loads"], 16)
                    for h in range(2):
                        load_experts(sp, d, s, h, h)
            with sa:
                self_attention(nc, d, s, sba, lambda n, sh: sa.enter_context(nc.psum_tensor(n, sh, F32)), sem)
            if stages == 3:
                with ExitStack() as sf:
                    switch_head(nc, d, s, lambda n, sh, dt: sf.enter_context(nc.sbuf_tensor(n, sh, dt)),
                                lambda n, sh: sf.enter_context(nc.psum_tensor(n, sh, F32)), sem)
            wrote = sem("wrote")
            with nc.Block() as block:
                @block.sync
                def _(sp):
                    sp.dma_start(out.rearrange("(n p) f -> p n f", p=P), s["x2"][:, :, :])\
                      .then_inc(wrote, 16)
                    sp.wait_ge(wrote, 16)


def layout(i):
    import numpy as _np
    C = _np.ascontiguousarray
    v = _np.asarray(i["L0_ffn_v_w"]).reshape(FH, FE, DM, FP).transpose(2, 0, 1, 3).reshape(DM, FH, FE * FP)
    o = _np.asarray(i["L0_ffn_o_w"]).reshape(FH, FE, FP, DM).transpose(0, 2, 1, 3).reshape(FH, FP, FE * DM)
    sel = _np.stack([_np.asarray(i[f"L0_ffn_sel_{n}_w"]).reshape(FH, FE, DM) for n in "vo"], axis=1).reshape(2 * FH * FE, DM)
    aw = _np.asarray(i["L0_attn_W_attn"]).T
    av = aw[:, 2 * DM:].reshape(DM, H // 2, 2, DK).transpose(0, 2, 1, 3).reshape(DM, DM)
    qk = _np.concatenate([_np.asarray(i[f"L0_ffn_{n}_w"]).reshape(FH, FP, DM) for n in "qk"], axis=1)
    ins = {
        "x": _np.asarray(i["x"]).reshape(TOK, DM),
        "ctxT": C(_np.asarray(i["ctx_1024"]).transpose(0, 2, 1)),
        "mask": _np.asarray(i["mask_Bx1x1xS2_bk0"]).reshape(B, TK),
        "xWqD": C(_np.stack(2 * [_np.asarray(i["L0_xattn_Wq"]).T.reshape(DM, 4, 64)], axis=2).reshape(DM, 4, P)),
        "xWkT": C(_np.asarray(i["L0_xattn_Wk"]).T),
        "xWvT": C(_np.asarray(i["L0_xattn_Wv"]).T), "xWoT": C(_np.asarray(i["L0_xattn_Wo"]).T),
        "rbT": C(_np.asarray(i["L0_xattn_rel_bias"]).T),
        "aWT": C(_np.concatenate([aw[:, 0:2 * DM], av], axis=1)), "aPT": C(_np.asarray(i["L0_attn_W_proj"]).T),
        "qkT": C(qk.transpose(2, 0, 1)),
        "vw": C(v), "ow": C(o), "selT": C(sel.T), "route": C(_np.asarray(i["L0_ffn_route_scale"])),
    }
    ins.update(constants())
    return ins


def kernel(**inputs):
    import concourse.bacc as _bacc
    from concourse import mybir as _mybir
    from concourse.bass_utils import run_bass_kernel_spmd as _run

    nc = _bacc.Bacc("TRN2", target_bir_lowering=False, num_devices=1)
    arrays, args = {}, {}
    for name, a in layout(inputs).items():
        arrays[f"in_{name}"] = a
        args[name] = nc.dram_tensor(f"in_{name}", a.shape, _mybir.dt.from_np(a.dtype), kind="ExternalInput").ap()
    out = nc.dram_tensor("out_0", (TOK, DM), F32, kind="ExternalOutput").ap()
    build(nc, args, out)
    r = _run(nc, [arrays], core_ids=[0])
    return r.results[0]["out_0"].reshape(B, TQ, DM)
```
